# Optimizing a Trainium2 kernel written in Bass

```python
import numpy as np
import jax
import jax.numpy as jnp

def _softmax(x, axis=-1):
    return jax.nn.softmax(x, axis=axis)

def _gelu(x):
    return jax.nn.gelu(x, approximate=True)

def _silu(x):
    return jax.nn.silu(x)

def _sigmoid(x):
    return jax.nn.sigmoid(x)

def _layernorm(x, axis=-1, eps=1e-05):
    m = jnp.mean(x, axis=axis, keepdims=True)
    v = jnp.var(x, axis=axis, keepdims=True)
    return (x - m) / jnp.sqrt(v + eps)

def _scatter_add(tgt, idx, src, axis=0):
    return tgt.at[idx].add(src)

def _segment_sum(src, seg, n):
    return jax.ops.segment_sum(src, seg, n)
kernel_name = 'mk_decoder_postln_d2_seqx_r8_f33d34'

def setup_inputs(seed: int=0):
    np.random.seed(seed)
    _w = jnp.asarray

    def _rec_inputs():
        import jax
        import jax.numpy as jnp
        _rk = jax.random.key(seed)
        x = 7.22e-05 + 1 * jax.random.normal(jax.random.fold_in(_rk, 1), (128, 64, 128), jnp.float32)
        _lenS = 64 - jax.random.randint(jax.random.fold_in(_rk, 7), (128,), 0, max(1, 64 // 4) + 1, jnp.int32)
        _lenS2 = 64 - jax.random.randint(jax.random.fold_in(_rk, 8), (128,), 0, max(1, 64 // 4) + 1, jnp.int32)
        _ctx_1024P = jax.random.normal(jax.random.fold_in(_rk, 11), (128, 16, 128), jnp.float32)
        _ctx_1024c = jax.random.dirichlet(jax.random.fold_in(_rk, 511), 0.3 * jnp.ones((16,), jnp.float32), (128, 64))
        _ctx_1024t = jnp.einsum('bsk,bkd->bsd', _ctx_1024c, _ctx_1024P)
        _ctx_1024t = _ctx_1024t * jax.lax.rsqrt(jnp.mean(jnp.square(_ctx_1024t)) + 1e-12) * 0.953939
        ctx_1024 = 4.13588e-05 + 0.999923 * (_ctx_1024t + 0.3 * jax.random.normal(jax.random.fold_in(_rk, 611), (128, 64, 128), jnp.float32))
        pos_BxS2 = jnp.broadcast_to(jnp.arange(64, dtype=jnp.int32), (128, 64))
        _validS = jnp.arange(64)[None, :] < _lenS[:, None]
        _validS2 = jnp.arange(64)[None, :] < _lenS2[:, None]
        _causal = jnp.tril(jnp.ones((64, 64), dtype=bool))
        mask_Bx1xSxS2_ff1 = jnp.where(jnp.ones((128, 1, 64, 64), dtype=bool), 1.0, 0.0).astype(jnp.float32)
        return (x, ctx_1024, pos_BxS2, mask_Bx1xSxS2_ff1)
    x, ctx_1024, pos_BxS2, mask_Bx1xSxS2_ff1 = _rec_inputs()

    def _L0_attn_setup():
        import jax, jax.numpy as jnp
        import numpy as np
        DT_MIN, DT_MAX = (0.001, 0.1)
        EPS = 1e-05

        def rmsnorm(x, w):
            return x * jax.lax.rsqrt(jnp.mean(x * x, axis=-1, keepdims=True) + EPS) * w
        key = jax.random.key(seed)
        ks = jax.random.split(key, 12)
        B, T, D = (1, 256, 128)
        E, N, I, K = (2 * D, 64, 256, 4)
        s = lambda k, sh, fan: jax.random.normal(k, sh, jnp.float32) / np.sqrt(fan).astype(np.float32)
        return {'x': jax.random.normal(ks[0], (B, T, D), jnp.float32), 'input_norm_w': jnp.ones((D,), jnp.float32), 'ffn_norm_w': jnp.ones((D,), jnp.float32), 'in_proj_W': s(ks[1], (D, 2 * E), D), 'conv_W': s(ks[2], (K, 1, E), K), 'conv_b': jnp.zeros((E,), jnp.float32), 'dt_W': s(ks[3], (E, E), E), 'dt_b': jnp.zeros((E,), jnp.float32), 'B_W': s(ks[4], (E, N), E), 'C_W': s(ks[5], (E, N), E), 'A_log': -jnp.log(jnp.arange(1, N + 1, dtype=jnp.float32)), 'out_proj_W': s(ks[6], (E, D), E), 'gate_W': s(ks[7], (D, I), D), 'up_W': s(ks[8], (D, I), D), 'down_W': s(ks[9], (I, D), I)}
    _L0_attn_all = _L0_attn_setup()
    _L0_attn_in = {k: v for k, v in _L0_attn_all.items() if k in ('input_norm_w', 'ffn_norm_w', 'in_proj_W', 'conv_W', 'conv_b', 'dt_W', 'dt_b', 'B_W', 'C_W', 'A_log', 'out_proj_W', 'gate_W', 'up_W', 'down_W')}
    del _L0_attn_all

    def _L0_xattn_setup():
        import jax, jax.numpy as jnp
        import numpy as np
        D_MODEL = 128
        NUM_HEADS = 16
        HEAD_DIM = D_MODEL // NUM_HEADS
        THETA = 10000.0
        B, S = (4, 256)

        def _rope(x, pos):
            half = HEAD_DIM // 2
            inv_freq = THETA ** (-(jnp.arange(half, dtype=jnp.float32) * 2.0) / HEAD_DIM)
            ang = pos.astype(jnp.float32)[:, None, :, None] * inv_freq
            cos, sin = (jnp.cos(ang), jnp.sin(ang))
            x1, x2 = (x[..., 0::2], x[..., 1::2])
            r1 = x1 * cos - x2 * sin
            r2 = x1 * sin + x2 * cos
            return jnp.stack([r1, r2], axis=-1).reshape(x.shape)
        key = jax.random.key(seed)
        ks = jax.random.split(key, 12)
        scale = 1.0 / np.sqrt(D_MODEL)
        inp = {'query': jax.random.normal(ks[0], (B, S, D_MODEL), dtype=jnp.float32), 'key': jax.random.normal(ks[1], (B, S, D_MODEL), dtype=jnp.float32), 'value': jax.random.normal(ks[2], (B, S, D_MODEL), dtype=jnp.float32), 'token_positions': jnp.broadcast_to(jnp.arange(S, dtype=jnp.int32), (B, S)), 'w_q': jax.random.normal(ks[3], (D_MODEL, D_MODEL), dtype=jnp.float32) * scale, 'b_q': jnp.zeros((D_MODEL,), dtype=jnp.float32), 'w_k': jax.random.normal(ks[4], (D_MODEL, D_MODEL), dtype=jnp.float32) * scale, 'b_k': jnp.zeros((D_MODEL,), dtype=jnp.float32), 'w_v': jax.random.normal(ks[5], (D_MODEL, D_MODEL), dtype=jnp.float32) * scale, 'b_v': jnp.zeros((D_MODEL,), dtype=jnp.float32), 'w_o': jax.random.normal(ks[6], (D_MODEL, D_MODEL), dtype=jnp.float32) * scale, 'b_o': jnp.zeros((D_MODEL,), dtype=jnp.float32)}
        return inp
    _L0_xattn_all = _L0_xattn_setup()
    _L0_xattn_in = {k: v for k, v in _L0_xattn_all.items() if k in ('w_q', 'b_q', 'w_k', 'b_k', 'w_v', 'b_v', 'w_o', 'b_o')}
    del _L0_xattn_all

    def _L0_ffn_setup():
        import jax, jax.numpy as jnp
        import numpy as np
        D_MODEL = 128
        N_HEADS = 16
        D_HEAD = D_MODEL // N_HEADS
        N_EXPERTS = 8
        TOP_K = 2
        D_FF = 256
        EPS = 1e-06

        def rmsnorm(x, w):
            return x * jax.lax.rsqrt(jnp.mean(x * x, axis=-1, keepdims=True) + EPS) * w

        def swiglu(x, w_gate, w_up, w_down):
            return jax.nn.silu(x @ w_gate) * (x @ w_up) @ w_down
        key = jax.random.key(seed)
        ks = jax.random.split(key, 16)
        s = 0.02
        B, S = (2, 256)
        return {'X': jax.random.normal(ks[0], (B, S, D_MODEL), dtype=jnp.float32), 'norm1_w': jnp.ones((D_MODEL,), jnp.float32), 'norm2_w': jnp.ones((D_MODEL,), jnp.float32), 'wq': jax.random.normal(ks[1], (D_MODEL, D_MODEL), jnp.float32) * s, 'wk': jax.random.normal(ks[2], (D_MODEL, D_MODEL), jnp.float32) * s, 'wv': jax.random.normal(ks[3], (D_MODEL, D_MODEL), jnp.float32) * s, 'wo': jax.random.normal(ks[4], (D_MODEL, D_MODEL), jnp.float32) * s, 'router_w': jax.random.normal(ks[5], (D_MODEL, N_EXPERTS), jnp.float32) * s, 'sh_gate': jax.random.normal(ks[6], (D_MODEL, D_FF), jnp.float32) * s, 'sh_up': jax.random.normal(ks[7], (D_MODEL, D_FF), jnp.float32) * s, 'sh_down': jax.random.normal(ks[8], (D_FF, D_MODEL), jnp.float32) * s, 'e_gate': jax.random.normal(ks[9], (N_EXPERTS, D_MODEL, D_FF), jnp.float32) * s, 'e_up': jax.random.normal(ks[10], (N_EXPERTS, D_MODEL, D_FF), jnp.float32) * s, 'e_down': jax.random.normal(ks[11], (N_EXPERTS, D_FF, D_MODEL), jnp.float32) * s}
    _L0_ffn_all = _L0_ffn_setup()
    _L0_ffn_in = {k: v for k, v in _L0_ffn_all.items() if k in ('norm1_w', 'norm2_w', 'wq', 'wk', 'wv', 'wo', 'router_w', 'sh_gate', 'sh_up', 'sh_down', 'e_gate', 'e_up', 'e_down')}
    del _L0_ffn_all

    def _L1_attn_setup():
        import jax, jax.numpy as jnp
        import numpy as np
        import math
        B, L, D = (2, 256, 128)
        H, KV, HD = (16, 4, 64)
        GROUPS = H // KV
        ROPE_BASE = 10000.0

        def _alibi_slopes(n_heads):

            def pow2(n):
                start = 2.0 ** (-2.0 ** (-(math.log2(n) - 3)))
                return [start * start ** i for i in range(n)]
            if math.log2(n_heads).is_integer():
                return pow2(n_heads)
            c = 2 ** math.floor(math.log2(n_heads))
            return pow2(c) + _alibi_slopes(2 * c)[0::2][:n_heads - c]

        def _rope_cos_sin(seq_len, dim, dtype):
            inv_freq = 1.0 / ROPE_BASE ** (jnp.arange(0, dim, 2, dtype=jnp.float32) / dim)
            t = jnp.arange(seq_len, dtype=jnp.float32)
            freqs = t[:, None] * inv_freq[None, :]
            emb = jnp.concatenate([freqs, freqs], axis=-1)
            return (jnp.cos(emb).astype(dtype), jnp.sin(emb).astype(dtype))

        def _rotate_half(x):
            x1, x2 = (x[..., :x.shape[-1] // 2], x[..., x.shape[-1] // 2:])
            return jnp.concatenate([-x2, x1], axis=-1)
        key = jax.random.key(seed)
        ks = jax.random.split(key, 5)
        s = 0.02
        return {'x': jax.random.normal(ks[0], (B, L, D), jnp.float32), 'Wq': jax.random.normal(ks[1], (D, H * HD), jnp.float32) * s, 'Wk': jax.random.normal(ks[2], (D, KV * HD), jnp.float32) * s, 'Wv': jax.random.normal(ks[3], (D, KV * HD), jnp.float32) * s, 'Wo': jax.random.normal(ks[4], (H * HD, D), jnp.float32) * s}
    _L1_attn_all = _L1_attn_setup()
    _L1_attn_in = {k: v for k, v in _L1_attn_all.items() if k in ('Wq', 'Wk', 'Wv', 'Wo')}
    del _L1_attn_all

    def _L1_xattn_setup():
        import jax, jax.numpy as jnp
        import numpy as np
        MODEL_SIZE = 128
        H = 16
        KEY_SIZE = MODEL_SIZE // H
        B, LQ, LK = (2, 256, 256)
        NEG_INF = -1000000000.0
        key = jax.random.key(seed)
        ks = jax.random.split(key, 10)
        s = 0.02
        return {'decoder_output': jax.random.normal(ks[0], (B, LQ, MODEL_SIZE), dtype=jnp.float32), 'encoder_output': jax.random.normal(ks[1], (B, LK, MODEL_SIZE), dtype=jnp.float32), 'mask': jnp.ones((B, 1, LQ, LK), dtype=jnp.float32), 'wq_w': jax.random.normal(ks[2], (MODEL_SIZE, MODEL_SIZE), dtype=jnp.float32) * s, 'wq_b': jnp.zeros((MODEL_SIZE,), dtype=jnp.float32), 'wk_w': jax.random.normal(ks[3], (MODEL_SIZE, MODEL_SIZE), dtype=jnp.float32) * s, 'wk_b': jnp.zeros((MODEL_SIZE,), dtype=jnp.float32), 'wv_w': jax.random.normal(ks[4], (MODEL_SIZE, MODEL_SIZE), dtype=jnp.float32) * s, 'wv_b': jnp.zeros((MODEL_SIZE,), dtype=jnp.float32), 'wo_w': jax.random.normal(ks[5], (MODEL_SIZE, MODEL_SIZE), dtype=jnp.float32) * s, 'wo_b': jnp.zeros((MODEL_SIZE,), dtype=jnp.float32)}
    _L1_xattn_all = _L1_xattn_setup()
    _L1_xattn_in = {k: v for k, v in _L1_xattn_all.items() if k in ('wq_w', 'wq_b', 'wk_w', 'wk_b', 'wv_w', 'wv_b', 'wo_w', 'wo_b')}
    del _L1_xattn_all

    def _L1_ffn_setup():
        import jax, jax.numpy as jnp
        import numpy as np
        B, S, D = (8, 64, 128)
        H = 16
        DFF = 512
        E = 4
        K = 2
        EPS = 1e-05

        def _layernorm(x, w, b):
            m = x.mean(-1, keepdims=True)
            v = ((x - m) ** 2).mean(-1, keepdims=True)
            return (x - m) / jnp.sqrt(v + EPS) * w + b

        def _encoder_layer(x, iw, ib, ow, ob, l1w, l1b, l2w, l2b, n1w, n1b, n2w, n2b):
            b, s, d = x.shape
            hd = d // H
            qkv = x @ iw.T + ib
            q, k, v = jnp.split(qkv, 3, axis=-1)
            rs = lambda t: t.reshape(b, s, H, hd).transpose(0, 2, 1, 3)
            q, k, v = (rs(q), rs(k), rs(v))
            scale = jnp.asarray(hd, x.dtype) ** 0.5
            scores = jnp.einsum('bhqd,bhkd->bhqk', q, k) / scale
            attn = jax.nn.softmax(scores, axis=-1)
            o = jnp.einsum('bhqk,bhkd->bhqd', attn, v).transpose(0, 2, 1, 3).reshape(b, s, d)
            o = o @ ow.T + ob
            x = _layernorm(x + o, n1w, n1b)
            ff = jax.nn.relu(x @ l1w.T + l1b) @ l2w.T + l2b
            return _layernorm(x + ff, n2w, n2b)
        key = jax.random.key(seed)
        ks = jax.random.split(key, 12)
        g = lambda k, shape: jax.random.normal(k, shape, dtype=jnp.float32) * 0.02
        return {'x': jax.random.normal(ks[0], (B, S, D), dtype=jnp.float32), 'in_proj_w': g(ks[1], (E, 3 * D, D)), 'in_proj_b': g(ks[2], (E, 3 * D)), 'out_proj_w': g(ks[3], (E, D, D)), 'out_proj_b': g(ks[4], (E, D)), 'ln1_w': jnp.ones((E, D), jnp.float32), 'ln1_b': jnp.zeros((E, D), jnp.float32), 'lin1_w': g(ks[5], (E, DFF, D)), 'lin1_b': g(ks[6], (E, DFF)), 'lin2_w': g(ks[7], (E, D, DFF)), 'lin2_b': g(ks[8], (E, D)), 'ln2_w': jnp.ones((E, D), jnp.float32), 'ln2_b': jnp.zeros((E, D), jnp.float32), 'gate_w': g(ks[9], (E, D)), 'gate_b': g(ks[10], (E,))}
    _L1_ffn_all = _L1_ffn_setup()
    _L1_ffn_in = {k: v for k, v in _L1_ffn_all.items() if k in ('in_proj_w', 'in_proj_b', 'out_proj_w', 'out_proj_b', 'ln1_w', 'ln1_b', 'lin1_w', 'lin1_b', 'lin2_w', 'lin2_b', 'ln2_w', 'ln2_b', 'gate_w', 'gate_b')}
    del _L1_ffn_all
    return {'x': x, 'ctx_1024': ctx_1024, 'pos_BxS2': pos_BxS2, 'mask_Bx1xSxS2_ff1': mask_Bx1xSxS2_ff1, 'L0_attn_input_norm_w': _L0_attn_in['input_norm_w'], 'L0_attn_ffn_norm_w': _L0_attn_in['ffn_norm_w'], 'L0_attn_in_proj_W': _L0_attn_in['in_proj_W'], 'L0_attn_conv_W': _L0_attn_in['conv_W'], 'L0_attn_conv_b': _L0_attn_in['conv_b'], 'L0_attn_dt_W': _L0_attn_in['dt_W'], 'L0_attn_dt_b': _L0_attn_in['dt_b'], 'L0_attn_B_W': _L0_attn_in['B_W'], 'L0_attn_C_W': _L0_attn_in['C_W'], 'L0_attn_A_log': _L0_attn_in['A_log'], 'L0_attn_out_proj_W': _L0_attn_in['out_proj_W'], 'L0_attn_gate_W': _L0_attn_in['gate_W'], 'L0_attn_up_W': _L0_attn_in['up_W'], 'L0_attn_down_W': _L0_attn_in['down_W'], 'L0_xattn_w_q': _L0_xattn_in['w_q'], 'L0_xattn_b_q': _L0_xattn_in['b_q'], 'L0_xattn_w_k': _L0_xattn_in['w_k'], 'L0_xattn_b_k': _L0_xattn_in['b_k'], 'L0_xattn_w_v': _L0_xattn_in['w_v'], 'L0_xattn_b_v': _L0_xattn_in['b_v'], 'L0_xattn_w_o': _L0_xattn_in['w_o'], 'L0_xattn_b_o': _L0_xattn_in['b_o'], 'L0_ffn_norm1_w': _L0_ffn_in['norm1_w'], 'L0_ffn_norm2_w': _L0_ffn_in['norm2_w'], 'L0_ffn_wq': _L0_ffn_in['wq'], 'L0_ffn_wk': _L0_ffn_in['wk'], 'L0_ffn_wv': _L0_ffn_in['wv'], 'L0_ffn_wo': _L0_ffn_in['wo'], 'L0_ffn_router_w': _L0_ffn_in['router_w'], 'L0_ffn_sh_gate': _L0_ffn_in['sh_gate'], 'L0_ffn_sh_up': _L0_ffn_in['sh_up'], 'L0_ffn_sh_down': _L0_ffn_in['sh_down'], 'L0_ffn_e_gate': _L0_ffn_in['e_gate'], 'L0_ffn_e_up': _L0_ffn_in['e_up'], 'L0_ffn_e_down': _L0_ffn_in['e_down'], 'L1_attn_Wq': _L1_attn_in['Wq'], 'L1_attn_Wk': _L1_attn_in['Wk'], 'L1_attn_Wv': _L1_attn_in['Wv'], 'L1_attn_Wo': _L1_attn_in['Wo'], 'L1_xattn_wq_w': _L1_xattn_in['wq_w'], 'L1_xattn_wq_b': _L1_xattn_in['wq_b'], 'L1_xattn_wk_w': _L1_xattn_in['wk_w'], 'L1_xattn_wk_b': _L1_xattn_in['wk_b'], 'L1_xattn_wv_w': _L1_xattn_in['wv_w'], 'L1_xattn_wv_b': _L1_xattn_in['wv_b'], 'L1_xattn_wo_w': _L1_xattn_in['wo_w'], 'L1_xattn_wo_b': _L1_xattn_in['wo_b'], 'L1_ffn_in_proj_w': _L1_ffn_in['in_proj_w'], 'L1_ffn_in_proj_b': _L1_ffn_in['in_proj_b'], 'L1_ffn_out_proj_w': _L1_ffn_in['out_proj_w'], 'L1_ffn_out_proj_b': _L1_ffn_in['out_proj_b'], 'L1_ffn_ln1_w': _L1_ffn_in['ln1_w'], 'L1_ffn_ln1_b': _L1_ffn_in['ln1_b'], 'L1_ffn_lin1_w': _L1_ffn_in['lin1_w'], 'L1_ffn_lin1_b': _L1_ffn_in['lin1_b'], 'L1_ffn_lin2_w': _L1_ffn_in['lin2_w'], 'L1_ffn_lin2_b': _L1_ffn_in['lin2_b'], 'L1_ffn_ln2_w': _L1_ffn_in['ln2_w'], 'L1_ffn_ln2_b': _L1_ffn_in['ln2_b'], 'L1_ffn_gate_w': _L1_ffn_in['gate_w'], 'L1_ffn_gate_b': _L1_ffn_in['gate_b']}

def reference(x, ctx_1024, pos_BxS2, mask_Bx1xSxS2_ff1, L0_attn_input_norm_w, L0_attn_ffn_norm_w, L0_attn_in_proj_W, L0_attn_conv_W, L0_attn_conv_b, L0_attn_dt_W, L0_attn_dt_b, L0_attn_B_W, L0_attn_C_W, L0_attn_A_log, L0_attn_out_proj_W, L0_attn_gate_W, L0_attn_up_W, L0_attn_down_W, L0_xattn_w_q, L0_xattn_b_q, L0_xattn_w_k, L0_xattn_b_k, L0_xattn_w_v, L0_xattn_b_v, L0_xattn_w_o, L0_xattn_b_o, L0_ffn_norm1_w, L0_ffn_norm2_w, L0_ffn_wq, L0_ffn_wk, L0_ffn_wv, L0_ffn_wo, L0_ffn_router_w, L0_ffn_sh_gate, L0_ffn_sh_up, L0_ffn_sh_down, L0_ffn_e_gate, L0_ffn_e_up, L0_ffn_e_down, L1_attn_Wq, L1_attn_Wk, L1_attn_Wv, L1_attn_Wo, L1_xattn_wq_w, L1_xattn_wq_b, L1_xattn_wk_w, L1_xattn_wk_b, L1_xattn_wv_w, L1_xattn_wv_b, L1_xattn_wo_w, L1_xattn_wo_b, L1_ffn_in_proj_w, L1_ffn_in_proj_b, L1_ffn_out_proj_w, L1_ffn_out_proj_b, L1_ffn_ln1_w, L1_ffn_ln1_b, L1_ffn_lin1_w, L1_ffn_lin1_b, L1_ffn_lin2_w, L1_ffn_lin2_b, L1_ffn_ln2_w, L1_ffn_ln2_b, L1_ffn_gate_w, L1_ffn_gate_b):
    import jax
    import jax.numpy as jnp

    def _L0_attn_ref(x, input_norm_w, ffn_norm_w, in_proj_W, conv_W, conv_b, dt_W, dt_b, B_W, C_W, A_log, out_proj_W, gate_W, up_W, down_W):
        import jax, jax.numpy as jnp
        import numpy as np
        DT_MIN, DT_MAX = (0.001, 0.1)
        EPS = 1e-05

        def rmsnorm(x, w):
            return x * jax.lax.rsqrt(jnp.mean(x * x, axis=-1, keepdims=True) + EPS) * w
        Bsz, T, D = x.shape
        E = in_proj_W.shape[1] // 2
        N = A_log.shape[0]
        normed = rmsnorm(x, input_norm_w)
        xp = normed @ in_proj_W
        x_z, z = (xp[..., :E], xp[..., E:])
        xc = jax.lax.conv_general_dilated(x_z, conv_W, window_strides=(1,), padding='SAME', dimension_numbers=('NWC', 'WIO', 'NWC'), feature_group_count=E) + conv_b
        xc = jax.nn.silu(xc)
        dt = jnp.clip(jax.nn.softplus(xc @ dt_W + dt_b), DT_MIN, DT_MAX)
        Bp = xc @ B_W
        Cp = xc @ C_W
        A = -jnp.exp(A_log)

        def step(h, ins):
            x_t, dt_t, B_t, C_t = ins
            dA = jnp.exp(dt_t[..., None] * A)
            h = dA * h + dt_t[..., None] * B_t[:, None, :] * x_t[..., None]
            y_t = jnp.einsum('ben,bn->be', h, C_t)
            return (h, y_t)
        h0 = jnp.zeros((Bsz, E, N), x.dtype)
        _, y = jax.lax.scan(step, h0, (xc.transpose(1, 0, 2), dt.transpose(1, 0, 2), Bp.transpose(1, 0, 2), Cp.transpose(1, 0, 2)))
        y = y.transpose(1, 0, 2) * jax.nn.silu(z)
        x = x + y @ out_proj_W
        n2 = rmsnorm(x, ffn_norm_w)
        ffn = jax.nn.silu(n2 @ gate_W) * (n2 @ up_W) @ down_W
        return x + ffn

    def _L0_xattn_ref(query, key, value, token_positions, w_q, b_q, w_k, b_k, w_v, b_v, w_o, b_o):
        import jax, jax.numpy as jnp
        import numpy as np
        D_MODEL = 128
        NUM_HEADS = 16
        HEAD_DIM = D_MODEL // NUM_HEADS
        THETA = 10000.0
        B, S = (4, 256)

        def _rope(x, pos):
            half = HEAD_DIM // 2
            inv_freq = THETA ** (-(jnp.arange(half, dtype=jnp.float32) * 2.0) / HEAD_DIM)
            ang = pos.astype(jnp.float32)[:, None, :, None] * inv_freq
            cos, sin = (jnp.cos(ang), jnp.sin(ang))
            x1, x2 = (x[..., 0::2], x[..., 1::2])
            r1 = x1 * cos - x2 * sin
            r2 = x1 * sin + x2 * cos
            return jnp.stack([r1, r2], axis=-1).reshape(x.shape)
        b, s, _ = query.shape
        Q = query @ w_q + b_q
        K = key @ w_k + b_k
        V = value @ w_v + b_v
        Q = Q.reshape(b, s, NUM_HEADS, HEAD_DIM).transpose(0, 2, 1, 3)
        K = K.reshape(b, s, NUM_HEADS, HEAD_DIM).transpose(0, 2, 1, 3)
        V = V.reshape(b, s, NUM_HEADS, HEAD_DIM).transpose(0, 2, 1, 3)
        Q = _rope(Q, token_positions)
        K = _rope(K, token_positions)
        scores = jnp.einsum('bhqd,bhkd->bhqk', Q, K) / jnp.sqrt(jnp.float32(HEAD_DIM))
        causal = jnp.tril(jnp.ones((s, s), dtype=bool))
        scores = jnp.where(causal, scores, -jnp.inf)
        attn = jax.nn.softmax(scores, axis=-1)
        out = jnp.einsum('bhqk,bhkd->bhqd', attn, V)
        out = out.transpose(0, 2, 1, 3).reshape(b, s, D_MODEL)
        return out @ w_o + b_o

    def _L0_ffn_ref(X, norm1_w, norm2_w, wq, wk, wv, wo, router_w, sh_gate, sh_up, sh_down, e_gate, e_up, e_down):
        import jax, jax.numpy as jnp
        import numpy as np
        D_MODEL = 128
        N_HEADS = 16
        D_HEAD = D_MODEL // N_HEADS
        N_EXPERTS = 8
        TOP_K = 2
        D_FF = 256
        EPS = 1e-06

        def rmsnorm(x, w):
            return x * jax.lax.rsqrt(jnp.mean(x * x, axis=-1, keepdims=True) + EPS) * w

        def swiglu(x, w_gate, w_up, w_down):
            return jax.nn.silu(x @ w_gate) * (x @ w_up) @ w_down
        B, S, d = X.shape
        scale = 1.0 / jnp.sqrt(jnp.asarray(D_HEAD, X.dtype))
        h = rmsnorm(X, norm1_w)
        q = (h @ wq).reshape(B, S, N_HEADS, D_HEAD)
        k = (h @ wk).reshape(B, S, N_HEADS, D_HEAD)
        v = (h @ wv).reshape(B, S, N_HEADS, D_HEAD)
        scores = jnp.einsum('bshd,bthd->bhst', q, k) * scale
        attn = jax.nn.softmax(scores, axis=-1)
        ctx = jnp.einsum('bhst,bthd->bshd', attn, v).reshape(B, S, d)
        X = X + ctx @ wo
        h2 = rmsnorm(X, norm2_w).reshape(B * S, d)
        logits = h2 @ router_w
        probs = jax.nn.softmax(logits, axis=-1)
        topw, topi = jax.lax.top_k(probs, TOP_K)
        topw = jax.nn.softmax(topw, axis=-1)
        combine = jnp.sum(jax.nn.one_hot(topi, N_EXPERTS, dtype=h2.dtype) * topw[..., None], axis=1)
        shared = swiglu(h2, sh_gate, sh_up, sh_down)
        gate = jnp.einsum('td,edf->etf', h2, e_gate)
        up = jnp.einsum('td,edf->etf', h2, e_up)
        eout = jnp.einsum('etf,efd->etd', jax.nn.silu(gate) * up, e_down)
        spec = jnp.einsum('etd,te->td', eout, combine)
        moe_out = (shared + spec).reshape(B, S, d)
        return X + moe_out

    def _L1_attn_ref(x, Wq, Wk, Wv, Wo):
        import jax, jax.numpy as jnp
        import numpy as np
        import math
        B, L, D = (2, 256, 128)
        H, KV, HD = (16, 4, 64)
        GROUPS = H // KV
        ROPE_BASE = 10000.0

        def _alibi_slopes(n_heads):

            def pow2(n):
                start = 2.0 ** (-2.0 ** (-(math.log2(n) - 3)))
                return [start * start ** i for i in range(n)]
            if math.log2(n_heads).is_integer():
                return pow2(n_heads)
            c = 2 ** math.floor(math.log2(n_heads))
            return pow2(c) + _alibi_slopes(2 * c)[0::2][:n_heads - c]

        def _rope_cos_sin(seq_len, dim, dtype):
            inv_freq = 1.0 / ROPE_BASE ** (jnp.arange(0, dim, 2, dtype=jnp.float32) / dim)
            t = jnp.arange(seq_len, dtype=jnp.float32)
            freqs = t[:, None] * inv_freq[None, :]
            emb = jnp.concatenate([freqs, freqs], axis=-1)
            return (jnp.cos(emb).astype(dtype), jnp.sin(emb).astype(dtype))

        def _rotate_half(x):
            x1, x2 = (x[..., :x.shape[-1] // 2], x[..., x.shape[-1] // 2:])
            return jnp.concatenate([-x2, x1], axis=-1)
        b, l, _ = x.shape
        q = (x @ Wq).reshape(b, l, H, HD).transpose(0, 2, 1, 3)
        k = (x @ Wk).reshape(b, l, KV, HD).transpose(0, 2, 1, 3)
        v = (x @ Wv).reshape(b, l, KV, HD).transpose(0, 2, 1, 3)
        k = jnp.repeat(k, GROUPS, axis=1)
        v = jnp.repeat(v, GROUPS, axis=1)
        cos, sin = _rope_cos_sin(l, HD, x.dtype)
        q = q * cos + _rotate_half(q) * sin
        k = k * cos + _rotate_half(k) * sin
        attn = jnp.einsum('bhqd,bhkd->bhqk', q, k) / math.sqrt(HD)
        pos = jnp.arange(l)
        rel = (pos[None, :] - pos[:, None]).astype(x.dtype)
        slopes = jnp.asarray(_alibi_slopes(H), dtype=x.dtype)
        attn = attn + slopes[None, :, None, None] * rel[None, None, :, :]
        attn = jax.nn.softmax(attn, axis=-1)
        out = jnp.einsum('bhqk,bhkd->bhqd', attn, v)
        out = out.transpose(0, 2, 1, 3).reshape(b, l, H * HD)
        return out @ Wo

    def _L1_xattn_ref(decoder_output, encoder_output, mask, wq_w, wq_b, wk_w, wk_b, wv_w, wv_b, wo_w, wo_b):
        import jax, jax.numpy as jnp
        import numpy as np
        MODEL_SIZE = 128
        H = 16
        KEY_SIZE = MODEL_SIZE // H
        B, LQ, LK = (2, 256, 256)
        NEG_INF = -1000000000.0
        b = decoder_output.shape[0]
        q = decoder_output @ wq_w + wq_b
        k = encoder_output @ wk_w + wk_b
        v = encoder_output @ wv_w + wv_b
        q = q.reshape(b, -1, H, KEY_SIZE).transpose(0, 2, 1, 3)
        k = k.reshape(b, -1, H, KEY_SIZE).transpose(0, 2, 1, 3)
        v = v.reshape(b, -1, H, KEY_SIZE).transpose(0, 2, 1, 3)
        score = jnp.einsum('bhqd,bhkd->bhqk', q, k) / jnp.sqrt(jnp.asarray(KEY_SIZE, dtype=jnp.float32))
        score = score * mask
        score = jnp.where(score == 0, jnp.float32(NEG_INF), score)
        alignment = jax.nn.softmax(score, axis=-1)
        context = jnp.einsum('bhqk,bhkd->bhqd', alignment, v)
        context = context.transpose(0, 2, 1, 3).reshape(b, -1, H * KEY_SIZE)
        heads = context @ wo_w + wo_b
        return heads

    def _L1_ffn_ref(x, in_proj_w, in_proj_b, out_proj_w, out_proj_b, ln1_w, ln1_b, lin1_w, lin1_b, lin2_w, lin2_b, ln2_w, ln2_b, gate_w, gate_b):
        import jax, jax.numpy as jnp
        import numpy as np
        B, S, D = (8, 64, 128)
        H = 16
        DFF = 512
        E = 4
        K = 2
        EPS = 1e-05

        def _layernorm(x, w, b):
            m = x.mean(-1, keepdims=True)
            v = ((x - m) ** 2).mean(-1, keepdims=True)
            return (x - m) / jnp.sqrt(v + EPS) * w + b

        def _encoder_layer(x, iw, ib, ow, ob, l1w, l1b, l2w, l2b, n1w, n1b, n2w, n2b):
            b, s, d = x.shape
            hd = d // H
            qkv = x @ iw.T + ib
            q, k, v = jnp.split(qkv, 3, axis=-1)
            rs = lambda t: t.reshape(b, s, H, hd).transpose(0, 2, 1, 3)
            q, k, v = (rs(q), rs(k), rs(v))
            scale = jnp.asarray(hd, x.dtype) ** 0.5
            scores = jnp.einsum('bhqd,bhkd->bhqk', q, k) / scale
            attn = jax.nn.softmax(scores, axis=-1)
            o = jnp.einsum('bhqk,bhkd->bhqd', attn, v).transpose(0, 2, 1, 3).reshape(b, s, d)
            o = o @ ow.T + ob
            x = _layernorm(x + o, n1w, n1b)
            ff = jax.nn.relu(x @ l1w.T + l1b) @ l2w.T + l2b
            return _layernorm(x + ff, n2w, n2b)
        gate_logits = x.mean(axis=1) @ gate_w.T + gate_b
        _, top_idx = jax.lax.top_k(gate_logits, K)
        gate_weights = jax.nn.softmax(gate_logits, axis=-1)
        mask = jnp.zeros_like(gate_weights).at[jnp.arange(x.shape[0])[:, None], top_idx].set(1.0)
        expert_outs = jax.vmap(_encoder_layer, in_axes=(None, 0, 0, 0, 0, 0, 0, 0, 0, 0, 0, 0, 0))(x, in_proj_w, in_proj_b, out_proj_w, out_proj_b, lin1_w, lin1_b, lin2_w, lin2_b, ln1_w, ln1_b, ln2_w, ln2_b)
        return jnp.einsum('be,ebsd->bsd', gate_weights * mask, expert_outs)
    x = _layernorm(x + _L0_attn_ref(x, L0_attn_input_norm_w, L0_attn_ffn_norm_w, L0_attn_in_proj_W, L0_attn_conv_W, L0_attn_conv_b, L0_attn_dt_W, L0_attn_dt_b, L0_attn_B_W, L0_attn_C_W, L0_attn_A_log, L0_attn_out_proj_W, L0_attn_gate_W, L0_attn_up_W, L0_attn_down_W), axis=-1)
    x = _layernorm(x + _L0_xattn_ref(x, ctx_1024, ctx_1024, pos_BxS2, L0_xattn_w_q, L0_xattn_b_q, L0_xattn_w_k, L0_xattn_b_k, L0_xattn_w_v, L0_xattn_b_v, L0_xattn_w_o, L0_xattn_b_o), axis=-1)
    x = _layernorm(x + _L0_ffn_ref(x, L0_ffn_norm1_w, L0_ffn_norm2_w, L0_ffn_wq, L0_ffn_wk, L0_ffn_wv, L0_ffn_wo, L0_ffn_router_w, L0_ffn_sh_gate, L0_ffn_sh_up, L0_ffn_sh_down, L0_ffn_e_gate, L0_ffn_e_up, L0_ffn_e_down), axis=-1)
    x = _layernorm(x + _L1_attn_ref(x, L1_attn_Wq, L1_attn_Wk, L1_attn_Wv, L1_attn_Wo), axis=-1)
    x = _layernorm(x + _L1_xattn_ref(x, ctx_1024, mask_Bx1xSxS2_ff1, L1_xattn_wq_w, L1_xattn_wq_b, L1_xattn_wk_w, L1_xattn_wk_b, L1_xattn_wv_w, L1_xattn_wv_b, L1_xattn_wo_w, L1_xattn_wo_b), axis=-1)
    x = _layernorm(x + _L1_ffn_ref(x, L1_ffn_in_proj_w, L1_ffn_in_proj_b, L1_ffn_out_proj_w, L1_ffn_out_proj_b, L1_ffn_ln1_w, L1_ffn_ln1_b, L1_ffn_lin1_w, L1_ffn_lin1_b, L1_ffn_lin2_w, L1_ffn_lin2_b, L1_ffn_ln2_w, L1_ffn_ln2_b, L1_ffn_gate_w, L1_ffn_gate_b), axis=-1)
    return x

_drawn_inputs = setup_inputs


def setup_inputs(seed=0):
    import zlib

    import numpy as np

    out = dict(_drawn_inputs(seed))
    spreads = {'L0_attn_input_norm_w': (1.0, 0.2),
     'L0_attn_ffn_norm_w': (1.0, 0.2),
     'L0_attn_conv_b': (0.0, 0.1),
     'L0_attn_dt_b': (0.0, 0.8),
     'L0_xattn_b_q': (0.0, 0.291),
     'L0_xattn_b_k': (0.0, 0.701),
     'L0_xattn_b_v': (0.0, 0.1),
     'L0_xattn_b_o': (0.0, 0.1),
     'L0_ffn_norm1_w': (1.0, 0.6),
     'L0_ffn_norm2_w': (1.0, 0.6),
     'L1_xattn_wq_b': (0.0, 0.8),
     'L1_xattn_wk_b': (0.0, 2.0),
     'L1_xattn_wv_b': (0.0, 0.1),
     'L1_xattn_wo_b': (0.0, 0.1),
     'L1_ffn_ln1_w': (1.0, 0.2),
     'L1_ffn_ln1_b': (0.0, 0.333),
     'L1_ffn_ln2_w': (1.0, 0.2),
     'L1_ffn_ln2_b': (0.0, 0.3)}
    factors = {'L0_attn_dt_W': 8.0,
     'L0_ffn_wq': 8.0,
     'L0_ffn_wk': 8.0,
     'L0_ffn_wv': 3.436,
     'L0_ffn_wo': 3.799,
     'L0_ffn_router_w': 8.0,
     'L0_ffn_sh_gate': 6.052,
     'L0_ffn_sh_up': 7.2,
     'L0_ffn_sh_down': 6.806,
     'L0_ffn_e_gate': 8.0,
     'L0_ffn_e_up': 8.0,
     'L0_ffn_e_down': 8.0,
     'L1_attn_Wq': 8.0,
     'L1_attn_Wk': 8.0,
     'L1_xattn_wq_w': 8.0,
     'L1_xattn_wk_w': 8.0,
     'L1_ffn_in_proj_w': 8.0,
     'L1_ffn_in_proj_b': 8.0,
     'L1_ffn_out_proj_w': 8.0,
     'L1_ffn_out_proj_b': 22.8,
     'L1_ffn_lin1_w': 3.695,
     'L1_ffn_lin1_b': 8.0,
     'L1_ffn_lin2_w': 3.0,
     'L1_ffn_lin2_b': 8.0}
    for name, (base, spread) in spreads.items():
        noise = np.random.default_rng([zlib.crc32(name.encode()), seed]).standard_normal(out[name].shape)
        drawn = base * np.exp(spread * noise) if base else spread * noise
        out[name] = jnp.asarray(drawn.astype(out[name].dtype))
    for name, factor in factors.items():
        out[name] = (out[name] * factor).astype(out[name].dtype)
    return out
```

```python
from contextlib import ExitStack

import numpy as np

import concourse.bass as bass
from concourse import mybir

F32 = mybir.dt.float32
BF16 = mybir.dt.bfloat16
I32 = mybir.dt.int32
ACT = mybir.ActivationFunctionType
ALU = mybir.AluOpType
AX = mybir.AxisListType

B, S, D = 128, 64, 128
TILES = B * S // 128
H8 = 16
LN_EPS = 1e-5


class Signal:

    def __init__(self, sem, per, unit=1):
        self.sem, self.per, self.unit = sem, per, unit

    def at(self, i, k=None):
        v = i * (self.per * self.unit) + ((self.per if k is None else k) * self.unit + 1)
        return max(v, 1) if isinstance(v, int) else v


class SlotSignal:

    def __init__(self, sems, per):
        self.sems, self.per = sems, per

    def of(self, u):
        return self.sems[u]

    def at(self, i, u):
        v = (i - u) * (8 * self.per) + (16 * self.per + 1)
        return max(v, 1) if isinstance(v, int) else v


class Stage:

    def __init__(self, nc, sems, mem, name):
        self.nc, self.mem, self.name, self.handles = nc, mem, name, []
        mem.callback(self.end)

    def begin(self):
        self.nc.all_engine_barrier()

    def end(self):
        self.nc.clear_and_free_semaphores(self.handles)
        self.nc.all_engine_barrier()

    def sb(self, name, shape, dt=F32):
        return self.mem.enter_context(self.nc.sbuf_tensor(f"{self.name}_{name}", shape, dt))

    def semaphore(self, name):
        sem = self.nc.alloc_semaphore(name=f"{self.name}_{name}")
        self.handles.append(sem)
        self.nc.gpsimd.sem_inc(sem, 1)
        return sem

    def counter(self, name, per=1):
        return Signal(self.semaphore(name), per)

    def dma_signal(self, name, per=1):
        return Signal(self.semaphore(name), per, 16)

    def slot_signal(self, name, per=1):
        return SlotSignal([self.semaphore(f"{name}{u}") for u in range(2)], per)


def bcast_rows(row, n=128):
    return row.rearrange("(a n) -> a n", a=1).to_broadcast([n, row.shape[0]])


def tiles_of(dram, i, n):
    return dram[bass.ds(i * n, n)].rearrange("t p d -> p t d")


def every_head(v):
    return bass.AP(v.tensor, v.offset, [[0, H8]] + list(v.ap))


def diagonal(v, h2):
    (row, rows), (block, blocks), _ = v.ap
    return bass.AP(v.tensor, v.offset + 8 * h2, [[row, rows], [block, blocks], [48, 2], [1, 8]])


def attention8(nc, sems, ps, name, x_in, x_out, w, ctx=None, pre_norm=False, qkv_bias=False, rope=None,
               causal=False, mask=None, tail="ln"):
    QUADS = TILES // 2
    SCALE = 8.0 ** -0.5
    has_ctx = ctx is not None
    with ExitStack() as mem:
        st = Stage(nc, sems, mem, name)
        ident = st.sb("ident", [128, 128])
        wq = st.sb("wq", [128, 128])
        wk = st.sb("wk", [128, 128])
        wv = st.sb("wv", [128, 128])
        wo = st.sb("wo", [128, 128])
        head_mask = st.sb("head_mask", [128, 4])
        x = st.sb("x", [128, 2, 2, 128])
        xr = st.sb("xr", [128, 2, 2, 128])
        qT = st.sb("qT", [128, 2, 256])
        kT = st.sb("kT", [128, 256])
        km = st.sb("km", [128, 2, 4, 4, 64])
        vbd = st.sb("vbd", [128, 2, 4, 4, 2, 32])
        p = st.sb("p", [128, 2, 2048])
        top = st.sb("top", [128, 32])
        total = st.sb("total", [128, 32])
        rec = st.sb("rec", [128, 32])
        pT = st.sb("pT", [128, 2, 1024])
        oT = st.sb("oT", [128, 256])
        res = st.sb("res", [128, 2, 128])
        stats = st.sb("stats", [128, 2, 6])
        mv = st.sb("mv", [128, 2, 2])
        rstd = st.sb("rstd", [128, 2])
        half_neg = st.sb("half_neg", [128, 2])
        eps = st.sb("eps", [128, 2])
        seen = st.sb("seen", [128, 2])
        y = st.sb("y", [128, 2, 2, 128])
        loads = [(ident[:], w["ident"]), (wq[:], w["wq"]), (wk[:], w["wk"]), (wv[:], w["wv"]),
                 (wo[:], w["wo"]), (head_mask[:], w["head_mask"])]
        if has_ctx:
            c = st.sb("c", [128, 2, 2, 128])
            xT = st.sb("xT", [128, 256])
        kvT = st.sb("kvT", [128, 4, 2, 64])
        kv_once = kvT[:, :, 0, :]
        q_src = xT[:] if has_ctx else kv_once
        if pre_norm:
            xn = st.sb("xn", [128, 2, 128])
            nstats = st.sb("nstats", [128, 2, 6])
            nmv = st.sb("nmv", [128, 2, 2])
            nsq = st.sb("nsq", [128, 2])
            nrstd = st.sb("nrstd", [128, 2])
            norm_eps = st.sb("norm_eps", [128, 2])
            norm_w = st.sb("norm_w", [128, 1])
            loads.append((norm_w[:], w["norm_w"]))
        if qkv_bias:
            bq = st.sb("bq", [128, 1])
            bk = st.sb("bk", [128, 1])
            bv = st.sb("bv", [128, 4, 128])
            bo = st.sb("bo", [128, 128])
            loads += [(bq[:], w["bq"]), (bk[:], w["bk"]), (bo[:], bcast_rows(w["bo"]))]
            loads += [(bv[:, b, :], bcast_rows(w["bv"])) for b in range(4)]
        if rope:
            wqs = st.sb("wqs", [128, 128])
            wks = st.sb("wks", [128, 128])
            bqs = st.sb("bqs", [128, 1])
            bks = st.sb("bks", [128, 1])
            cs = st.sb("cs", [128, 2, 2, 256])
            qs = st.sb("qs", [128, 2, 256])
            qc = st.sb("qc", [128, 2, 256])
            loads += [(wqs[:], w["wqs"]), (wks[:], w["wks"]), (bqs[:], w["bqs"]), (bks[:], w["bks"])]
        if causal:
            sel_q = st.sb("sel_q", [64, 128], BF16)
            future = st.sb("future", [64, 512], BF16)
            sel_q32 = st.sb("sel_q32", [64, 128])
            future32 = st.sb("future32", [64, 512])
            loads += [(sel_q32[:], w["sel_q"]), (future32[:], w["future"])]
        if mask is not None:
            mk = st.sb("mk", [128, 2, 2, 64])
            dead = st.sb("dead", [128, 2048])
        if tail == "affine":
            lnw = st.sb("lnw", [128, 128])
            lnb = st.sb("lnb", [128, 128])
            loads += [(lnw[:], bcast_rows(w["lnw"])), (lnb[:], bcast_rows(w["lnb"]))]

        w_loaded = st.dma_signal("w_loaded", len(loads))
        x_loaded = st.slot_signal("x_loaded", 1)
        c_loaded = st.slot_signal("c_loaded", 1)
        cs_loaded = st.slot_signal("cs_loaded", 2)
        mk_loaded = st.slot_signal("mk_loaded", 1)
        xr_loaded = st.slot_signal("xr_loaded", 1)
        y_stored = st.slot_signal("y_stored", 1)
        consts_set = st.counter("consts_set", 1 + 2 * causal)
        half_set = st.counter("half_set", 2 + pre_norm)
        normed = st.counter("normed", 6)
        nrstd_ready = st.counter("nrstd_ready", 2)
        xT_done = st.counter("xT_done")
        xT_ready = st.counter("xT_ready", 2 if has_ctx else 1)
        qk_done = st.counter("qk_done")
        qs_done = st.counter("qs_done")
        qk_taken = st.counter("qk_taken", 2)
        qs_taken = st.counter("qs_taken", 2)
        rot_ready = st.counter("rot_ready", 2)
        km_ready = st.counter("km_ready")
        v_done = st.counter("v_done")
        v_ready = st.counter("v_ready", 2)
        s_done = st.counter("s_done")
        masked = st.counter("masked", 2)
        dead_ready = st.counter("dead_ready", 1)
        s_masked = st.counter("s_masked", 1)
        top_ready = st.counter("top_ready")
        shifted = st.counter("shifted")
        exp_done = st.counter("exp_done")
        summed = st.counter("summed")
        rec_ready = st.counter("rec_ready")
        p_ready = st.counter("p_ready")
        pT_done = st.counter("pT_done", 2)
        pT_ready = st.counter("pT_ready", 2)
        o_done = st.counter("o_done", 2)
        oT_ready = st.counter("oT_ready")
        y_done = st.counter("y_done")
        biased = st.counter("biased")
        TAIL = {"none": 0, "ln": 6, "affine": 8}[tail]
        res_taken = st.counter("res_taken")
        tailed = st.counter("tailed", max(TAIL, 1))
        rstd_ready = st.counter("rstd_ready", 2)

        S_ps = ps[:, 0:4, :]
        P_g = p[:].rearrange("p u (g t h k) -> p u g t h k", g=4, t=2, h=4)
        Y_ps = ps[:, 5, 256:512]
        lead_ps = ps[:, 4, :]

        st.begin()
        with nc.Block() as block:

            @block.sync
            def _(sp):
                for dst, src in loads:
                    sp.dma_start(dst, src).then_inc(w_loaded.sem, 16)

                def lead(i, u):
                    sp.wait_ge(xT_done.sem, xT_done.at(i - 2))
                    sp.dma_start(x[:, u], tiles_of(x_in, i, 2)).then_inc(x_loaded.of(u), 16)
                    if has_ctx:
                        sp.dma_start(c[:, u], tiles_of(ctx, i, 2)).then_inc(c_loaded.of(u), 16)
                    if rope:
                        sp.wait_ge(rot_ready.sem, rot_ready.at(i - 2))
                        for z in range(2):
                            sp.dma_start(cs[:, u, z], every_head(rope[z][:, bass.ds(256 * i, 256)])).then_inc(
                                cs_loaded.of(u), 16)
                    if mask is not None:
                        sp.wait_ge(masked.sem, masked.at(i - 2))
                        sp.dma_start(mk[:, u], mask[bass.ds(2 * i, 2)].rearrange("t p k -> p t k")).then_inc(
                            mk_loaded.of(u), 16)

                def trail(i, u):
                    if qkv_bias:
                        sp.wait_ge(biased.sem, biased.at(i - 2))
                    sp.wait_ge(res_taken.sem, res_taken.at(i - 2))
                    sp.dma_start(xr[:, u], tiles_of(x_in, i, 2)).then_inc(xr_loaded.of(u), 16)

                def store(i, u):
                    if tail == "none":
                        sp.wait_ge(res_taken.sem, res_taken.at(i))
                    else:
                        sp.wait_ge(tailed.sem, tailed.at(i))
                    sp.dma_start(tiles_of(x_out, i, 2), y[:, u]).then_inc(y_stored.of(u), 16)

                lead(0, 0)
                lead(1, 1)
                trail(0, 0)
                lead(2, 0)
                trail(1, 1)
                lead(3, 1)
                trail(2, 0)
                store(0, 0)
                with sp.Fori(1, (QUADS - 2) // 2) as r:
                    for h in range(2):
                        i, u = 2 * r + (1 + h), (1 + h) % 2
                        lead(i + 1, 1 - u)
                        trail(i, u)
                        store(i - 2, u)
                trail(QUADS - 1, 1)
                for q in (QUADS - 3, QUADS - 2, QUADS - 1):
                    store(q, q % 2)
                for u in range(2):
                    sp.wait_ge(y_stored.of(u), y_stored.at(QUADS - 2 + u, u))

            @block.tensor
            def _(pe):
                def turn(i, u):
                    pe.wait_ge(v_ready.sem, v_ready.at(i - 1))
                    if pre_norm:
                        pe.wait_ge(normed.sem, normed.at(i))
                        src = xn[:]
                    else:
                        pe.wait_ge(x_loaded.of(u), x_loaded.at(i, u))
                        src = x[:, u]
                    if has_ctx:
                        pe.wait_ge(c_loaded.of(u), c_loaded.at(i, u))
                    for t in range(2):
                        mm = nc.tensor.transpose(lead_ps[:, 128 * t:128 * t + 128], src[:, t, :], ident[:])
                    if has_ctx:
                        for t in range(2):
                            mm = nc.tensor.transpose(lead_ps[:, 256 + 128 * t:384 + 128 * t], c[:, u, t, :], ident[:])
                    mm.then_inc(xT_done.sem, 1)

                def project_qk(i):
                    pe.wait_ge(xT_ready.sem, xT_ready.at(i))
                    nc.tensor.matmul(lead_ps[:, 0:256], wq[:], q_src, start=True, stop=True)
                    nc.tensor.matmul(lead_ps[:, 256:512], wk[:], kv_once, start=True, stop=True).then_inc(
                        qk_done.sem, 1)
                    if rope:
                        pe.wait_ge(qk_taken.sem, qk_taken.at(i))
                        nc.tensor.matmul(lead_ps[:, 0:256], wqs[:], q_src, start=True, stop=True)
                        nc.tensor.matmul(lead_ps[:, 256:512], wks[:], kv_once, start=True, stop=True).then_inc(
                            qs_done.sem, 1)

                def project_v(i):
                    if rope:
                        pe.wait_ge(qs_taken.sem, qs_taken.at(i))
                    else:
                        pe.wait_ge(qk_taken.sem, qk_taken.at(i))
                    for b in range(4):
                        mm = nc.tensor.matmul(lead_ps[:, 128 * b:128 * b + 128],
                                              kvT[:, b].rearrange("p a k -> p (a k)"), wv[:], start=True, stop=True)
                    mm.then_inc(v_done.sem, 1)

                def scores(i, u):
                    if mask is not None:
                        pe.wait_ge(masked.sem, masked.at(i - 1))
                    else:
                        pe.wait_ge(shifted.sem, shifted.at(i - 1))
                    pe.wait_ge(km_ready.sem, km_ready.at(i))
                    if rope:
                        pe.wait_ge(rot_ready.sem, rot_ready.at(i))
                    else:
                        pe.wait_ge(qk_taken.sem, qk_taken.at(i))
                    if causal:
                        for g in range(4):
                            nc.tensor.matmul(S_ps[:, g, :], sel_q[:], future[:], start=True, stop=False,
                                             skip_group_check=True)
                    for b in range(4):
                        t, b2 = b // 2, b % 2
                        for g in range(4):
                            rows = slice(32 * g, 32 * g + 32)
                            mm = nc.tensor.matmul(
                                S_ps[64 * b2:64 * b2 + 64, g, 256 * t:256 * t + 256], qT[rows, u, 64 * b:64 * b + 64],
                                km[rows, u, b].rearrange("p h k -> p (h k)"), start=not causal, stop=True,
                                skip_group_check=causal)
                    mm.then_inc(s_done.sem, 1)

                def turn_p(i, u, t):
                    pe.wait_ge(p_ready.sem, p_ready.at(i))
                    pe.wait_ge(pT_ready.sem, pT_ready.at(i, t))
                    for g in range(4):
                        for jj in range(2):
                            c0 = 128 * (2 * g + jj)
                            mm = nc.tensor.transpose(
                                ps[:, 6 + c0 // 512, c0 % 512:c0 % 512 + 128],
                                P_g[:, u, g, t, 2 * jj:2 * jj + 2, :].rearrange("p h k -> p (h k)"), ident[:])
                    mm.then_inc(pT_done.sem, 1)

                def values(i, u, t):
                    pe.wait_ge(pT_ready.sem, pT_ready.at(i, t + 1))
                    pe.wait_ge(v_ready.sem, v_ready.at(i))
                    pe.wait_ge(res_taken.sem, res_taken.at(i - 1))
                    for b2 in range(2):
                        tok = 128 * t + 64 * b2
                        for g in range(4):
                            for jj in range(2):
                                c0 = 128 * (2 * g + jj) + 64 * b2
                                mm = nc.tensor.matmul(ps[32 * g:32 * g + 32, 5, tok:tok + 64],
                                                      vbd[:, u, 2 * t + b2, g, jj, :], pT[:, t, c0:c0 + 64],
                                                      start=jj == 0, stop=jj == 1)
                    mm.then_inc(o_done.sem, 1)

                def project_o(i):
                    pe.wait_ge(oT_ready.sem, oT_ready.at(i))
                    for t in range(2):
                        mm = nc.tensor.matmul(Y_ps[:, 128 * t:128 * t + 128], oT[:, 128 * t:128 * t + 128], wo[:],
                                              start=True, stop=True)
                    mm.then_inc(y_done.sem, 1)

                def quad(i, u, lead, trail):
                    scores(i, u)
                    if trail:
                        turn_p(i - 1, 1 - u, 0)
                    if lead:
                        turn(i + 1, 1 - u)
                    if trail:
                        values(i - 1, 1 - u, 0)
                        turn_p(i - 1, 1 - u, 1)
                    if lead:
                        project_qk(i + 1)
                    if trail:
                        values(i - 1, 1 - u, 1)
                    if lead:
                        project_v(i + 1)
                    if trail:
                        project_o(i - 1)

                pe.wait_ge(w_loaded.sem, w_loaded.at(0))
                pe.wait_ge(consts_set.sem, consts_set.at(0))
                turn(0, 0)
                project_qk(0)
                project_v(0)
                quad(0, 0, True, False)
                with pe.Fori(0, (QUADS - 2) // 2) as r:
                    for h in range(2):
                        quad(2 * r + (1 + h), (1 + h) % 2, True, True)
                quad(QUADS - 1, 1, False, True)
                for t in range(2):
                    turn_p(QUADS - 1, 1, t)
                    values(QUADS - 1, 1, t)
                project_o(QUADS - 1)

            @block.scalar
            def _(act):
                def take_x(i):
                    act.wait_ge(xT_done.sem, xT_done.at(i))
                    act.wait_ge(v_done.sem, v_done.at(i - 1))
                    if has_ctx:
                        nc.scalar.copy(xT[:], lead_ps[:, 0:256]).then_inc(xT_ready.sem, 1)
                    kv = lead_ps[:, 256:512] if has_ctx else lead_ps[:, 0:256]
                    nc.scalar.activation(kvT[:], kv.rearrange("p (b a k) -> p b a k", b=4, a=1).to_broadcast([128, 4, 2, 64]),
                                         ACT.Identity, scale=norm_w[:, 0:1] if pre_norm else 1.0).then_inc(xT_ready.sem, 1)

                def take_qk(i, u):
                    if rope:
                        return
                    act.wait_ge(qk_done.sem, qk_done.at(i))
                    act.wait_ge(km_ready.sem, km_ready.at(i - 1))
                    act.wait_ge(s_done.sem, s_done.at(i - 2))
                    if qkv_bias:
                        nc.scalar.activation(kT[:], lead_ps[:, 256:512], ACT.Identity, bias=bk[:, 0:1]).then_inc(
                            qk_taken.sem, 1)
                        nc.scalar.activation(qT[:, u], lead_ps[:, 0:256], ACT.Identity, bias=bq[:, 0:1]).then_inc(
                            qk_taken.sem, 1)
                    else:
                        nc.scalar.copy(kT[:], lead_ps[:, 256:512]).then_inc(qk_taken.sem, 1)
                        nc.scalar.copy(qT[:, u], lead_ps[:, 0:256]).then_inc(qk_taken.sem, 1)

                def exponentials(i, u):
                    act.wait_ge(shifted.sem, shifted.at(i))
                    nc.scalar.activation(p[:, u], p[:, u], ACT.Exp, scale=SCALE).then_inc(exp_done.sem, 1)

                def take_p(i, t):
                    act.wait_ge(pT_done.sem, pT_done.at(i, t + 1))
                    act.wait_ge(o_done.sem, o_done.at(i - 1))
                    nc.scalar.copy(pT[:, t], ps[:, 6:8, :].rearrange("p a n -> p (a n)")).then_inc(pT_ready.sem, 1)

                def take_o(i):
                    act.wait_ge(o_done.sem, o_done.at(i))
                    act.wait_ge(y_done.sem, y_done.at(i - 1))
                    nc.scalar.copy(oT[:], ps[:, 5, 0:256]).then_inc(oT_ready.sem, 1)

                def quad(i, u, lead, trail):
                    if trail:
                        take_p(i - 1, 0)
                    if lead:
                        take_x(i + 1)
                    if mask is None:
                        exponentials(i, u)
                    if trail:
                        take_p(i - 1, 1)
                    if lead:
                        take_qk(i + 1, 1 - u)
                    if trail:
                        take_o(i - 1)
                    if mask is not None:
                        exponentials(i, u)

                act.wait_ge(w_loaded.sem, w_loaded.at(0))
                take_x(0)
                take_qk(0, 0)
                quad(0, 0, True, False)
                with act.Fori(0, (QUADS - 2) // 2) as r:
                    for h in range(2):
                        quad(2 * r + (1 + h), (1 + h) % 2, True, True)
                quad(QUADS - 1, 1, False, True)
                take_p(QUADS - 1, 0)
                take_p(QUADS - 1, 1)
                take_o(QUADS - 1)

            @block.gpsimd
            def _(pool):
                def norm_scale(i):
                    pool.wait_ge(normed.sem, normed.at(i, 4))
                    nc.gpsimd.tensor_tensor(nrstd[:], nsq[:], norm_eps[:], ALU.add).then_inc(nrstd_ready.sem, 1)
                    pool.wait_ge(nrstd_ready.sem, nrstd_ready.at(i, 1))
                    nc.gpsimd.tensor_tensor(nrstd[:], nrstd[:], half_neg[:], ALU.pow).then_inc(nrstd_ready.sem, 1)

                def mask_heads(i, u):
                    pool.wait_ge(s_done.sem, s_done.at(i - 2))
                    if rope:
                        pool.wait_ge(rot_ready.sem, rot_ready.at(i, 1))
                    else:
                        pool.wait_ge(qk_taken.sem, qk_taken.at(i, 1))
                    nc.gpsimd.tensor_tensor(
                        km[:, u], kT[:].rearrange("p (b a k) -> p b a k", b=4, a=1).to_broadcast([128, 4, 4, 64]),
                        head_mask[:].rearrange("p (a h c) -> p a h c", a=1, c=1).to_broadcast([128, 4, 4, 64]),
                        ALU.mult).then_inc(km_ready.sem, 1)

                def normalise(i, u):
                    pool.wait_ge(rec_ready.sem, rec_ready.at(i))
                    v = p[:, u].rearrange("p (c k) -> p c k", k=64)
                    nc.gpsimd.tensor_tensor(v, v, rec[:].rearrange("p (c a) -> p c a", a=1).to_broadcast([128, 32, 64]),
                                            ALU.mult).then_inc(p_ready.sem, 1)

                def add_bias(i, u):
                    pool.wait_ge(xr_loaded.of(u), xr_loaded.at(i, u))
                    nc.gpsimd.tensor_tensor(xr[:, u], xr[:, u],
                                            bo[:].rearrange("p (a d) -> p a d", a=1).to_broadcast([128, 2, 128]),
                                            ALU.add).then_inc(biased.sem, 1)

                def tail_scale(i):
                    pool.wait_ge(tailed.sem, tailed.at(i, 4))
                    nc.gpsimd.tensor_tensor(rstd[:], mv[:, :, 1], eps[:], ALU.add).then_inc(rstd_ready.sem, 1)
                    pool.wait_ge(rstd_ready.sem, rstd_ready.at(i, 1))
                    nc.gpsimd.tensor_tensor(rstd[:], rstd[:], half_neg[:], ALU.pow).then_inc(rstd_ready.sem, 1)

                def lead_steps(i, u):
                    mask_heads(i, u)

                def quad(i, u, lead, trail, end=True, ahead=True):
                    if end and tail != "none":
                        tail_scale(i - 2)
                    if ahead and pre_norm:
                        norm_scale(i + 2)
                    if trail and qkv_bias:
                        add_bias(i - 1, 1 - u)
                    if lead:
                        lead_steps(i + 1, 1 - u)
                    normalise(i, u)

                nc.gpsimd.memset(half_neg[:], -0.5).then_inc(half_set.sem, 1)
                nc.gpsimd.memset(eps[:], LN_EPS).then_inc(half_set.sem, 1)
                if pre_norm:
                    nc.gpsimd.memset(norm_eps[:], w["norm_eps"]).then_inc(half_set.sem, 1)
                pool.wait_ge(half_set.sem, half_set.at(0))
                pool.wait_ge(w_loaded.sem, w_loaded.at(0))
                if pre_norm:
                    norm_scale(0)
                lead_steps(0, 0)
                if pre_norm:
                    norm_scale(1)
                quad(0, 0, True, False, False)
                quad(1, 1, True, True, False)
                quad(2, 0, True, True)
                with pool.Fori(1, (QUADS - 4) // 2) as r:
                    for h in range(2):
                        quad(2 * r + (1 + h), (1 + h) % 2, True, True)
                quad(QUADS - 3, 1, True, True)
                quad(QUADS - 2, 0, True, True, True, False)
                quad(QUADS - 1, 1, False, True, True, False)
                if tail != "none":
                    tail_scale(QUADS - 2)
                if qkv_bias:
                    add_bias(QUADS - 1, 1)
                if tail != "none":
                    tail_scale(QUADS - 1)

            @block.vector
            def _(dve):
                def set_constants():
                    nc.vector.memset(vbd[:], 0.0).then_inc(consts_set.sem, 1)
                    if causal:
                        dve.wait_ge(w_loaded.sem, w_loaded.at(0))
                        nc.vector.tensor_copy(sel_q[:], sel_q32[:]).then_inc(consts_set.sem, 1)
                        nc.vector.tensor_copy(future[:], future32[:]).then_inc(consts_set.sem, 1)

                def pre(i, u):
                    dve.wait_ge(x_loaded.of(u), x_loaded.at(i, u))
                    for t in range(2):
                        ins = nc.vector.bn_stats(nstats[:, t], x[:, u, t])
                    ins.then_inc(normed.sem, 1)
                    dve.wait_ge(normed.sem, normed.at(i, 1))
                    nc.vector.tensor_copy(seen[:, 1:2], nstats[:, 0, 0:1])
                    for t in range(2):
                        ins = nc.vector.bn_aggr(nmv[:, t], nstats[:, t])
                    ins.then_inc(normed.sem, 1)
                    dve.wait_ge(normed.sem, normed.at(i, 2))
                    nc.vector.tensor_tensor(nsq[:], nmv[:, :, 0], nmv[:, :, 0], ALU.mult).then_inc(normed.sem, 1)
                    dve.wait_ge(normed.sem, normed.at(i, 3))
                    nc.vector.tensor_tensor(nsq[:], nsq[:], nmv[:, :, 1], ALU.add).then_inc(normed.sem, 1)
                    dve.wait_ge(nrstd_ready.sem, nrstd_ready.at(i))
                    dve.wait_ge(xT_done.sem, xT_done.at(i - 1))
                    for t in range(2):
                        nc.vector.tensor_scalar(xn[:, t], x[:, u, t], nrstd[:, t:t + 1], None, ALU.mult).then_inc(
                            normed.sem, 1)

                def times_cos(i, u):
                    dve.wait_ge(qk_done.sem, qk_done.at(i))
                    dve.wait_ge(rot_ready.sem, rot_ready.at(i - 1))
                    dve.wait_ge(cs_loaded.of(u), cs_loaded.at(i, u))
                    for z, b in enumerate((bq, bk)):
                        nc.vector.scalar_tensor_tensor(qc[:, z], lead_ps[:, 256 * z:256 * z + 256], b[:, 0:1], cs[:, u, 0],
                                                       ALU.add, ALU.mult).then_inc(qk_taken.sem, 1)

                def rotate(i, u):
                    dve.wait_ge(qs_done.sem, qs_done.at(i))
                    for z, b in enumerate((bqs, bks)):
                        nc.vector.scalar_tensor_tensor(qs[:, z], lead_ps[:, 256 * z:256 * z + 256], b[:, 0:1], cs[:, u, 1],
                                                       ALU.add, ALU.mult).then_inc(qs_taken.sem, 1)
                    dve.wait_ge(qs_taken.sem, qs_taken.at(i))
                    dve.wait_ge(km_ready.sem, km_ready.at(i - 1))
                    nc.vector.tensor_tensor(kT[:], qc[:, 1], qs[:, 1], ALU.add).then_inc(rot_ready.sem, 1)
                    dve.wait_ge(s_done.sem, s_done.at(i - 2))
                    nc.vector.tensor_tensor(qT[:, u], qc[:, 0], qs[:, 0], ALU.add).then_inc(rot_ready.sem, 1)

                def lay_values(i, u):
                    dve.wait_ge(v_done.sem, v_done.at(i))
                    dve.wait_ge(o_done.sem, o_done.at(i - 2))
                    for h2 in range(2):
                        rows = slice(64 * h2, 64 * h2 + 64)
                        dst = vbd[rows, u].rearrange("p b g j e -> p (b g) (j e)")
                        dst = diagonal(dst, h2)
                        src = ps[rows, 4, :].rearrange("p (c j h e) -> p c j h e", j=2, h=2, e=8)[:, :, :, h2]
                        if qkv_bias:
                            bias = bv[rows].rearrange("p b (g j h e) -> p (b g) j h e", j=2, h=2, e=8)[:, :, :, h2]
                            nc.vector.tensor_tensor(dst, src, bias, ALU.add).then_inc(v_ready.sem, 1)
                        else:
                            nc.vector.tensor_copy(dst, src).then_inc(v_ready.sem, 1)

                def softmax_shift(i, u):
                    dve.wait_ge(s_done.sem, s_done.at(i))
                    dve.wait_ge(pT_done.sem, pT_done.at(i - 2))
                    src = S_ps.rearrange("p g (c k) -> p (g c) k", k=64)
                    dst = p[:, u].rearrange("p (c k) -> p c k", k=64)
                    if mask is not None:
                        dve.wait_ge(mk_loaded.of(u), mk_loaded.at(i, u))
                        for t in range(2):
                            m = mk[:, u, t].rearrange("p (a c k) -> p a c k", a=1, c=1).to_broadcast([128, 4, 4, 64])
                            nc.vector.tensor_tensor(P_g[:, u, :, t], S_ps.rearrange("p g (t h k) -> p g t h k", t=2, h=4)[
                                :, :, t], m, ALU.mult).then_inc(masked.sem, 1)
                        dve.wait_ge(masked.sem, masked.at(i))
                        nc.vector.tensor_scalar(dead[:], p[:, u], 0.0, -1e9 / SCALE, ALU.is_equal, ALU.mult).then_inc(
                            dead_ready.sem, 1)
                        dve.wait_ge(dead_ready.sem, dead_ready.at(i))
                        nc.vector.tensor_tensor(p[:, u], p[:, u], dead[:], ALU.add).then_inc(s_masked.sem, 1)
                        dve.wait_ge(s_masked.sem, s_masked.at(i))
                        src = dst
                    nc.vector.reduce_max(top[:], src, AX.X).then_inc(top_ready.sem, 1)
                    dve.wait_ge(top_ready.sem, top_ready.at(i))
                    nc.vector.tensor_tensor(dst, src, top[:].rearrange("p (c a) -> p c a", a=1).to_broadcast([128, 32, 64]),
                                            ALU.subtract).then_inc(shifted.sem, 1)

                def sums(i, u):
                    dve.wait_ge(exp_done.sem, exp_done.at(i))
                    nc.vector.reduce_sum(total[:], p[:, u].rearrange("p (c k) -> p c k", k=64), AX.X).then_inc(
                        summed.sem, 1)
                    dve.wait_ge(p_ready.sem, p_ready.at(i - 1))
                    dve.wait_ge(summed.sem, summed.at(i))
                    nc.vector.reciprocal(rec[:], total[:]).then_inc(rec_ready.sem, 1)

                def finish(i, u):
                    dve.wait_ge(y_done.sem, y_done.at(i))
                    if qkv_bias:
                        dve.wait_ge(biased.sem, biased.at(i))
                    else:
                        dve.wait_ge(xr_loaded.of(u), xr_loaded.at(i, u))
                    if tail != "none":
                        dve.wait_ge(tailed.sem, tailed.at(i - 1))
                    proj = Y_ps.rearrange("p (t d) -> p t d", t=2)
                    if tail == "none":
                        dve.wait_ge(y_stored.of(u), y_stored.at(i - 2, u))
                        nc.vector.tensor_tensor(y[:, u], proj, xr[:, u], ALU.add).then_inc(res_taken.sem, 1)
                        return
                    nc.vector.tensor_tensor(res[:], proj, xr[:, u], ALU.add).then_inc(res_taken.sem, 1)
                    dve.wait_ge(res_taken.sem, res_taken.at(i))
                    for t in range(2):
                        nc.vector.bn_stats(stats[:, t], res[:, t]).then_inc(tailed.sem, 1)
                    dve.wait_ge(tailed.sem, tailed.at(i, 2))
                    nc.vector.tensor_copy(seen[:, 0:1], stats[:, 0, 0:1])
                    for t in range(2):
                        nc.vector.bn_aggr(mv[:, t], stats[:, t]).then_inc(tailed.sem, 1)

                def scale(i, u):
                    dve.wait_ge(rstd_ready.sem, rstd_ready.at(i))
                    dve.wait_ge(y_stored.of(u), y_stored.at(i - 2, u))
                    for t in range(2):
                        nc.vector.tensor_scalar(y[:, u, t], res[:, t], mv[:, t, 0:1], rstd[:, t:t + 1],
                                                ALU.subtract, ALU.mult).then_inc(tailed.sem, 1)
                    if tail == "affine":
                        dve.wait_ge(tailed.sem, tailed.at(i, 6))
                        nc.vector.tensor_tensor(y[:, u], y[:, u], lnw[:].rearrange("p (a d) -> p a d", a=1).to_broadcast(
                            [128, 2, 128]), ALU.mult).then_inc(tailed.sem, 1)
                        dve.wait_ge(tailed.sem, tailed.at(i, 7))
                        nc.vector.tensor_tensor(y[:, u], y[:, u], lnb[:].rearrange("p (a d) -> p a d", a=1).to_broadcast(
                            [128, 2, 128]), ALU.add).then_inc(tailed.sem, 1)

                def quad(i, u, lead, end=True, ahead=True):
                    if end:
                        finish(i - 2, u)
                    softmax_shift(i, u)
                    if ahead and pre_norm:
                        pre(i + 2, u)
                    if end and tail != "none":
                        scale(i - 2, u)
                    if lead and rope:
                        times_cos(i + 1, 1 - u)
                    sums(i, u)
                    if lead and rope:
                        rotate(i + 1, 1 - u)
                    if lead:
                        lay_values(i + 1, 1 - u)

                set_constants()
                if pre_norm:
                    pre(0, 0)
                dve.wait_ge(w_loaded.sem, w_loaded.at(0))
                dve.wait_ge(consts_set.sem, consts_set.at(0))
                if rope:
                    times_cos(0, 0)
                    rotate(0, 0)
                lay_values(0, 0)
                if pre_norm:
                    pre(1, 1)
                quad(0, 0, True, False)
                quad(1, 1, True, False)
                quad(2, 0, True)
                with dve.Fori(1, (QUADS - 4) // 2) as r:
                    for h in range(2):
                        quad(2 * r + (1 + h), (1 + h) % 2, True)
                quad(QUADS - 3, 1, True)
                quad(QUADS - 2, 0, True, True, False)
                quad(QUADS - 1, 1, False, True, False)
                for h in range(2):
                    finish(QUADS - 2 + h, h)
                    if tail != "none":
                        scale(QUADS - 2 + h, h)


def mamba(nc, sems, ps, dram, x_in, x_out):
    CHUNKS, N, G = TILES // 4, 64, 2
    GROUPS = N // G
    SLOTS, AHEAD = 8, 2
    LOG1P = [1.0, -1 / 2, 1 / 3, -1 / 4, 1 / 5, -1 / 6, 1 / 7]
    NORM_EPS = 1e-5
    with ExitStack() as mem:
        st = Stage(nc, sems, mem, "mb")
        ident = st.sb("ident", [128, 128])
        sel = st.sb("sel", [128, N], BF16)
        sel_f = st.sb("sel_f", [128, N])
        norm_w = st.sb("norm_w", [128, 1])
        w_in = st.sb("w_in", [128, 4, 128])
        conv_w = st.sb("conv_w", [128, 2, 4])
        conv_b = st.sb("conv_b", [128, 2])
        w_dt = st.sb("w_dt", [128, 2, 2, 128])
        dt_b = st.sb("dt_b", [128, 2])
        w_bc = st.sb("w_bc", [128, 2, 2, 128])
        a_neg = st.sb("a_neg", [128, N])
        w_out = st.sb("w_out", [128, 2, 128])
        x = st.sb("x", [128, 2, 4, 128])
        xn = st.sb("xn", [128, 4, 128])
        xT = st.sb("xT", [128, 512])
        xpad = st.sb("xpad", [128, 2, 8, 67])
        cv = st.sb("cv", [128, 2, 8, 64])
        xc = st.sb("xc", [128, 2, 512])
        zs = st.sb("zs", [128, 2, 2, 512])
        ex = st.sb("ex", [128, 2, 512])
        lp = st.sb("lp", [128, 2, 512])
        dt = st.sb("dt", [128, 2, 2, 8, 64])
        w = st.sb("w", [128, 2, 2, 512])
        bc = st.sb("bc", [128, 2, 512])
        rest = st.sb("rest", [64, 2, 512])
        mid = st.sb("mid", [64, 2, 512], BF16)
        bc_hi = st.sb("bc_hi", [128, 2, 2, 512], BF16)
        bc_lo = st.sb("bc_lo", [128, 2, 2, 512], BF16)
        Bb = st.sb("Bb", [128, 2, G, 512])
        dA = st.sb("dA", [128, SLOTS, G, 8, 64])
        h = st.sb("h", [128, SLOTS, G, 512])
        yz = st.sb("yz", [128, 2, 512])
        y = st.sb("y", [128, 2, 4, 128])
        stats = st.sb("stats", [128, 4, 6])
        mv = st.sb("mv", [128, 4, 2])
        msq = st.sb("msq", [128, 4])
        nrstd = st.sb("nrstd", [128, 4])
        half_neg = st.sb("half_neg", [128, 4])
        eps = st.sb("eps", [128, 4])
        seen = st.sb("seen", [128, 1])

        loads = [(ident[:], dram["ident"]), (sel_f[:], dram["mb_sel"]), (norm_w[:], dram["mb_norm_w"]),
                 (w_in[:], dram["mb_in"]), (conv_w[:], dram["mb_conv_w"]), (conv_b[:], dram["mb_conv_b"]),
                 (w_dt[:], dram["mb_dt"]), (dt_b[:], dram["mb_dt_b"]), (w_bc[:], dram["mb_bc"]),
                 (a_neg[:], bcast_rows(dram["mb_a_log"])), (w_out[:], dram["mb_out"])]
        K = 2 * GROUPS
        w_loaded = st.dma_signal("w_loaded", len(loads))
        x_loaded = st.slot_signal("x_loaded")
        y_stored = st.slot_signal("y_stored")
        set_pool = st.counter("set_pool", 4 + SLOTS)
        set_act = st.counter("set_act", 2)
        set_dve = st.counter("set_dve", 1)
        normed = st.counter("normed", 5)
        nrstd_ready = st.counter("nrstd_ready", 2)
        xT_done = st.counter("xT_done")
        xT_ready = st.counter("xT_ready")
        in_done = st.counter("in_done", 4)
        in_taken = st.counter("in_taken", 4)
        conv_step = st.counter("conv_step", 8)
        xc_ready = st.counter("xc_ready", 2)
        bc_done = st.counter("bc_done", 2)
        bc_taken = st.counter("bc_taken", 2)
        hi_ready = st.counter("hi_ready", 2)
        rest_ready = st.counter("rest_ready", 2)
        mid_ready = st.counter("mid_ready", 1)
        lo_ready = st.counter("lo_ready", 1)
        dt_done = st.counter("dt_done", 2)
        ex_ready = st.counter("ex_ready", 2)
        dt_step = st.counter("dt_step", 20)
        b_done = st.counter("b_done", N)
        b_taken = st.counter("b_taken", N)
        c_done = st.counter("c_done", GROUPS)
        dA_ready = st.counter("dA_ready", K)
        u_ready = st.counter("u_ready", K)
        scanned = st.counter("scanned", K)
        weighed = st.counter("weighed", K)
        summed = st.counter("summed", K)
        gated = st.counter("gated", 2)
        out_done = st.counter("out_done")
        y_ready = st.counter("y_ready")

        def bcast_sel(n):
            return sel[:, n:n + 1].to_broadcast([128, 128])

        def loop(eng, chunk, first, last):
            first()
            chunk(0, 0, True, False)
            with eng.Fori(0, (CHUNKS - 2) // 2) as r:
                for v in range(2):
                    chunk(2 * r + (1 + v), (1 + v) % 2, True, True)
            chunk(CHUNKS - 1, (CHUNKS - 1) % 2, False, True)
            last(CHUNKS - 1, (CHUNKS - 1) % 2)

        st.begin()
        with nc.Block() as block:

            @block.sync
            def _(sp):
                for dst, src in loads:
                    sp.dma_start(dst, src).then_inc(w_loaded.sem, 16)

                def load(i, u):
                    sp.wait_ge(y_ready.sem, y_ready.at(i - 2))
                    sp.dma_start(x[:, u], tiles_of(x_in, i, 4)).then_inc(x_loaded.of(u), 16)

                def store(i, u):
                    sp.wait_ge(y_ready.sem, y_ready.at(i))
                    sp.dma_start(tiles_of(x_out, i, 4), y[:, u]).then_inc(y_stored.of(u), 16)

                load(0, 0)
                load(1, 1)
                with sp.Fori(0, CHUNKS // 2 - 1) as r:
                    for u in range(2):
                        store(2 * r + u, u)
                        load(2 * r + (u + 2), u)
                for u in range(2):
                    store(CHUNKS - 2 + u, u)
                for u in range(2):
                    sp.wait_ge(y_stored.of(u), y_stored.at(CHUNKS - 2 + u, u))

            @block.tensor
            def _(pe):
                def turn(i):
                    pe.wait_ge(normed.sem, normed.at(i))
                    pe.wait_ge(y_ready.sem, y_ready.at(i - 2))
                    for t in range(4):
                        mm = nc.tensor.transpose(ps[:, 1, 128 * t:128 * t + 128], xn[:, t], ident[:])
                    mm.then_inc(xT_done.sem, 1)

                def project_in(i, m):
                    if m == 0:
                        pe.wait_ge(xT_ready.sem, xT_ready.at(i))
                    else:
                        pe.wait_ge(in_taken.sem, in_taken.at(i, m))
                    nc.tensor.matmul(ps[:, 1, :], w_in[:, m], xT[:], start=True, stop=True).then_inc(in_done.sem, 1)

                def project_bc(i, z):
                    if z == 0:
                        pe.wait_ge(in_taken.sem, in_taken.at(i))
                        pe.wait_ge(xc_ready.sem, xc_ready.at(i))
                    else:
                        pe.wait_ge(bc_taken.sem, bc_taken.at(i, 1))
                    nc.tensor.matmul(ps[:, 1, :], w_bc[:, 0, z], xc[:, 0], start=True, stop=False)
                    nc.tensor.matmul(ps[:, 1, :], w_bc[:, 1, z], xc[:, 1], start=False, stop=True).then_inc(bc_done.sem, 1)

                def project_dt(i, f):
                    if f == 0:
                        pe.wait_ge(bc_taken.sem, bc_taken.at(i))
                    else:
                        pe.wait_ge(ex_ready.sem, ex_ready.at(i, 1))
                    nc.tensor.matmul(ps[:, 1, :], w_dt[:, 0, f], xc[:, 0], start=True, stop=False)
                    nc.tensor.matmul(ps[:, 1, :], w_dt[:, 1, f], xc[:, 1], start=False, stop=True).then_inc(dt_done.sem, 1)

                pieces = {6: turn} | {8 + 2 * m: lambda i, m=m: project_in(i, m) for m in range(4)} | {
                    16: lambda i: project_bc(i, 0), 18: lambda i: project_bc(i, 1),
                    20: lambda i: project_dt(i, 0), 22: lambda i: project_dt(i, 1)}

                def spread_b(i, u, q, j):
                    n = G * q + j
                    pe.wait_ge(b_taken.sem, b_taken.at(i, n))
                    if n == 0:
                        pe.wait_ge(lo_ready.sem, lo_ready.at(i))
                    nc.tensor.matmul(ps[:, 0, :], bcast_sel(n), bc_hi[:, u, 0], start=True, stop=False)
                    nc.tensor.matmul(ps[:, 0, :], bcast_sel(n), bc_lo[:, u, 0], start=False, stop=True).then_inc(
                        b_done.sem, 1)

                def spread_c(i, u, q):
                    pe.wait_ge(weighed.sem, weighed.at(i, 2 * (q - 1)))
                    if q == 0:
                        pe.wait_ge(lo_ready.sem, lo_ready.at(i))
                    for j in range(G):
                        n, bank = G * q + j, 2 + 2 * (q % 2) + j
                        nc.tensor.matmul(ps[:, bank, :], bcast_sel(n), bc_hi[:, u, 1], start=True, stop=False)
                        mm = nc.tensor.matmul(ps[:, bank, :], bcast_sel(n), bc_lo[:, u, 1], start=False, stop=True)
                    mm.then_inc(c_done.sem, 1)

                def sum_state(i, q, f, j):
                    if j == 0:
                        pe.wait_ge(weighed.sem, weighed.at(i, 2 * q + f + 1))
                        if q == 0:
                            pe.wait_ge(gated.sem, gated.at(i - 1))
                    mm = nc.tensor.matmul(ps[:, 6 + f, :], ident[:], h[:, (2 * q + f) % SLOTS, j], start=q == 0 and j == 0,
                                          stop=q == GROUPS - 1 and j == G - 1)
                    if j == G - 1:
                        mm.then_inc(summed.sem, 1)

                def project_out(i):
                    pe.wait_ge(gated.sem, gated.at(i))
                    if isinstance(i, int) and i == CHUNKS - 1:
                        pe.wait_ge(ex_ready.sem, ex_ready.at(i))
                    else:
                        pe.wait_ge(ex_ready.sem, ex_ready.at(i + 1))
                    for t in range(4):
                        for f in range(2):
                            mm = nc.tensor.matmul(ps[:, 1, 128 * t:128 * t + 128], yz[:, f, 128 * t:128 * t + 128],
                                                  w_out[:, f], start=f == 0, stop=f == 1)
                    mm.then_inc(out_done.sem, 1)

                def first():
                    pe.wait_ge(w_loaded.sem, w_loaded.at(0))
                    pe.wait_ge(set_act.sem, set_act.at(0))
                    for q in sorted(pieces):
                        pieces[q](0)
                    for q in range(AHEAD):
                        for j in range(G):
                            spread_b(0, 0, q, j)
                    spread_c(0, 0, 0)

                def chunk(i, u, lead, trail):
                    for q in range(GROUPS):
                        for j in range(G):
                            if q < GROUPS - AHEAD:
                                spread_b(i, u, q + AHEAD, j)
                            elif lead:
                                spread_b(i + 1, 1 - u, q + AHEAD - GROUPS, j)
                            if j == 0:
                                if q < GROUPS - 1:
                                    spread_c(i, u, q + 1)
                                elif lead:
                                    spread_c(i + 1, 1 - u, 0)
                            for g in range(G):
                                if q >= 1:
                                    sum_state(i, q - 1, j, g)
                                elif trail:
                                    sum_state(i - 1, GROUPS - 1, j, g)
                        if q == 1 and trail:
                            project_out(i - 1)
                        if lead and q in pieces:
                            pieces[q](i + 1)

                def last(i, u):
                    for f in range(2):
                        for j in range(G):
                            sum_state(i, GROUPS - 1, f, j)
                    project_out(i)

                loop(pe, chunk, first, last)

            @block.scalar
            def _(act):
                def take_turn(i):
                    act.wait_ge(xT_done.sem, xT_done.at(i))
                    act.wait_ge(in_done.sem, in_done.at(i - 1))
                    nc.scalar.activation(xT[:], ps[:, 1, :], ACT.Identity, scale=norm_w[:, 0:1]).then_inc(xT_ready.sem, 1)

                def take_x(i, f):
                    act.wait_ge(in_done.sem, in_done.at(i, f + 1))
                    act.wait_ge(conv_step.sem, conv_step.at(i - 1))
                    nc.scalar.copy(xpad[:, f, :, 1:65], ps[:, 1, :].rearrange("p (b t) -> p b t", b=8)).then_inc(
                        in_taken.sem, 1)

                def take_z(i, u, f):
                    act.wait_ge(in_done.sem, in_done.at(i, f + 3))
                    act.wait_ge(gated.sem, gated.at(i - 2))
                    nc.scalar.activation(zs[:, u, f], ps[:, 1, :], ACT.Silu).then_inc(in_taken.sem, 1)

                def silu_x(i, f):
                    act.wait_ge(conv_step.sem, conv_step.at(i, 4 * f + 4))
                    act.wait_ge(dt_step.sem, dt_step.at(i - 1))
                    nc.scalar.activation(xc[:, f], cv[:, f].rearrange("p b t -> p (b t)"), ACT.Silu).then_inc(
                        xc_ready.sem, 1)

                def take_bc(i, u, z):
                    act.wait_ge(bc_done.sem, bc_done.at(i, z + 1))
                    act.wait_ge(rest_ready.sem, rest_ready.at(i - 1))
                    act.wait_ge(c_done.sem, c_done.at(i - 2))
                    nc.scalar.copy(bc[:, z], ps[:, 1, :]).then_inc(bc_taken.sem, 1)
                    act.wait_ge(bc_taken.sem, bc_taken.at(i, z + 1))
                    nc.scalar.copy(bc_hi[:, u, z], bc[:, z]).then_inc(hi_ready.sem, 1)

                def round_mid(i):
                    act.wait_ge(rest_ready.sem, rest_ready.at(i, 1))
                    act.wait_ge(lo_ready.sem, lo_ready.at(i - 1))
                    nc.scalar.copy(mid[:], rest[:]).then_inc(mid_ready.sem, 1)

                def exp_dt(i, f):
                    act.wait_ge(dt_done.sem, dt_done.at(i, f + 1))
                    act.wait_ge(dt_step.sem, dt_step.at(i - 1))
                    nc.scalar.activation(ex[:, f], ps[:, 1, :], ACT.Exp, bias=dt_b[:, f:f + 1]).then_inc(ex_ready.sem, 1)

                pieces = {6: [lambda i, u: take_turn(i)], 8: [lambda i, u: take_x(i, 0)],
                          10: [lambda i, u: take_x(i, 1)], 12: [lambda i, u: take_z(i, u, 0), lambda i, u: silu_x(i, 0)],
                          14: [lambda i, u: take_z(i, u, 1), lambda i, u: silu_x(i, 1)],
                          16: [lambda i, u: take_bc(i, u, 0)], 18: [lambda i, u: take_bc(i, u, 1)],
                          20: [lambda i, u: exp_dt(i, 0)], 22: [lambda i, u: exp_dt(i, 1)],
                          24: [lambda i, u: round_mid(i)]}

                def take_b(i, q, j):
                    act.wait_ge(b_done.sem, b_done.at(i, G * q + j + 1))
                    if j == 0:
                        act.wait_ge(u_ready.sem, u_ready.at(i, 2 * (q - 1)))
                    nc.scalar.copy(Bb[:, q % 2, j], ps[:, 0, :]).then_inc(b_taken.sem, 1)

                def decay(i, u, q, f):
                    k = 2 * q + f
                    act.wait_ge(scanned.sem, scanned.at(i, k + 1 - SLOTS))
                    if q == 0:
                        act.wait_ge(dt_step.sem, dt_step.at(i))
                    for j in range(G):
                        n = G * q + j
                        ins = nc.scalar.activation(dA[:, k % SLOTS, j, :, 1:64], dt[:, u, f, :, 1:64], ACT.Exp,
                                                   scale=a_neg[:, n:n + 1])
                    ins.then_inc(dA_ready.sem, 1)

                def first():
                    act.wait_ge(w_loaded.sem, w_loaded.at(0))
                    nc.scalar.copy(sel[:], sel_f[:]).then_inc(set_act.sem, 1)
                    nc.scalar.activation(a_neg[:], a_neg[:], ACT.Exp).then_inc(set_act.sem, 1)
                    act.wait_ge(set_pool.sem, set_pool.at(0))
                    act.wait_ge(set_dve.sem, set_dve.at(0))
                    for q in sorted(pieces):
                        for piece in pieces[q]:
                            piece(0, 0)
                    for q in range(AHEAD):
                        for j in range(G):
                            take_b(0, q, j)
                    for f in range(2):
                        decay(0, 0, 0, f)

                def chunk(i, u, lead, trail):
                    for q in range(GROUPS):
                        end = q == GROUPS - 1
                        if not end:
                            decay(i, u, q + 1, 0)
                        elif lead:
                            decay(i + 1, 1 - u, 0, 0)
                        for j in range(G):
                            if q < GROUPS - AHEAD:
                                take_b(i, q + AHEAD, j)
                            elif lead:
                                take_b(i + 1, q + AHEAD - GROUPS, j)
                        if lead and q in pieces:
                            for piece in pieces[q]:
                                piece(i + 1, 1 - u)
                        if not end:
                            decay(i, u, q + 1, 1)
                        elif lead:
                            decay(i + 1, 1 - u, 0, 1)

                loop(act, chunk, first, lambda i, u: None)

            @block.gpsimd
            def _(pool):
                def norm_scale(i):
                    pool.wait_ge(normed.sem, normed.at(i, 4))
                    nc.gpsimd.tensor_tensor(nrstd[:], msq[:], eps[:], ALU.add).then_inc(nrstd_ready.sem, 1)
                    pool.wait_ge(nrstd_ready.sem, nrstd_ready.at(i, 1))
                    nc.gpsimd.tensor_tensor(nrstd[:], nrstd[:], half_neg[:], ALU.pow).then_inc(nrstd_ready.sem, 1)


                def take_rest(i, u):
                    pool.wait_ge(nrstd_ready.sem, nrstd_ready.at(i))
                    pool.wait_ge(u_ready.sem, u_ready.at(i - 1, 2 * 21 + 1))
                    pool.wait_ge(hi_ready.sem, hi_ready.at(i))
                    pool.wait_ge(lo_ready.sem, lo_ready.at(i - 1))
                    nc.gpsimd.tensor_tensor(rest[:], bc[0:64], bc_hi[0:64, u], ALU.subtract).then_inc(rest_ready.sem, 1)
                    pool.wait_ge(rest_ready.sem, rest_ready.at(i, 1))

                def take_mid(i, u):
                    pool.wait_ge(u_ready.sem, u_ready.at(i - 1, 2 * 23 + 1))
                    nc.gpsimd.tensor_tensor(bc_hi[64:128, u], bc[64:128], bc_hi[64:128, u], ALU.subtract).then_inc(
                        rest_ready.sem, 1)
                    pool.wait_ge(rest_ready.sem, rest_ready.at(i, 2))

                def take_lo(i, u):
                    pool.wait_ge(u_ready.sem, u_ready.at(i - 1, 2 * 27 + 1))
                    pool.wait_ge(mid_ready.sem, mid_ready.at(i))
                    nc.gpsimd.tensor_tensor(bc_lo[0:64, u], rest[:], mid[:], ALU.subtract).then_inc(lo_ready.sem, 1)
                    pool.wait_ge(lo_ready.sem, lo_ready.at(i))

                pieces = {4: lambda i, u: norm_scale(i), 20: take_rest, 22: take_mid, 26: take_lo}

                def inputs(i, u, q, f):
                    k = 2 * q + f
                    pool.wait_ge(summed.sem, summed.at(i, k + 1 - SLOTS))
                    if f == 0:
                        pool.wait_ge(b_taken.sem, b_taken.at(i, G * (q + 1)))
                    if q == 0:
                        pool.wait_ge(dt_step.sem, dt_step.at(i))
                    nc.gpsimd.tensor_tensor(h[:, k % SLOTS], Bb[:, q % 2],
                                            w[:, u, f].rearrange("p (a t) -> p a t", a=1).to_broadcast([128, G, 512]),
                                            ALU.mult).then_inc(u_ready.sem, 1)

                def first():
                    nc.gpsimd.memset(half_neg[:], -0.5).then_inc(set_pool.sem, 1)
                    nc.gpsimd.memset(eps[:], NORM_EPS).then_inc(set_pool.sem, 1)
                    nc.gpsimd.memset(xpad[:], 0.0).then_inc(set_pool.sem, 1)
                    nc.gpsimd.memset(bc_lo[:], 0.0).then_inc(set_pool.sem, 1)
                    for s in range(SLOTS):
                        nc.gpsimd.memset(dA[:, s, :, :, 0:1], 0.0).then_inc(set_pool.sem, 1)
                    pool.wait_ge(set_pool.sem, set_pool.at(0))
                    for q in sorted(pieces):
                        pieces[q](0, 0)
                    for f in range(2):
                        inputs(0, 0, 0, f)

                def chunk(i, u, lead, trail):
                    for q in range(GROUPS):
                        for f in range(2):
                            if q < GROUPS - 1:
                                inputs(i, u, q + 1, f)
                            elif lead:
                                inputs(i + 1, 1 - u, 0, f)
                            if f == 0 and lead and q in pieces:
                                pieces[q](i + 1, 1 - u)

                loop(pool, chunk, first, lambda i, u: None)

            @block.vector
            def _(dve):
                def norm(i, u):
                    dve.wait_ge(x_loaded.of(u), x_loaded.at(i, u))
                    for t in range(4):
                        ins = nc.vector.bn_stats(stats[:, t], x[:, u, t])
                    ins.then_inc(normed.sem, 1)
                    dve.wait_ge(normed.sem, normed.at(i, 1))
                    nc.vector.tensor_copy(seen[:], stats[:, 0, 0:1])
                    for t in range(4):
                        ins = nc.vector.bn_aggr(mv[:, t], stats[:, t])
                    ins.then_inc(normed.sem, 1)
                    dve.wait_ge(normed.sem, normed.at(i, 2))
                    nc.vector.tensor_tensor(msq[:], mv[:, :, 0], mv[:, :, 0], ALU.mult).then_inc(normed.sem, 1)
                    dve.wait_ge(normed.sem, normed.at(i, 3))
                    nc.vector.tensor_tensor(msq[:], msq[:], mv[:, :, 1], ALU.add).then_inc(normed.sem, 1)

                def scale(i, u):
                    dve.wait_ge(nrstd_ready.sem, nrstd_ready.at(i))
                    dve.wait_ge(xT_done.sem, xT_done.at(i - 1))
                    for t in range(4):
                        ins = nc.vector.tensor_scalar(xn[:, t], x[:, u, t], nrstd[:, t:t + 1], None, ALU.mult)
                    ins.then_inc(normed.sem, 1)

                def conv(i, f):
                    dve.wait_ge(in_taken.sem, in_taken.at(i, f + 1))
                    dve.wait_ge(xc_ready.sem, xc_ready.at(i - 1))
                    nc.vector.tensor_scalar(cv[:, f], xpad[:, f, :, 0:64], conv_w[:, f, 0:1], conv_b[:, f:f + 1], ALU.mult,
                                            ALU.add).then_inc(conv_step.sem, 1)
                    for k in range(1, 4):
                        dve.wait_ge(conv_step.sem, conv_step.at(i, 4 * f + k))
                        nc.vector.scalar_tensor_tensor(cv[:, f], xpad[:, f, :, k:k + 64], conv_w[:, f, k:k + 1], cv[:, f],
                                                       ALU.mult, ALU.add).then_inc(conv_step.sem, 1)

                def step(i, f, k, ins):
                    ins.then_inc(dt_step.sem, 1)
                    dve.wait_ge(dt_step.sem, dt_step.at(i, 10 * f + k))

                def make_dt(i, u, f):
                    e, p, d = ex[:, f], lp[:, f], dt[:, u, f].rearrange("p b t -> p (b t)")
                    dve.wait_ge(ex_ready.sem, ex_ready.at(i, f + 1))
                    dve.wait_ge(dA_ready.sem, dA_ready.at(i - 2))
                    dve.wait_ge(u_ready.sem, u_ready.at(i - 2))
                    step(i, f, 1, nc.vector.tensor_scalar(e, e, 0.11, None, ALU.min))
                    step(i, f, 2, nc.vector.tensor_scalar(p, e, LOG1P[6], LOG1P[5], ALU.mult, ALU.add))
                    step(i, f, 3, nc.vector.tensor_tensor(p, p, e, ALU.mult))
                    for n, c in enumerate(LOG1P[4::-1]):
                        step(i, f, 4 + n, nc.vector.scalar_tensor_tensor(p, p, c, e, ALU.add, ALU.mult))
                    step(i, f, 9, nc.vector.tensor_scalar(d, p, 1e-3, 0.1, ALU.max, ALU.min))
                    step(i, f, 10, nc.vector.tensor_tensor(w[:, u, f], d, xc[:, f], ALU.mult))

                pieces = {4: norm, 6: scale, 10: lambda i, u: conv(i, 0), 12: lambda i, u: conv(i, 1),
                          22: lambda i, u: make_dt(i, u, 0), 24: lambda i, u: make_dt(i, u, 1)}

                def scan(i, q, f):
                    k = 2 * q + f
                    dve.wait_ge(dA_ready.sem, dA_ready.at(i, k + 1))
                    dve.wait_ge(u_ready.sem, u_ready.at(i, k + 1))
                    s = k % SLOTS
                    nc.vector.tensor_tensor_scan(h[:, s].rearrange("p n t -> p (n t)"),
                                                 dA[:, s].rearrange("p n b t -> p (n b t)"),
                                                 h[:, s].rearrange("p n t -> p (n t)"), 0.0, ALU.mult, ALU.add).then_inc(
                                                     scanned.sem, 1)

                def weigh(i, q, f):
                    k = 2 * q + f
                    dve.wait_ge(scanned.sem, scanned.at(i, k + 1))
                    dve.wait_ge(c_done.sem, c_done.at(i, q + 1))
                    c = 2 + 2 * (q % 2)
                    nc.vector.tensor_tensor(h[:, k % SLOTS], h[:, k % SLOTS], ps[:, c:c + 2, :], ALU.mult).then_inc(weighed.sem, 1)

                def gating(i, u):
                    dve.wait_ge(summed.sem, summed.at(i))
                    dve.wait_ge(out_done.sem, out_done.at(i - 1))
                    for f in range(2):
                        nc.vector.tensor_tensor(yz[:, f], ps[:, 6 + f, :], zs[:, u, f], ALU.mult).then_inc(gated.sem, 1)

                def output(i, u):
                    dve.wait_ge(out_done.sem, out_done.at(i))
                    dve.wait_ge(y_stored.of(u), y_stored.at(i - 2, u))
                    nc.vector.tensor_tensor(y[:, u], ps[:, 1, :].rearrange("p (t d) -> p t d", t=4), x[:, u],
                                            ALU.add).then_inc(y_ready.sem, 1)

                def first():
                    dve.wait_ge(w_loaded.sem, w_loaded.at(0))
                    dve.wait_ge(set_act.sem, set_act.at(0))
                    nc.vector.tensor_scalar(a_neg[:], a_neg[:], -1.0, None, ALU.mult).then_inc(set_dve.sem, 1)
                    dve.wait_ge(set_pool.sem, set_pool.at(0))
                    for q in sorted(pieces):
                        pieces[q](0, 0)

                def chunk(i, u, lead, trail):
                    for q in range(GROUPS):
                        scan(i, q, 0)
                        if q == 1 and trail:
                            gating(i - 1, 1 - u)
                        weigh(i, q, 0)
                        scan(i, q, 1)
                        if q == 2 and trail:
                            output(i - 1, 1 - u)
                        if lead and q in pieces:
                            pieces[q](i + 1, 1 - u)
                        weigh(i, q, 1)

                def last(i, u):
                    gating(i, u)
                    output(i, u)

                loop(dve, chunk, first, last)


def rope_tables(nc, sems, dram, tables):
    PARTS = 128 // 8
    N = B * S // PARTS
    TWO_PI = 2 * np.pi
    C1 = 6.28125
    C2 = float(np.float32(np.floor((TWO_PI - C1) * 2.0 ** 21) / 2.0 ** 21))
    C3 = float(TWO_PI - C1 - C2)
    ROUND = 1.5 * 2.0 ** 23
    PI_IN = 3.1415925
    with ExitStack() as mem:
        st = Stage(nc, sems, mem, "rope")
        freq = st.sb("freq", [128, 1])
        sign = st.sb("sign", [128, 1])
        pos_i = st.sb("pos_i", [128, N], I32)
        angle = st.sb("angle", [128, N])
        count = st.sb("count", [128, 2, N])
        turned = st.sb("turned", [128, 2, N])
        loaded = st.dma_signal("loaded", 2 + PARTS)
        cast = st.counter("cast", 2)
        reduced = st.counter("reduced", 14)
        sine = st.counter("sine", 2)
        signed = st.counter("signed")
        stored = st.dma_signal("stored", 2 * PARTS)
        st.begin()
        with nc.Block() as block:

            @block.sync
            def _(sp):
                sp.dma_start(freq[:], dram["rope_freq"]).then_inc(loaded.sem, 16)
                sp.dma_start(sign[:], dram["rope_sign"]).then_inc(loaded.sem, 16)
                for c in range(PARTS):
                    sp.dma_start(pos_i[8 * c:8 * c + 8, :], bcast_rows(dram["pos"][N * c:N * c + N], 8)).then_inc(
                        loaded.sem, 16)
                for z, ready in enumerate((sine, signed)):
                    sp.wait_ge(ready.sem, ready.at(0, 1))
                    for c in range(PARTS):
                        sp.dma_start(tables[z][:, N * c:N * c + N], turned[8 * c:8 * c + 8, z]).then_inc(stored.sem, 16)
                sp.wait_ge(stored.sem, stored.at(0))

            @block.vector
            def _(dve):
                dve.wait_ge(loaded.sem, loaded.at(0))
                nc.vector.tensor_copy(angle[:], pos_i[:]).then_inc(cast.sem, 1)
                dve.wait_ge(cast.sem, cast.at(0, 1))
                nc.vector.tensor_scalar(angle[:], angle[:], freq[:, 0:1], None, ALU.mult).then_inc(cast.sem, 1)
                dve.wait_ge(cast.sem, cast.at(0, 2))
                for z, shift in enumerate((0.25, 0.0)):
                    k, n, v = 7 * z, count[:, z], turned[:, z]
                    steps = [lambda: nc.vector.tensor_scalar(n, angle[:], 1.0 / TWO_PI, shift, ALU.mult, ALU.add),
                             lambda: nc.vector.tensor_scalar(n, n, ROUND, None, ALU.add),
                             lambda: nc.vector.tensor_scalar(n, n, ROUND, None, ALU.subtract),
                             lambda: nc.vector.scalar_tensor_tensor(v, n, -C1, angle[:], ALU.mult, ALU.add),
                             lambda: nc.vector.scalar_tensor_tensor(v, n, -C2, v, ALU.mult, ALU.add),
                             lambda: nc.vector.scalar_tensor_tensor(v, n, -C3, v, ALU.mult, ALU.add)]
                    if z == 0:
                        steps.append(lambda: nc.vector.tensor_scalar(v, v, np.pi / 2, PI_IN, ALU.add, ALU.min))
                    else:
                        steps.append(lambda: nc.vector.tensor_scalar(v, v, PI_IN, -PI_IN, ALU.min, ALU.max))
                    for m, step in enumerate(steps):
                        step().then_inc(reduced.sem, 1)
                        dve.wait_ge(reduced.sem, reduced.at(0, k + m + 1))
                dve.wait_ge(sine.sem, sine.at(0))
                nc.vector.tensor_scalar(turned[:, 1], turned[:, 1], sign[:, 0:1], None, ALU.mult).then_inc(signed.sem, 1)

            @block.scalar
            def _(act):
                for z in range(2):
                    act.wait_ge(reduced.sem, reduced.at(0, 7 * z + 7))
                    nc.scalar.activation(turned[:, z], turned[:, z], ACT.Sin).then_inc(sine.sem, 1)


def swiglu(nc, sems, ps, name, dram, x_skip, x_in, x_out):
    moe = name == "mo"
    E = 9 if moe else 1
    CHUNKS = TILES // 4
    norm_eps = 1e-6 if moe else 1e-5
    with ExitStack() as mem:
        st = Stage(nc, sems, mem, name)
        ident = st.sb("ident", [128, 128])
        norm_w = st.sb("norm_w", [128, 1])
        wg = st.sb("wg", [128, E, 256])
        wu = st.sb("wu", [128, E, 256])
        wd = st.sb("wd", [128, E, 2, 128])
        x = st.sb("x", [128, 2, 4, 128])
        skip = st.sb("skip", [128, 2, 4, 128])
        xn = st.sb("xn", [128, 4, 128])
        hT = st.sb("hT", [128, 2, 512])
        gate = st.sb("gate", [128, 2, 512])
        gu = st.sb("gu", [128, 4, 512])
        acc = st.sb("acc", [128, 4, 128])
        y = st.sb("y", [128, 2, 4, 128])
        stats = st.sb("stats", [128, 4, 6])
        mv = st.sb("mv", [128, 4, 2])
        msq = st.sb("msq", [128, 4])
        nrstd = st.sb("nrstd", [128, 4])
        ystats = st.sb("ystats", [128, 4, 6])
        ymv = st.sb("ymv", [128, 4, 2])
        rstd = st.sb("rstd", [128, 4])
        half_neg = st.sb("half_neg", [128, 4])
        eps = st.sb("eps", [128, 4])
        eps_n = st.sb("eps_n", [128, 4])
        seen = st.sb("seen", [128, 2])
        loads = [(ident[:], dram["ident"]), (norm_w[:], dram[name + "norm_w"])]
        loads += [(wg[:], dram[name + "wg"]), (wu[:], dram[name + "wu"]), (wd[:], dram[name + "wd"])]
        if moe:
            wr = st.sb("wr", [128, 8])
            order = st.sb("order", [128, 8])
            loads += [(wr[:], dram["router"]), (order[:], bcast_rows(dram["order"]))]
            lg = st.sb("lg", [128, 4, 8])
            pr = st.sb("pr", [128, 4, 8])
            cand = st.sb("cand", [128, 4, 8])
            one1 = st.sb("one1", [128, 4, 8])
            one2 = st.sb("one2", [128, 4, 8])
            r1 = st.sb("r1", [128, 4])
            m1 = st.sb("m1", [128, 4])
            m2 = st.sb("m2", [128, 4])
            comb = st.sb("comb", [128, 4, 8])
        w_loaded = st.dma_signal("w_loaded", len(loads))
        x_loaded = st.slot_signal("x_loaded", 2)
        y_stored = st.slot_signal("y_stored", 1)
        half_set = st.counter("half_set", 3)
        normed = st.counter("normed", 5)
        nrstd_ready = st.counter("nrstd_ready", 2)
        xT_done = st.counter("xT_done")
        hT_ready = st.counter("hT_ready")
        gu_done = st.counter("gu_done", 2 * E)
        gate_ready = st.counter("gate_ready", 2 * E)
        gu_ready = st.counter("gu_ready", 2 * E)
        down_done = st.counter("down_done", E)
        acc_set = st.counter("acc_set")
        added = st.counter("added", E)
        r_done = st.counter("r_done")
        r_step = st.counter("r_step", 24)
        r_exp = st.counter("r_exp", 2)
        tailed = st.counter("tailed", 2)
        y_ready = st.counter("y_ready")
        rstd_ready = st.counter("rstd_ready", 2)

        st.begin()
        with nc.Block() as block:

            @block.sync
            def _(sp):
                for dst, src in loads:
                    sp.dma_start(dst, src).then_inc(w_loaded.sem, 16)

                def load(i, u):
                    sp.wait_ge(y_ready.sem, y_ready.at(i - 2))
                    sp.dma_start(x[:, u], tiles_of(x_in, i, 4)).then_inc(x_loaded.of(u), 16)
                    sp.dma_start(skip[:, u], tiles_of(x_skip, i, 4)).then_inc(x_loaded.of(u), 16)

                def store(i, u):
                    sp.wait_ge(y_ready.sem, y_ready.at(i))
                    sp.dma_start(tiles_of(x_out, i, 4), y[:, u]).then_inc(y_stored.of(u), 16)

                load(0, 0)
                load(1, 1)
                with sp.Fori(0, CHUNKS // 2 - 1) as r:
                    for u in range(2):
                        store(2 * r + u, u)
                        load(2 * r + (u + 2), u)
                for u in range(2):
                    store(CHUNKS - 2 + u, u)
                for u in range(2):
                    sp.wait_ge(y_stored.of(u), y_stored.at(CHUNKS - 2 + u, u))

            @block.tensor
            def _(pe):
                def turn(i):
                    pe.wait_ge(normed.sem, normed.at(i))
                    pe.wait_ge(hT_ready.sem, hT_ready.at(i - 1))
                    for t in range(4):
                        mm = nc.tensor.transpose(ps[:, 6, 128 * t:128 * t + 128], xn[:, t], ident[:])
                    mm.then_inc(xT_done.sem, 1)

                def route(i, u):
                    pe.wait_ge(hT_ready.sem, hT_ready.at(i))
                    pe.wait_ge(r_step.sem, r_step.at(i - 1))
                    for t in range(4):
                        mm = nc.tensor.matmul(ps[:, 7, 8 * t:8 * t + 8], hT[:, u, 128 * t:128 * t + 128], wr[:],
                                              start=True, stop=True)
                    mm.then_inc(r_done.sem, 1)

                def gate_up(i, u, n):
                    e, f, b = n // 2, n % 2, 2 * (n % 2)
                    if n >= 2:
                        pe.wait_ge(gu_ready.sem, gu_ready.at(i, n - 1))
                    else:
                        pe.wait_ge(gu_ready.sem, gu_ready.at(i - 1))
                        pe.wait_ge(hT_ready.sem, hT_ready.at(i))
                    nc.tensor.matmul(ps[:, b, :], wg[:, e, 128 * f:128 * f + 128], hT[:, u], start=True, stop=True)
                    nc.tensor.matmul(ps[:, b + 1, :], wu[:, e, 128 * f:128 * f + 128], hT[:, u], start=True,
                                     stop=True).then_inc(gu_done.sem, 1)

                def down(i, e):
                    pe.wait_ge(gu_ready.sem, gu_ready.at(i, 2 * e + 2))
                    if e >= 2:
                        pe.wait_ge(added.sem, added.at(i, e - 1))
                    else:
                        pe.wait_ge(added.sem, added.at(i - 1))
                    s = 2 * (e % 2)
                    for t in range(4):
                        for f in range(2):
                            mm = nc.tensor.matmul(ps[:, 4 + e % 2, 128 * t:128 * t + 128],
                                                  gu[:, s + f, 128 * t:128 * t + 128], wd[:, e, f], start=f == 0,
                                                  stop=f == 1)
                    mm.then_inc(down_done.sem, 1)

                def chunk(i, u, lead):
                    if moe:
                        route(i, u)
                    for n in range(2 * E):
                        gate_up(i, u, n)
                        if n >= 3 and n % 2:
                            down(i, (n - 3) // 2)
                        if n == min(3, 2 * E - 1) and lead:
                            turn(i + 1)
                    down(i, E - 1)

                pe.wait_ge(w_loaded.sem, w_loaded.at(0))
                turn(0)
                with pe.Fori(0, CHUNKS // 2 - 1) as r:
                    for u in range(2):
                        chunk(2 * r + u, u, True)
                chunk(CHUNKS - 2, 0, True)
                chunk(CHUNKS - 1, 1, False)

            @block.scalar
            def _(act):
                def take(i, u):
                    act.wait_ge(xT_done.sem, xT_done.at(i))
                    act.wait_ge(gu_done.sem, gu_done.at(i - 2))
                    nc.scalar.activation(hT[:, u], ps[:, 6, :], ACT.Identity, scale=norm_w[:, 0:1]).then_inc(
                        hT_ready.sem, 1)

                def router_exp(i):
                    act.wait_ge(r_step.sem, r_step.at(i, 2))
                    nc.scalar.activation(pr[:], lg[:], ACT.Exp).then_inc(r_exp.sem, 1)
                    act.wait_ge(r_step.sem, r_step.at(i, 17))
                    nc.scalar.activation(m2[:], m2[:], ACT.Exp).then_inc(r_exp.sem, 1)

                def gates(i, n):
                    act.wait_ge(gu_done.sem, gu_done.at(i, n + 1))
                    if n >= 2:
                        act.wait_ge(gu_ready.sem, gu_ready.at(i, n - 1))
                    else:
                        act.wait_ge(gu_ready.sem, gu_ready.at(i - 1))
                    nc.scalar.activation(gate[:, n % 2], ps[:, 2 * (n % 2), :], ACT.Silu).then_inc(gate_ready.sem, 1)

                def chunk(i, u, lead):
                    if moe:
                        router_exp(i)
                    for n in range(2 * E):
                        gates(i, n)
                        if n == min(5, 2 * E - 1) and lead:
                            take(i + 1, 1 - u)

                act.wait_ge(w_loaded.sem, w_loaded.at(0))
                take(0, 0)
                with act.Fori(0, CHUNKS // 2 - 1) as r:
                    for u in range(2):
                        chunk(2 * r + u, u, True)
                chunk(CHUNKS - 2, 0, True)
                chunk(CHUNKS - 1, 1, False)

            @block.gpsimd
            def _(pool):
                def norm_scale(i):
                    pool.wait_ge(normed.sem, normed.at(i, 4))
                    nc.gpsimd.tensor_tensor(nrstd[:], msq[:], eps_n[:], ALU.add).then_inc(nrstd_ready.sem, 1)
                    pool.wait_ge(nrstd_ready.sem, nrstd_ready.at(i, 1))
                    nc.gpsimd.tensor_tensor(nrstd[:], nrstd[:], half_neg[:], ALU.pow).then_inc(nrstd_ready.sem, 1)

                def tail_scale(i):
                    pool.wait_ge(tailed.sem, tailed.at(i))
                    nc.gpsimd.tensor_tensor(rstd[:], ymv[:, :, 1], eps[:], ALU.add).then_inc(rstd_ready.sem, 1)
                    pool.wait_ge(rstd_ready.sem, rstd_ready.at(i, 1))
                    nc.gpsimd.tensor_tensor(rstd[:], rstd[:], half_neg[:], ALU.pow).then_inc(rstd_ready.sem, 1)

                nc.gpsimd.memset(half_neg[:], -0.5).then_inc(half_set.sem, 1)
                nc.gpsimd.memset(eps[:], LN_EPS).then_inc(half_set.sem, 1)
                nc.gpsimd.memset(eps_n[:], norm_eps).then_inc(half_set.sem, 1)
                pool.wait_ge(half_set.sem, half_set.at(0))
                norm_scale(0)
                with pool.Fori(0, CHUNKS - 1) as i:
                    norm_scale(i + 1)
                    tail_scale(i)
                tail_scale(CHUNKS - 1)

            @block.vector
            def _(dve):
                def pre(i, u):
                    dve.wait_ge(x_loaded.of(u), x_loaded.at(i, u))
                    for t in range(4):
                        ins = nc.vector.bn_stats(stats[:, t], x[:, u, t])
                    ins.then_inc(normed.sem, 1)
                    dve.wait_ge(normed.sem, normed.at(i, 1))
                    nc.vector.tensor_copy(seen[:, 0:1], stats[:, 0, 0:1])
                    for t in range(4):
                        ins = nc.vector.bn_aggr(mv[:, t], stats[:, t])
                    ins.then_inc(normed.sem, 1)
                    dve.wait_ge(normed.sem, normed.at(i, 2))
                    nc.vector.tensor_tensor(msq[:], mv[:, :, 0], mv[:, :, 0], ALU.mult).then_inc(normed.sem, 1)
                    dve.wait_ge(normed.sem, normed.at(i, 3))
                    nc.vector.tensor_tensor(msq[:], msq[:], mv[:, :, 1], ALU.add).then_inc(normed.sem, 1)
                    dve.wait_ge(nrstd_ready.sem, nrstd_ready.at(i))
                    dve.wait_ge(xT_done.sem, xT_done.at(i - 1))
                    for t in range(4):
                        ins = nc.vector.tensor_scalar(xn[:, t], x[:, u, t], nrstd[:, t:t + 1], None, ALU.mult)
                    ins.then_inc(normed.sem, 1)

                def start_acc(i, u):
                    dve.wait_ge(x_loaded.of(u), x_loaded.at(i, u))
                    dve.wait_ge(y_ready.sem, y_ready.at(i - 1))
                    nc.vector.tensor_tensor(acc[:], x[:, u], skip[:, u], ALU.add).then_inc(acc_set.sem, 1)

                def multiply(i, n):
                    e = n // 2
                    dve.wait_ge(gate_ready.sem, gate_ready.at(i, n + 1))
                    if e >= 2:
                        dve.wait_ge(down_done.sem, down_done.at(i, e - 1))
                    else:
                        dve.wait_ge(down_done.sem, down_done.at(i - 1))
                    nc.vector.tensor_tensor(gu[:, n % 4], gate[:, n % 2], ps[:, 2 * (n % 2) + 1, :], ALU.mult).then_inc(
                        gu_ready.sem, 1)

                def add(i, e):
                    dve.wait_ge(down_done.sem, down_done.at(i, e + 1))
                    out = ps[:, 4 + e % 2, :].rearrange("p (t d) -> p t d", t=4)
                    if e == 0:
                        dve.wait_ge(acc_set.sem, acc_set.at(i))
                        nc.vector.tensor_tensor(acc[:], acc[:], out, ALU.add).then_inc(added.sem, 1)
                        return
                    dve.wait_ge(added.sem, added.at(i, e))
                    if e == 1:
                        dve.wait_ge(r_step.sem, r_step.at(i))
                    for t in range(4):
                        ins = nc.vector.scalar_tensor_tensor(acc[:, t], out[:, t], comb[:, t, e - 1:e], acc[:, t],
                                                             ALU.mult, ALU.add)
                    ins.then_inc(added.sem, 1)

                def finish(i, u):
                    dve.wait_ge(added.sem, added.at(i))
                    for t in range(4):
                        ins = nc.vector.bn_stats(ystats[:, t], acc[:, t])
                    ins.then_inc(tailed.sem, 1)
                    dve.wait_ge(tailed.sem, tailed.at(i, 1))
                    nc.vector.tensor_copy(seen[:, 1:2], ystats[:, 0, 0:1])
                    for t in range(4):
                        ins = nc.vector.bn_aggr(ymv[:, t], ystats[:, t])
                    ins.then_inc(tailed.sem, 1)
                    dve.wait_ge(rstd_ready.sem, rstd_ready.at(i))
                    dve.wait_ge(y_stored.of(u), y_stored.at(i - 2, u))
                    for t in range(4):
                        ins = nc.vector.tensor_scalar(y[:, u, t], acc[:, t], ymv[:, t, 0:1], rstd[:, t:t + 1],
                                                      ALU.subtract, ALU.mult)
                    ins.then_inc(y_ready.sem, 1)

                def wide(v):
                    return v.rearrange("p (t a) -> p t a", a=1).to_broadcast([128, 4, 8])

                def step(i, k, ins):
                    ins.then_inc(r_step.sem, 1)
                    dve.wait_ge(r_step.sem, r_step.at(i, k))

                def pick(i, k, src, top, onehot):
                    step(i, k + 1, nc.vector.reduce_max(top[:], src[:], AX.X))
                    step(i, k + 2, nc.vector.tensor_tensor(cand[:], src[:], wide(top[:]), ALU.is_equal))
                    step(i, k + 3, nc.vector.tensor_tensor(
                        cand[:], cand[:], order[:].rearrange("p (a e) -> p a e", a=1).to_broadcast([128, 4, 8]), ALU.mult))
                    step(i, k + 4, nc.vector.reduce_max(r1[:], cand[:], AX.X))
                    step(i, k + 5, nc.vector.tensor_tensor(onehot[:], cand[:], wide(r1[:]), ALU.is_equal))

                def router(i):
                    dve.wait_ge(r_done.sem, r_done.at(i))
                    logits = ps[:, 7, 0:32].rearrange("p (t e) -> p t e", t=4)
                    step(i, 1, nc.vector.reduce_max(r1[:], logits, AX.X))
                    step(i, 2, nc.vector.tensor_tensor(lg[:], logits, wide(r1[:]), ALU.subtract))
                    dve.wait_ge(r_exp.sem, r_exp.at(i, 1))
                    step(i, 3, nc.vector.reduce_sum(r1[:], pr[:], AX.X))
                    step(i, 4, nc.vector.reciprocal(r1[:], r1[:]))
                    step(i, 5, nc.vector.tensor_tensor(pr[:], pr[:], wide(r1[:]), ALU.mult))
                    pick(i, 5, pr, m1, one1)
                    step(i, 11, nc.vector.scalar_tensor_tensor(pr[:], one1[:], -4.0, pr[:], ALU.mult, ALU.add))
                    pick(i, 11, pr, m2, one2)
                    step(i, 17, nc.vector.tensor_tensor(m2[:], m2[:], m1[:], ALU.subtract))
                    dve.wait_ge(r_exp.sem, r_exp.at(i, 2))
                    step(i, 18, nc.vector.tensor_scalar(m1[:], m2[:], 1.0, None, ALU.add))
                    step(i, 19, nc.vector.reciprocal(m1[:], m1[:]))
                    step(i, 20, nc.vector.tensor_tensor(m2[:], m2[:], m1[:], ALU.mult))
                    step(i, 21, nc.vector.tensor_tensor(one1[:], one1[:], wide(m1[:]), ALU.mult))
                    step(i, 22, nc.vector.tensor_tensor(one2[:], one2[:], wide(m2[:]), ALU.mult))
                    step(i, 23, nc.vector.tensor_tensor(comb[:], one1[:], one2[:], ALU.add))
                    step(i, 24, nc.vector.tensor_copy(cand[:, 0, 0:1], comb[:, 0, 0:1]))

                def chunk(i, u, lead):
                    start_acc(i, u)
                    if moe:
                        router(i)
                    for n in range(2 * E):
                        multiply(i, n)
                        if n >= 4 and n % 2 == 0:
                            add(i, (n - 4) // 2)
                        if n == 1 and lead:
                            pre(i + 1, 1 - u)
                    for e in range(max(E - 2, 0), E):
                        add(i, e)
                    finish(i, u)

                dve.wait_ge(w_loaded.sem, w_loaded.at(0))
                pre(0, 0)
                with dve.Fori(0, CHUNKS // 2 - 1) as r:
                    for u in range(2):
                        chunk(2 * r + u, u, True)
                chunk(CHUNKS - 2, 0, True)
                chunk(CHUNKS - 1, 1, False)


def gqa(nc, sems, ps, dram, x_in, x_out):
    QUADS = TILES // 2
    SCALE = 64.0 ** -0.5
    TURN_X, Q0, Q1, K, V, QT0, QT1, KT = range(8)
    P0, O0, OT0, P1, O1, OT1, WO, BACK = range(8)
    with ExitStack() as mem:
        st = Stage(nc, sems, mem, "gq")
        ident = st.sb("ident", [128, 128])
        wq = st.sb("wq", [128, 1024])
        wk = st.sb("wk", [128, 256])
        wv = st.sb("wv", [128, 256])
        wo = st.sb("wo", [128, 8, 128])
        cos = st.sb("cos", [128, 64])
        sin = st.sb("sin", [128, 64])
        alibi = st.sb("alibi", [128, 1024])
        x = st.sb("x", [128, 2, 2, 128])
        xr = st.sb("xr", [128, 2, 2, 128])
        xT = st.sb("xT", [128, 4, 2, 64])
        xT1 = st.sb("xT1", [128, 256])
        qc = st.sb("qc", [128, 1024])
        qs = st.sb("qs", [128, 1024])
        qr = st.sb("qr", [128, 2, 1024])
        kc = st.sb("kc", [128, 512])
        ks = st.sb("ks", [128, 512])
        kr = st.sb("kr", [128, 8, 2, 64])
        qT = st.sb("qT", [128, 2, 2, 1024])
        kbd = st.sb("kbd", [128, 2, 4, 4, 128])
        vbd = st.sb("vbd", [128, 2, 4, 4, 128])
        p = st.sb("p", [128, 2, 2048])
        top = st.sb("top", [128, 32])
        total = st.sb("total", [128, 32])
        rec = st.sb("rec", [128, 32])
        pT = st.sb("pT", [128, 1024])
        o = st.sb("o", [128, 1024])
        oT = st.sb("oT", [128, 8, 256])
        yT = st.sb("yT", [128, 256])
        res = st.sb("res", [128, 2, 128])
        stats = st.sb("stats", [128, 2, 6])
        mv = st.sb("mv", [128, 2, 2])
        rstd = st.sb("rstd", [128, 2])
        half_neg = st.sb("half_neg", [128, 2])
        eps = st.sb("eps", [128, 2])
        seen = st.sb("seen", [128, 1])
        y = st.sb("y", [128, 2, 2, 128])
        loads = [(ident[:], dram["ident"]), (wq[:], dram["g_wq"]), (wk[:], dram["g_wk"]), (wv[:], dram["g_wv"]),
                 (wo[:], dram["g_wo"]), (cos[:], dram["g_cos"]), (sin[:], dram["g_sin"]), (alibi[:], dram["g_alibi"])]
        w_loaded = st.dma_signal("w_loaded", len(loads))
        x_loaded = st.slot_signal("x_loaded")
        xr_loaded = st.slot_signal("xr_loaded")
        y_stored = st.slot_signal("y_stored")
        blank = st.counter("blank", 2)
        half_set = st.counter("half_set", 2)
        lead_done = st.counter("lead_done", 8)
        lead_taken = st.counter("lead_taken", 8)
        trail_done = st.counter("trail_done", 8)
        trail_taken = st.counter("trail_taken", 8)
        q_turned = st.counter("q_turned", 2)
        k_turned = st.counter("k_turned")
        s_done = st.counter("s_done")
        biased = st.counter("biased")
        top_ready = st.counter("top_ready")
        shifted = st.counter("shifted")
        exp_done = st.counter("exp_done")
        summed = st.counter("summed")
        rec_ready = st.counter("rec_ready")
        p_ready = st.counter("p_ready")
        tailed = st.counter("tailed", 6)
        rstd_ready = st.counter("rstd_ready", 2)

        lead_ps = ps[:, 4:6, :].rearrange("p a n -> p (a n)")
        trail_ps = ps[:, 6:8, :].rearrange("p a n -> p (a n)")
        S_ps = ps[:, 0:4, :].rearrange("p a n -> p (a n)")

        def cols(bank0, c, n):
            return slice(None), bank0 + c // 512, slice(c % 512, c % 512 + n)

        st.begin()
        with nc.Block() as block:

            @block.sync
            def _(sp):
                for dst, src in loads:
                    sp.dma_start(dst, src).then_inc(w_loaded.sem, 16)

                def lead(i, u):
                    sp.wait_ge(lead_done.sem, lead_done.at(i - 2))
                    sp.dma_start(x[:, u], tiles_of(x_in, i, 2)).then_inc(x_loaded.of(u), 16)

                def trail(i, u):
                    sp.wait_ge(trail_taken.sem, trail_taken.at(i - 2))
                    sp.dma_start(xr[:, u], tiles_of(x_in, i, 2)).then_inc(xr_loaded.of(u), 16)

                def store(i, u):
                    sp.wait_ge(tailed.sem, tailed.at(i))
                    sp.dma_start(tiles_of(x_out, i, 2), y[:, u]).then_inc(y_stored.of(u), 16)

                lead(0, 0)
                lead(1, 1)
                trail(0, 0)
                with sp.Fori(0, (QUADS - 2) // 2) as r:
                    for h in range(2):
                        i, u = 2 * r + (1 + h), (1 + h) % 2
                        lead(i + 1, 1 - u)
                        trail(i, u)
                        store(i - 1, 1 - u)
                trail(QUADS - 1, 1)
                store(QUADS - 2, 0)
                store(QUADS - 1, 1)
                for u in range(2):
                    sp.wait_ge(y_stored.of(u), y_stored.at(QUADS - 2 + u, u))

            @block.tensor
            def _(pe):
                def lead(i, u, step):
                    pe.wait_ge(lead_taken.sem, lead_taken.at(i, step))
                    if step == TURN_X:
                        pe.wait_ge(x_loaded.of(u), x_loaded.at(i, u))
                        for t in range(2):
                            mm = nc.tensor.transpose(ps[:, 4, 128 * t:128 * t + 128], x[:, u, t], ident[:])
                    elif step in (Q0, Q1):
                        t = step - Q0
                        for n in range(2):
                            mm = nc.tensor.matmul(ps[:, 4 + n, :], xT1[:, 128 * t:128 * t + 128],
                                                  wq[:, 512 * n:512 * n + 512], start=True, stop=True)
                    elif step == K:
                        for t in range(2):
                            mm = nc.tensor.matmul(ps[:, 4, 256 * t:256 * t + 256], xT1[:, 128 * t:128 * t + 128], wk[:],
                                                  start=True, stop=True)
                    elif step == V:
                        for b in range(4):
                            mm = nc.tensor.matmul(ps[cols(4, 256 * b, 256)], xT[:, b].rearrange("p a k -> p (a k)"), wv[:],
                                                  start=True, stop=True)
                    elif step in (QT0, QT1):
                        t = step - QT0
                        pe.wait_ge(q_turned.sem, q_turned.at(i, t + 1))
                        for j in range(8):
                            mm = nc.tensor.transpose(ps[cols(4, 128 * j, 128)], qr[:, t, 128 * j:128 * j + 128], ident[:])
                    else:
                        pe.wait_ge(k_turned.sem, k_turned.at(i))
                        for c in range(8):
                            mm = nc.tensor.transpose(ps[cols(4, 128 * c, 128)], kr[:, c].rearrange("p a d -> p (a d)"),
                                                     ident[:])
                    mm.then_inc(lead_done.sem, 1)

                def scores(i, u):
                    pe.wait_ge(biased.sem, biased.at(i - 1))
                    pe.wait_ge(lead_taken.sem, lead_taken.at(i))
                    nc.tensor.transpose(ps[:, 0, 0:128], ident[:], ident[:])
                    for t in range(2):
                        for b2 in range(2):
                            for j in range(8):
                                c = 1024 * t + 128 * j
                                mm = nc.tensor.matmul(
                                    ps[64 * b2:64 * b2 + 64, c // 512, c % 512:c % 512 + 128],
                                    qT[:, u, t, 128 * j + 64 * b2:128 * j + 64 * b2 + 64],
                                    kbd[:, u, 2 * t + b2, j // 2], start=True, stop=True)
                    mm.then_inc(s_done.sem, 1)

                def trail(i, u, step):
                    pe.wait_ge(trail_taken.sem, trail_taken.at(i, step))
                    if step in (P0, P1):
                        t = int(step == P1)
                        pe.wait_ge(p_ready.sem, p_ready.at(i))
                        for j in range(8):
                            c = 1024 * t + 128 * j
                            mm = nc.tensor.transpose(ps[cols(6, 128 * j, 128)], p[:, u, c:c + 128], ident[:])
                    elif step in (O0, O1):
                        t = int(step == O1)
                        nc.tensor.transpose(ps[:, 6, 0:128], ident[:], ident[:])
                        for b2 in range(2):
                            for j in range(8):
                                mm = nc.tensor.matmul(
                                    ps[64 * b2:64 * b2 + 64, 6 + j // 4, 128 * (j % 4):128 * (j % 4) + 128],
                                    pT[:, 128 * j + 64 * b2:128 * j + 64 * b2 + 64], vbd[:, u, 2 * t + b2, j // 2],
                                    start=True, stop=True)
                    elif step in (OT0, OT1):
                        for j in range(8):
                            mm = nc.tensor.transpose(ps[cols(6, 128 * j, 128)], o[:, 128 * j:128 * j + 128], ident[:])
                    elif step == WO:
                        for j in range(8):
                            mm = nc.tensor.matmul(ps[:, 6, 0:256], wo[:, j], oT[:, j], start=j == 0, stop=j == 7)
                    else:
                        for t in range(2):
                            mm = nc.tensor.transpose(ps[:, 7, 128 * t:128 * t + 128], yT[:, 128 * t:128 * t + 128], ident[:])
                    mm.then_inc(trail_done.sem, 1)

                def quad(i, u, with_lead, with_trail):
                    scores(i, u)
                    for step in range(8):
                        if with_trail:
                            trail(i - 1, 1 - u, step)
                        if with_lead:
                            lead(i + 1, 1 - u, step)

                pe.wait_ge(w_loaded.sem, w_loaded.at(0))
                for step in range(8):
                    lead(0, 0, step)
                quad(0, 0, True, False)
                with pe.Fori(0, (QUADS - 2) // 2) as r:
                    for h in range(2):
                        quad(2 * r + (1 + h), (1 + h) % 2, True, True)
                quad(QUADS - 1, 1, False, True)
                for step in range(8):
                    trail(QUADS - 1, 1, step)

            @block.scalar
            def _(act):
                def lead(i, u, step):
                    act.wait_ge(lead_done.sem, lead_done.at(i, step + 1))
                    if step == TURN_X:
                        nc.scalar.copy(xT1[:], ps[:, 4, 0:256])
                        ins = nc.scalar.activation(xT[:], ps[:, 4, 0:256].rearrange(
                            "p (b a k) -> p b a k", b=4, a=1).to_broadcast([128, 4, 2, 64]), ACT.Identity)
                    elif step in (QT0, QT1):
                        act.wait_ge(s_done.sem, s_done.at(i - 2))
                        ins = nc.scalar.copy(qT[:, u, step - QT0], lead_ps)
                    else:
                        src = lead_ps.rearrange("p (t v b k) -> p t v b k", t=2, v=4, b=2)
                        for t in range(2):
                            for h2 in range(2):
                                rows = slice(64 * h2, 64 * h2 + 64)
                                ins = nc.scalar.copy(
                                    kbd[rows, u, 2 * t:2 * t + 2, :, 64 * h2:64 * h2 + 64].rearrange("p b v k -> p v b k"),
                                    src[rows, t])
                    ins.then_inc(lead_taken.sem, 1)

                def trail(i, step):
                    act.wait_ge(trail_done.sem, trail_done.at(i, step + 1))
                    if step in (P0, P1):
                        ins = nc.scalar.copy(pT[:], trail_ps)
                    elif step in (OT0, OT1):
                        t = int(step == OT1)
                        ins = nc.scalar.copy(oT[:, :, 128 * t:128 * t + 128],
                                             trail_ps.rearrange("p (j q) -> p j q", j=8))
                    else:
                        ins = nc.scalar.copy(yT[:], ps[:, 6, 0:256])
                    ins.then_inc(trail_taken.sem, 1)

                def exponentials(i, u):
                    act.wait_ge(shifted.sem, shifted.at(i))
                    nc.scalar.activation(p[:, u], p[:, u], ACT.Exp, scale=SCALE).then_inc(exp_done.sem, 1)

                def quad(i, u, with_lead, with_trail):
                    if with_trail:
                        trail(i - 1, P0)
                    if with_lead:
                        lead(i + 1, 1 - u, TURN_X)
                    if with_trail:
                        trail(i - 1, OT0)
                        trail(i - 1, P1)
                    exponentials(i, u)
                    if with_trail:
                        trail(i - 1, OT1)
                    if with_lead:
                        lead(i + 1, 1 - u, QT0)
                    if with_trail:
                        trail(i - 1, WO)
                    if with_lead:
                        lead(i + 1, 1 - u, QT1)
                        lead(i + 1, 1 - u, KT)

                act.wait_ge(blank.sem, blank.at(0))
                for step in (TURN_X, QT0, QT1, KT):
                    lead(0, 0, step)
                quad(0, 0, True, False)
                with act.Fori(0, (QUADS - 2) // 2) as r:
                    for h in range(2):
                        quad(2 * r + (1 + h), (1 + h) % 2, True, True)
                quad(QUADS - 1, 1, False, True)
                for step in (P0, OT0, P1, OT1, WO):
                    trail(QUADS - 1, step)

            @block.gpsimd
            def _(pool):
                def turn_q(i, t):
                    pool.wait_ge(lead_taken.sem, lead_taken.at(i, Q0 + t + 1))
                    nc.gpsimd.tensor_tensor(qr[:, t], qc[:], qs[:], ALU.add).then_inc(q_turned.sem, 1)

                def turn_k(i):
                    pool.wait_ge(lead_taken.sem, lead_taken.at(i, K + 1))
                    nc.gpsimd.tensor_tensor(
                        kr[:], kc[:].rearrange("p (c a d) -> p c a d", c=8, a=1).to_broadcast([128, 8, 2, 64]),
                        ks[:].rearrange("p (c a d) -> p c a d", c=8, a=1).to_broadcast([128, 8, 2, 64]),
                        ALU.add).then_inc(k_turned.sem, 1)

                def normalise(i, u):
                    pool.wait_ge(rec_ready.sem, rec_ready.at(i))
                    v = p[:, u].rearrange("p (c k) -> p c k", k=64)
                    nc.gpsimd.tensor_tensor(v, v, rec[:].rearrange("p (c a) -> p c a", a=1).to_broadcast([128, 32, 64]),
                                            ALU.mult).then_inc(p_ready.sem, 1)

                def tail_scale(i):
                    pool.wait_ge(tailed.sem, tailed.at(i, 4))
                    nc.gpsimd.tensor_tensor(rstd[:], mv[:, :, 1], eps[:], ALU.add).then_inc(rstd_ready.sem, 1)
                    pool.wait_ge(rstd_ready.sem, rstd_ready.at(i, 1))
                    nc.gpsimd.tensor_tensor(rstd[:], rstd[:], half_neg[:], ALU.pow).then_inc(rstd_ready.sem, 1)

                def lead_steps(i):
                    turn_q(i, 0)
                    turn_q(i, 1)
                    turn_k(i)

                def quad(i, u, with_lead, with_trail):
                    if with_lead:
                        lead_steps(i + 1)
                    normalise(i, u)
                    if with_trail:
                        tail_scale(i - 1)

                nc.gpsimd.memset(half_neg[:], -0.5).then_inc(half_set.sem, 1)
                nc.gpsimd.memset(eps[:], LN_EPS).then_inc(half_set.sem, 1)
                pool.wait_ge(half_set.sem, half_set.at(0))
                lead_steps(0)
                quad(0, 0, True, False)
                with pool.Fori(0, (QUADS - 2) // 2) as r:
                    for h in range(2):
                        quad(2 * r + (1 + h), (1 + h) % 2, True, True)
                quad(QUADS - 1, 1, False, True)
                tail_scale(QUADS - 1)

            @block.vector
            def _(dve):
                def rotate(src, c, s, heads):
                    src = src.rearrange("p (h d) -> p h d", d=64)
                    cv, sv = c.rearrange("p (h d) -> p h d", d=64), s.rearrange("p (h d) -> p h d", d=64)
                    one = lambda a, n: a.rearrange("p (h d) -> p h d", h=1).to_broadcast([128, heads, n])
                    nc.vector.tensor_tensor(cv, src, one(cos[:], 64), ALU.mult)
                    nc.vector.tensor_tensor(sv[:, :, 0:32], src[:, :, 32:64], one(sin[:, 0:32], 32), ALU.mult)
                    return nc.vector.tensor_tensor(sv[:, :, 32:64], src[:, :, 0:32], one(sin[:, 32:64], 32), ALU.mult)

                def lead(i, u, step):
                    dve.wait_ge(lead_done.sem, lead_done.at(i, step + 1))
                    if step in (Q0, Q1):
                        if step == Q0:
                            dve.wait_ge(q_turned.sem, q_turned.at(i - 1))
                        else:
                            dve.wait_ge(q_turned.sem, q_turned.at(i, 1))
                        ins = rotate(lead_ps, qc[:], qs[:], 16)
                    elif step == K:
                        dve.wait_ge(k_turned.sem, k_turned.at(i - 1))
                        ins = rotate(ps[:, 4, :], kc[:], ks[:], 8)
                    else:
                        dve.wait_ge(trail_done.sem, trail_done.at(i - 2, O1 + 1))
                        for h2 in range(2):
                            rows = slice(64 * h2, 64 * h2 + 64)
                            ins = nc.vector.tensor_copy(
                                vbd[rows, u].rearrange("p b v d -> p (b v) d")[:, :, 64 * h2:64 * h2 + 64],
                                lead_ps[rows].rearrange("p (c d) -> p c d", d=64))
                    ins.then_inc(lead_taken.sem, 1)

                def take_o(i, step):
                    dve.wait_ge(trail_done.sem, trail_done.at(i, step + 1))
                    nc.vector.tensor_copy(o[:], trail_ps).then_inc(trail_taken.sem, 1)

                def softmax_shift(i, u):
                    dve.wait_ge(s_done.sem, s_done.at(i))
                    dve.wait_ge(trail_done.sem, trail_done.at(i - 2))
                    nc.vector.tensor_tensor(p[:, u].rearrange("p (t n) -> p t n", t=2), S_ps.rearrange(
                        "p (t n) -> p t n", t=2), alibi[:].rearrange("p (a n) -> p a n", a=1).to_broadcast(
                            [128, 2, 1024]), ALU.add).then_inc(biased.sem, 1)
                    v = p[:, u].rearrange("p (c k) -> p c k", k=64)
                    dve.wait_ge(biased.sem, biased.at(i))
                    nc.vector.reduce_max(top[:], v, AX.X).then_inc(top_ready.sem, 1)
                    dve.wait_ge(top_ready.sem, top_ready.at(i))
                    nc.vector.tensor_tensor(v, v, top[:].rearrange("p (c a) -> p c a", a=1).to_broadcast([128, 32, 64]),
                                            ALU.subtract).then_inc(shifted.sem, 1)

                def sums(i, u):
                    dve.wait_ge(exp_done.sem, exp_done.at(i))
                    nc.vector.reduce_sum(total[:], p[:, u].rearrange("p (c k) -> p c k", k=64), AX.X).then_inc(
                        summed.sem, 1)
                    dve.wait_ge(p_ready.sem, p_ready.at(i - 1))
                    dve.wait_ge(summed.sem, summed.at(i))
                    nc.vector.reciprocal(rec[:], total[:]).then_inc(rec_ready.sem, 1)

                def finish(i, u):
                    dve.wait_ge(trail_done.sem, trail_done.at(i))
                    dve.wait_ge(xr_loaded.of(u), xr_loaded.at(i, u))
                    dve.wait_ge(tailed.sem, tailed.at(i - 1))
                    dve.wait_ge(y_stored.of(u), y_stored.at(i - 2, u))
                    nc.vector.tensor_tensor(res[:], ps[:, 7, 0:256].rearrange("p (t d) -> p t d", t=2), xr[:, u],
                                            ALU.add).then_inc(trail_taken.sem, 1)
                    dve.wait_ge(trail_taken.sem, trail_taken.at(i))
                    for t in range(2):
                        nc.vector.bn_stats(stats[:, t], res[:, t]).then_inc(tailed.sem, 1)
                    dve.wait_ge(tailed.sem, tailed.at(i, 2))
                    nc.vector.tensor_copy(seen[:], stats[:, 0, 0:1])
                    for t in range(2):
                        nc.vector.bn_aggr(mv[:, t], stats[:, t]).then_inc(tailed.sem, 1)
                    dve.wait_ge(rstd_ready.sem, rstd_ready.at(i))
                    for t in range(2):
                        nc.vector.tensor_scalar(y[:, u, t], res[:, t], mv[:, t, 0:1], rstd[:, t:t + 1],
                                                ALU.subtract, ALU.mult).then_inc(tailed.sem, 1)

                def quad(i, u, with_lead, with_trail):
                    if with_trail:
                        take_o(i - 1, O0)
                    if with_lead:
                        lead(i + 1, 1 - u, Q0)
                    softmax_shift(i, u)
                    if with_lead:
                        lead(i + 1, 1 - u, Q1)
                        lead(i + 1, 1 - u, K)
                    if with_trail:
                        take_o(i - 1, O1)
                    if with_lead:
                        lead(i + 1, 1 - u, V)
                    sums(i, u)
                    if with_trail:
                        finish(i - 1, 1 - u)

                nc.vector.memset(kbd[:], 0.0).then_inc(blank.sem, 1)
                nc.vector.memset(vbd[:], 0.0).then_inc(blank.sem, 1)
                dve.wait_ge(blank.sem, blank.at(0))
                dve.wait_ge(w_loaded.sem, w_loaded.at(0))
                for step in (Q0, Q1, K, V):
                    lead(0, 0, step)
                quad(0, 0, True, False)
                with dve.Fori(0, (QUADS - 2) // 2) as r:
                    for h in range(2):
                        quad(2 * r + (1 + h), (1 + h) % 2, True, True)
                quad(QUADS - 1, 1, False, True)
                take_o(QUADS - 1, O0)
                take_o(QUADS - 1, O1)
                finish(QUADS - 1, 1)


def experts(nc, sems, ps, dram, x_in, t_in, x_out):
    E, F = 4, 4
    CHUNKS = TILES // 4
    with ExitStack() as mem:
        st = Stage(nc, sems, mem, "ex")
        ident = st.sb("ident", [128, 128])
        average = st.sb("average", [128, 128])
        w1 = st.sb("w1", [128, E, 512])
        b1 = st.sb("b1", [128, E, F])
        w2 = st.sb("w2", [128, E, F, 128])
        b2 = st.sb("b2", [128, E])
        lnw = st.sb("lnw", [128, E, 128])
        lnb = st.sb("lnb", [128, E, 128])
        wg = st.sb("wg", [128, E])
        bg = st.sb("bg", [128, E])
        order = st.sb("order", [128, E])
        x = st.sb("x", [128, 2, 4, 128])
        tk = st.sb("tk", [128, 2, 4, 128])
        meanT = st.sb("meanT", [128, 512])
        tT = st.sb("tT", [128, 2, 512])
        hid = st.sb("hid", [128, 2, 4, 512])
        fT = st.sb("fT", [128, 512])
        z = st.sb("z", [128, 4, 128])
        zw = st.sb("zw", [128, 2, 4, 128])
        acc = st.sb("acc", [128, 4, 128])
        y = st.sb("y", [128, 2, 4, 128])
        stats = st.sb("stats", [128, 4, 6])
        mv = st.sb("mv", [128, 4, 2])
        rstd = st.sb("rstd", [128, 4])
        half_neg = st.sb("half_neg", [128, 4])
        eps = st.sb("eps", [128, 4])
        seen = st.sb("seen", [128, 1])
        lg = st.sb("lg", [128, 4, E])
        rest = st.sb("rest", [128, 4, E])
        pr = st.sb("pr", [128, 4, E])
        cand = st.sb("cand", [128, 4, E])
        one1 = st.sb("one1", [128, 4, E])
        one2 = st.sb("one2", [128, 4, E])
        r1 = st.sb("r1", [128, 4])
        m1 = st.sb("m1", [128, 4])
        gate = st.sb("gate", [128, 4, E])
        loads = [(ident[:], dram["ident"]), (average[:], dram["average"]), (w1[:], dram["ex_w1"]), (b1[:], dram["ex_b1"]),
                 (w2[:], dram["ex_w2"]), (b2[:], dram["ex_b2"]), (wg[:], dram["ex_wg"]), (bg[:], bcast_rows(dram["ex_bg"])),
                 (order[:], bcast_rows(dram["ex_order"])),
                 (lnw[:].rearrange("p e d -> p (e d)"), bcast_rows(dram["ex_lnw"])),
                 (lnb[:].rearrange("p e d -> p (e d)"), bcast_rows(dram["ex_lnb"]))]
        w_loaded = st.dma_signal("w_loaded", len(loads))
        x_loaded = st.slot_signal("x_loaded")
        t_loaded = [st.dma_signal(f"t_loaded{s}", 2) for s in range(2)]
        y_stored = st.slot_signal("y_stored")
        half_set = st.counter("half_set", 2)
        turn_done = st.counter("turn_done", 1 + E)
        turn_taken = st.counter("turn_taken", 1 + E)
        g_done = st.counter("g_done")
        g_step = st.counter("g_step", 16)
        g_exp = st.counter("g_exp")
        up_done = st.counter("up_done", E * F)
        up_taken = st.counter("up_taken", E * F)
        down_done = st.counter("down_done", E)
        down_taken = st.counter("down_taken", E)
        back_done = st.counter("back_done", E)
        res_taken = st.counter("res_taken", E)
        st_done = st.counter("st_done", E + 1)
        mv_ready = st.counter("mv_ready", E + 1)
        rstd_ready = st.counter("rstd_ready", 2 * (E + 1))
        scaled = st.counter("scaled", E + 1)
        weighted = st.counter("weighted", E)
        shifted = st.counter("shifted", E)
        added = st.counter("added", E)
        g_end = st.counter("g_end", 3)

        st.begin()
        with nc.Block() as block:

            @block.sync
            def _(sp):
                for dst, src in loads:
                    sp.dma_start(dst, src).then_inc(w_loaded.sem, 16)

                def store(i, u):
                    sp.wait_ge(scaled.sem, scaled.at(i))
                    sp.dma_start(tiles_of(x_out, i, 4), y[:, u]).then_inc(y_stored.of(u), 16)

                def chunk(i, u, ahead):
                    if ahead:
                        sp.wait_ge(added.sem, added.at(i - 1))
                        sp.dma_start(x[:, 1 - u], tiles_of(x_in, i + 1, 4)).then_inc(x_loaded.of(1 - u), 16)
                    for e in range(E):
                        if e == 0:
                            sp.wait_ge(res_taken.sem, res_taken.at(i - 1))
                        else:
                            sp.wait_ge(res_taken.sem, res_taken.at(i, e - 1))
                        sp.dma_start(tk[:, e % 2], tiles_of(t_in[e], i, 4)).then_inc(t_loaded[e % 2].sem, 16)
                    store(i, u)

                sp.dma_start(x[:, 0], tiles_of(x_in, 0, 4)).then_inc(x_loaded.of(0), 16)
                with sp.Fori(0, CHUNKS // 2 - 1) as r:
                    for u in range(2):
                        chunk(2 * r + u, u, True)
                chunk(CHUNKS - 2, 0, True)
                chunk(CHUNKS - 1, 1, False)
                for u in range(2):
                    sp.wait_ge(y_stored.of(u), y_stored.at(CHUNKS - 2 + u, u))

            @block.tensor
            def _(pe):
                def gates(i, u):
                    pe.wait_ge(x_loaded.of(u), x_loaded.at(i, u))
                    pe.wait_ge(turn_taken.sem, turn_taken.at(i - 1))
                    for t in range(4):
                        mm = nc.tensor.matmul(ps[:, 6, 128 * t:128 * t + 128], x[:, u, t], average[:], start=True, stop=True)
                    mm.then_inc(turn_done.sem, 1)
                    pe.wait_ge(turn_taken.sem, turn_taken.at(i, 1))
                    pe.wait_ge(g_step.sem, g_step.at(i - 1))
                    for t in range(4):
                        mm = nc.tensor.matmul(ps[:, 7, E * t:E * t + E], meanT[:, 128 * t:128 * t + 128], wg[:],
                                              start=True, stop=True)
                    mm.then_inc(g_done.sem, 1)

                def turn(i, e):
                    pe.wait_ge(t_loaded[e % 2].sem, t_loaded[e % 2].at(i, e // 2 + 1))
                    pe.wait_ge(turn_taken.sem, turn_taken.at(i, e + 1))
                    for t in range(4):
                        mm = nc.tensor.transpose(ps[:, 6, 128 * t:128 * t + 128], tk[:, e % 2, t], ident[:])
                    mm.then_inc(turn_done.sem, 1)

                def up(i, e):
                    pe.wait_ge(turn_taken.sem, turn_taken.at(i, e + 2))
                    for f in range(F):
                        pe.wait_ge(up_taken.sem, up_taken.at(i, F * (e - 1) + f + 1) if e else up_taken.at(i - 1))
                        nc.tensor.matmul(ps[:, f, :], w1[:, e, 128 * f:128 * f + 128], tT[:, e % 2], start=True,
                                         stop=True).then_inc(up_done.sem, 1)

                def down(i, e):
                    pe.wait_ge(down_taken.sem, down_taken.at(i, e))
                    for f in range(F):
                        pe.wait_ge(up_taken.sem, up_taken.at(i, F * e + f + 1))
                        mm = nc.tensor.matmul(ps[:, 4, :], w2[:, e, f], hid[:, e % 2, f], start=f == 0, stop=f == F - 1)
                    mm.then_inc(down_done.sem, 1)

                def back(i, e):
                    pe.wait_ge(down_taken.sem, down_taken.at(i, e + 1))
                    pe.wait_ge(res_taken.sem, res_taken.at(i, e))
                    for t in range(4):
                        mm = nc.tensor.transpose(ps[:, 5, 128 * t:128 * t + 128], fT[:, 128 * t:128 * t + 128], ident[:])
                    mm.then_inc(back_done.sem, 1)

                def chunk(i, u):
                    gates(i, u)
                    turn(i, 0)
                    for e in range(E):
                        up(i, e)
                        if e >= 1:
                            back(i, e - 1)
                        if e < E - 1:
                            turn(i, e + 1)
                        down(i, e)
                    back(i, E - 1)

                pe.wait_ge(w_loaded.sem, w_loaded.at(0))
                with pe.Fori(0, CHUNKS // 2) as r:
                    for u in range(2):
                        chunk(2 * r + u, u)

            @block.scalar
            def _(act):
                def take_turn(i, k):
                    act.wait_ge(turn_done.sem, turn_done.at(i, k + 1))
                    if k == 0:
                        act.wait_ge(g_done.sem, g_done.at(i - 1))
                        dst = meanT[:]
                    else:
                        e = k - 1
                        act.wait_ge(up_done.sem, up_done.at(i, F * (e - 1)) if e >= 1 else up_done.at(i - 1))
                        dst = tT[:, e % 2]
                    nc.scalar.copy(dst, ps[:, 6, :]).then_inc(turn_taken.sem, 1)

                def relus(i, e):
                    act.wait_ge(down_done.sem, down_done.at(i, e - 1) if e >= 1 else down_done.at(i - 1))
                    for f in range(F):
                        act.wait_ge(up_done.sem, up_done.at(i, F * e + f + 1))
                        nc.scalar.activation(hid[:, e % 2, f], ps[:, f, :], ACT.Relu, bias=b1[:, e, f:f + 1]).then_inc(
                            up_taken.sem, 1)

                def take_down(i, e):
                    act.wait_ge(down_done.sem, down_done.at(i, e + 1))
                    act.wait_ge(back_done.sem, back_done.at(i, e))
                    nc.scalar.activation(fT[:], ps[:, 4, :], ACT.Identity, bias=b2[:, e:e + 1]).then_inc(down_taken.sem, 1)

                def chunk(i):
                    take_turn(i, 0)
                    take_turn(i, 1)
                    for e in range(E):
                        relus(i, e)
                        if e == 0:
                            act.wait_ge(g_step.sem, g_step.at(i, 3))
                            nc.scalar.activation(pr[:], lg[:], ACT.Exp).then_inc(g_exp.sem, 1)
                        if e < E - 1:
                            take_turn(i, e + 2)
                        take_down(i, e)

                act.wait_ge(w_loaded.sem, w_loaded.at(0))
                with act.Fori(0, CHUNKS) as i:
                    chunk(i)

            @block.gpsimd
            def _(pool):
                def scale(i, n):
                    pool.wait_ge(mv_ready.sem, mv_ready.at(i, n + 1))
                    nc.gpsimd.tensor_tensor(rstd[:], mv[:, :, 1], eps[:], ALU.add).then_inc(rstd_ready.sem, 1)
                    pool.wait_ge(rstd_ready.sem, rstd_ready.at(i, 2 * n + 1))
                    nc.gpsimd.tensor_tensor(rstd[:], rstd[:], half_neg[:], ALU.pow).then_inc(rstd_ready.sem, 1)

                def affine(i, e):
                    pool.wait_ge(added.sem, added.at(i, e - 1) if e >= 1 else added.at(i - 1))
                    pool.wait_ge(scaled.sem, scaled.at(i, e + 1))
                    row = lambda w: w[:, e].rearrange("p (a d) -> p a d", a=1).to_broadcast([128, 4, 128])
                    nc.gpsimd.tensor_tensor(zw[:, e % 2], z[:], row(lnw), ALU.mult).then_inc(weighted.sem, 1)
                    pool.wait_ge(weighted.sem, weighted.at(i, e + 1))
                    nc.gpsimd.tensor_tensor(zw[:, e % 2], zw[:, e % 2], row(lnb), ALU.add).then_inc(shifted.sem, 1)

                nc.gpsimd.memset(half_neg[:], -0.5).then_inc(half_set.sem, 1)
                nc.gpsimd.memset(eps[:], LN_EPS).then_inc(half_set.sem, 1)
                pool.wait_ge(half_set.sem, half_set.at(0))
                pool.wait_ge(w_loaded.sem, w_loaded.at(0))
                with pool.Fori(0, CHUNKS) as i:
                    for e in range(E):
                        scale(i, e)
                        affine(i, e)
                    scale(i, E)

            @block.vector
            def _(dve):
                def wide(v):
                    return v.rearrange("p (t a) -> p t a", a=1).to_broadcast([128, 4, E])

                def row(v):
                    return v.rearrange("p (a e) -> p a e", a=1).to_broadcast([128, 4, E])

                def step(i, k, ins):
                    ins.then_inc(g_step.sem, 1)
                    dve.wait_ge(g_step.sem, g_step.at(i, k))

                def pick(i, k, src, onehot):
                    step(i, k + 1, nc.vector.reduce_max(m1[:], src[:], AX.X))
                    step(i, k + 2, nc.vector.tensor_tensor(cand[:], src[:], wide(m1[:]), ALU.is_equal))
                    step(i, k + 3, nc.vector.tensor_tensor(cand[:], cand[:], row(order[:]), ALU.mult))
                    step(i, k + 4, nc.vector.reduce_max(r1[:], cand[:], AX.X))
                    step(i, k + 5, nc.vector.tensor_tensor(onehot[:], cand[:], wide(r1[:]), ALU.is_equal))

                def gates(i):
                    dve.wait_ge(g_done.sem, g_done.at(i))
                    dve.wait_ge(scaled.sem, scaled.at(i - 1))
                    step(i, 1, nc.vector.tensor_tensor(rest[:], ps[:, 7, 0:4 * E].rearrange("p (t e) -> p t e", t=4),
                                                       row(bg[:]), ALU.add))
                    step(i, 2, nc.vector.reduce_max(r1[:], rest[:], AX.X))
                    step(i, 3, nc.vector.tensor_tensor(lg[:], rest[:], wide(r1[:]), ALU.subtract))
                    pick(i, 3, lg, one1)
                    step(i, 9, nc.vector.scalar_tensor_tensor(rest[:], one1[:], -3e38, lg[:], ALU.mult, ALU.add))
                    pick(i, 9, rest, one2)
                    dve.wait_ge(g_exp.sem, g_exp.at(i))
                    step(i, 15, nc.vector.reduce_sum(r1[:], pr[:], AX.X))
                    step(i, 16, nc.vector.reciprocal(r1[:], r1[:]))

                def gates_end(i):
                    nc.vector.tensor_tensor(one1[:], one1[:], one2[:], ALU.add).then_inc(g_end.sem, 1)
                    dve.wait_ge(g_end.sem, g_end.at(i, 1))
                    nc.vector.tensor_tensor(gate[:], pr[:], one1[:], ALU.mult).then_inc(g_end.sem, 1)
                    dve.wait_ge(g_end.sem, g_end.at(i, 2))
                    nc.vector.tensor_tensor(gate[:], gate[:], wide(r1[:]), ALU.mult).then_inc(g_end.sem, 1)
                    dve.wait_ge(g_end.sem, g_end.at(i, 3))

                def statistics(i, n, src):
                    for t in range(4):
                        ins = nc.vector.bn_stats(stats[:, t], src[:, t])
                    ins.then_inc(st_done.sem, 1)
                    dve.wait_ge(st_done.sem, st_done.at(i, n + 1))
                    nc.vector.tensor_copy(seen[:], stats[:, 0, 0:1])
                    for t in range(4):
                        ins = nc.vector.bn_aggr(mv[:, t], stats[:, t])
                    ins.then_inc(mv_ready.sem, 1)
                    dve.wait_ge(rstd_ready.sem, rstd_ready.at(i, 2 * n + 2))

                def norm(i, e):
                    dve.wait_ge(back_done.sem, back_done.at(i, e + 1))
                    dve.wait_ge(weighted.sem, weighted.at(i, e))
                    nc.vector.tensor_tensor(z[:], ps[:, 5, :].rearrange("p (t d) -> p t d", t=4), tk[:, e % 2],
                                            ALU.add).then_inc(res_taken.sem, 1)
                    dve.wait_ge(res_taken.sem, res_taken.at(i, e + 1))
                    statistics(i, e, z)
                    for t in range(4):
                        ins = nc.vector.tensor_scalar(z[:, t], z[:, t], mv[:, t, 0:1], rstd[:, t:t + 1], ALU.subtract,
                                                      ALU.mult)
                    ins.then_inc(scaled.sem, 1)

                def add(i, u, e):
                    dve.wait_ge(shifted.sem, shifted.at(i, e + 1))
                    dve.wait_ge(added.sem, added.at(i, e))
                    src = x[:, u] if e == 0 else acc[:]
                    for t in range(4):
                        ins = nc.vector.scalar_tensor_tensor(acc[:, t], zw[:, e % 2, t], gate[:, t, e:e + 1], src[:, t],
                                                             ALU.mult, ALU.add)
                    ins.then_inc(added.sem, 1)

                def chunk(i, u):
                    gates(i)
                    gates_end(i)
                    for e in range(E):
                        norm(i, e)
                        if e >= 1:
                            add(i, u, e - 1)
                    add(i, u, E - 1)
                    dve.wait_ge(added.sem, added.at(i, E))
                    dve.wait_ge(y_stored.of(u), y_stored.at(i - 2, u))
                    for t in range(4):
                        ins = nc.vector.bn_stats(stats[:, t], acc[:, t])
                    ins.then_inc(st_done.sem, 1)
                    dve.wait_ge(st_done.sem, st_done.at(i, E + 1))
                    nc.vector.tensor_copy(seen[:], stats[:, 0, 0:1])
                    for t in range(4):
                        ins = nc.vector.bn_aggr(mv[:, t], stats[:, t])
                    ins.then_inc(mv_ready.sem, 1)
                    dve.wait_ge(rstd_ready.sem, rstd_ready.at(i, 2 * E + 2))
                    for t in range(4):
                        ins = nc.vector.tensor_scalar(y[:, u, t], acc[:, t], mv[:, t, 0:1], rstd[:, t:t + 1],
                                                      ALU.subtract, ALU.mult)
                    ins.then_inc(scaled.sem, 1)

                dve.wait_ge(w_loaded.sem, w_loaded.at(0))
                with dve.Fori(0, CHUNKS // 2 - 1) as r:
                    for u in range(2):
                        chunk(2 * r + u, u)
                chunk(CHUNKS - 2, 0)
                chunk(CHUNKS - 1, 1)


def more_layout(a, inp):
    f = np.float32
    part = np.arange(128)
    freq = (f(10000.0) ** (-(np.arange(4, dtype=f) * f(2.0)) / f(8))).astype(f)
    a["rope_freq"] = freq[(part % 8) // 2].reshape(128, 1)
    a["rope_sign"] = np.where(part % 2 == 0, f(-1), f(1)).reshape(128, 1)
    up = lambda w: w.transpose(1, 0, 2)
    down = lambda w: w.reshape(-1, 2, 128, D).transpose(2, 0, 1, 3)
    t = "L0_attn_"
    a["mb_sel"] = (part[:, None] % 64 == np.arange(64)[None, :]).astype(f)
    a["mb_norm_w"] = inp[t + "input_norm_w"].reshape(D, 1)
    a["mb_in"] = inp[t + "in_proj_W"].reshape(D, 4, 128)
    a["mb_conv_w"] = inp[t + "conv_W"].reshape(4, 2, 128).transpose(2, 1, 0)
    a["mb_conv_b"], a["mb_dt_b"] = inp[t + "conv_b"].reshape(2, 128).T, inp[t + "dt_b"].reshape(2, 128).T
    a["mb_dt"] = inp[t + "dt_W"].reshape(2, 128, 2, 128).transpose(1, 0, 2, 3)
    twice = [np.tile(inp[t + z].reshape(2, 128, 64), (1, 1, 2)) for z in ("B_W", "C_W")]
    a["mb_bc"] = np.stack(twice, 2).transpose(1, 0, 2, 3)
    a["mb_a_log"] = inp[t + "A_log"]
    a["mb_out"] = inp[t + "out_proj_W"].reshape(2, 128, D).transpose(1, 0, 2)
    a["s0norm_w"] = inp[t + "ffn_norm_w"].reshape(D, 1)
    a["s0wg"], a["s0wu"], a["s0wd"] = up(inp[t + "gate_W"][None]), up(inp[t + "up_W"][None]), down(inp[t + "down_W"][None])
    t = "L0_ffn_"
    a["monorm_w"] = inp[t + "norm2_w"].reshape(D, 1)
    a["mowg"] = up(np.concatenate([inp[t + "sh_gate"][None], inp[t + "e_gate"]]))
    a["mowu"] = up(np.concatenate([inp[t + "sh_up"][None], inp[t + "e_up"]]))
    a["mowd"] = down(np.concatenate([inp[t + "sh_down"][None], inp[t + "e_down"]]))
    a["router"] = inp[t + "router_w"]
    a["order"] = np.arange(8, 0, -1).astype(f)
    t = "L1_attn_"
    a["g_wq"], a["g_wk"], a["g_wv"] = inp[t + "Wq"], inp[t + "Wk"], inp[t + "Wv"]
    a["g_wo"] = inp[t + "Wo"].reshape(8, 128, D).transpose(1, 0, 2)
    inv = f(1) / f(10000.0) ** (np.arange(0, 64, 2, dtype=f) / f(64))
    ang = (part % 64).astype(f)[:, None] * np.concatenate([inv, inv])[None, :]
    a["g_cos"] = np.cos(ang)
    a["g_sin"] = np.sin(ang) * np.where(np.arange(64) < 32, f(-1), f(1))
    t = "L1_ffn_"
    a["average"] = np.where(part[:, None] // 64 == part[None, :] // 64, f(1 / 64), f(0))
    a["ex_w1"] = inp[t + "lin1_w"].transpose(2, 0, 1)
    a["ex_b1"] = inp[t + "lin1_b"].reshape(4, 4, 128).transpose(2, 0, 1)
    a["ex_w2"] = inp[t + "lin2_w"].reshape(4, D, 4, 128).transpose(3, 0, 2, 1)
    a["ex_b2"] = inp[t + "lin2_b"].T
    a["ex_wg"], a["ex_bg"] = inp[t + "gate_w"].T, inp[t + "gate_b"]
    a["ex_order"] = np.arange(4, 0, -1).astype(f)
    a["ex_lnw"], a["ex_lnb"] = inp[t + "ln2_w"].reshape(-1), inp[t + "ln2_b"].reshape(-1)
    slopes = ((2.0 ** -0.5) ** (1 + np.arange(16))).astype(f)
    rel = (np.arange(64)[None, :] - (part % 64)[:, None]).astype(f)
    a["g_alibi"] = (f(8) * (slopes[None, :, None] * rel[:, None, :])).reshape(128, 1024)


def host_layout(inp):
    f = np.float32
    a = {}
    a["x"] = inp["x"].reshape(TILES, 128, D)
    a["ctx"] = inp["ctx_1024"].reshape(TILES, 128, D)
    a["pos"] = inp["pos_BxS2"].reshape(B * S)
    a["mask"] = inp["mask_Bx1xSxS2_ff1"].reshape(TILES, 128, S)
    part = np.arange(128)
    a["ident"] = np.eye(128, dtype=f)
    a["head_mask"] = ((part[:, None] // 8) % 4 == np.arange(4)[None, :]).astype(f)
    a["sel_q"] = (part[None, :] % 64 == np.arange(64)[:, None]).astype(f)
    a["future"] = np.where(np.arange(512)[None, :] % 64 > np.arange(64)[:, None], f(-1e30), f(0))

    def pair_swap(v):
        return v.reshape(v.shape[:-1] + (-1, 2))[..., ::-1].reshape(v.shape)

    col = lambda v: v.reshape(-1, 1)
    for pre, q, k, v, o, t in (("x0", "w_q", "w_k", "w_v", "w_o", "L0_xattn_"), ("f0", "wq", "wk", "wv", "wo", "L0_ffn_"),
                               ("x1", "wq_w", "wk_w", "wv_w", "wo_w", "L1_xattn_")):
        a[pre + "wq"], a[pre + "wk"], a[pre + "wv"] = inp[t + q], inp[t + k], inp[t + v]
        a[pre + "wo"] = inp[t + o]
    for pre, b in (("x0", "L0_xattn_b_%s"), ("x1", "L1_xattn_w%s_b")):
        for z in "qkvo":
            v = inp[b % z]
            a[pre + "b" + z] = col(v) if z in "qk" else v
    a["x0wqs"], a["x0wks"] = pair_swap(inp["L0_xattn_w_q"]), pair_swap(inp["L0_xattn_w_k"])
    a["x0bqs"], a["x0bks"] = col(pair_swap(inp["L0_xattn_b_q"])), col(pair_swap(inp["L0_xattn_b_k"]))
    a["f0norm_w"] = col(inp["L0_ffn_norm1_w"])
    for e in range(4):
        w, b = inp["L1_ffn_in_proj_w"][e], inp["L1_ffn_in_proj_b"][e]
        for n, z in enumerate("qkv"):
            a[f"e{e}w{z}"] = w[n * D:(n + 1) * D].T
            a[f"e{e}b{z}"] = col(b[n * D:(n + 1) * D]) if z != "v" else b[n * D:(n + 1) * D]
        a[f"e{e}wo"] = inp["L1_ffn_out_proj_w"][e].T
        a[f"e{e}bo"] = inp["L1_ffn_out_proj_b"][e]
        a[f"e{e}lnw"], a[f"e{e}lnb"] = inp["L1_ffn_ln1_w"][e], inp["L1_ffn_ln1_b"][e]
    more_layout(a, inp)
    return {k: np.ascontiguousarray(v) for k, v in a.items()}


def stage_weights(dram, prefix, names):
    return {n: dram[prefix + n] for n in names} | {"ident": dram["ident"], "head_mask": dram["head_mask"]}


def build(nc, dram, out):
    with ExitStack() as sems:
        ps = sems.enter_context(nc.psum_tensor("ps", [128, 8, 512], F32))
        h = [nc.dram_tensor(f"hidden{n}", (TILES, 128, D), F32, kind="Internal").ap() for n in range(7)]
        wn = ["wq", "wk", "wv", "wo"]
        bn = ["bq", "bk", "bv", "bo"]
        x = dram["x"]

        def xattn0(src, dst):
            tables = [nc.dram_tensor(f"rope{z}", (8, B * S), F32, kind="Internal").ap() for z in range(2)]
            rope_tables(nc, sems, dram, tables)
            w = stage_weights(dram, "x0", wn + bn + ["wqs", "wks", "bqs", "bks"])
            w |= {"sel_q": dram["sel_q"], "future": dram["future"]}
            attention8(nc, sems, ps, "x0", src, dst, w, ctx=dram["ctx"], qkv_bias=True,
                       rope=tables, causal=True)

        def attn_moe(src, dst):
            w = stage_weights(dram, "f0", wn + ["norm_w"]) | {"norm_eps": 1e-6}
            attention8(nc, sems, ps, "f0", src, dst, w, pre_norm=True, tail="none")

        def xattn1(src, dst):
            attention8(nc, sems, ps, "x1", src, dst, stage_weights(dram, "x1", wn + bn), ctx=dram["ctx"],
                       qkv_bias=True, mask=dram["mask"])

        def expert_attn(e, src, dst):
            attention8(nc, sems, ps, f"e{e}", src, dst, stage_weights(dram, f"e{e}", wn + bn + ["lnw", "lnb"]),
                       qkv_bias=True, tail="affine")

        mamba(nc, sems, ps, dram, x, h[0])
        swiglu(nc, sems, ps, "s0", dram, x, h[0], h[1])
        xattn0(h[1], h[2])
        attn_moe(h[2], h[3])
        swiglu(nc, sems, ps, "mo", dram, h[2], h[3], h[4])
        gqa(nc, sems, ps, dram, h[4], h[5])
        xattn1(h[5], h[6])
        for e in range(4):
            expert_attn(e, h[6], h[e])
        experts(nc, sems, ps, dram, h[6], h[0:4], out)


def kernel(**inputs):
    import concourse.bacc as bacc
    from concourse.bass_utils import run_bass_kernel_spmd

    arrays = host_layout({k: np.asarray(v) for k, v in inputs.items()})
    nc = bacc.Bacc("TRN2", target_bir_lowering=False, num_devices=1)
    dram = {k: nc.dram_tensor("in_" + k, v.shape, mybir.dt.from_np(v.dtype), kind="ExternalInput").ap()
            for k, v in arrays.items()}
    out = nc.dram_tensor("out", (TILES, 128, D), F32, kind="ExternalOutput").ap()
    build(nc, dram, out)
    got = run_bass_kernel_spmd(nc, [{"in_" + k: v for k, v in arrays.items()}], core_ids=[0])
    return got.results[0]["out"].reshape(B, S, D)
```

```python
from contextlib import ExitStack

import numpy as np

import concourse.bass as bass
from concourse import mybir

F32 = mybir.dt.float32
BF16 = mybir.dt.bfloat16
I32 = mybir.dt.int32
ACT = mybir.ActivationFunctionType
ALU = mybir.AluOpType
AX = mybir.AxisListType

B, S, D = 128, 64, 128
TILES = B * S // 128
H8 = 16
SLOTS = 280
LN_EPS = 1e-5


class Signal:

    def __init__(self, sem, per, unit=1):
        self.sem, self.per, self.unit = sem, per, unit

    def at(self, i, k=None):
        v = i * (self.per * self.unit) + ((self.per if k is None else k) * self.unit + 1)
        return max(v, 1) if isinstance(v, int) else v


class SlotSignal:

    def __init__(self, sems, per):
        self.sems, self.per = sems, per

    def of(self, u):
        return self.sems[u]

    def at(self, i, u):
        v = (i - u) * (16 // len(self.sems) * self.per) + (16 * self.per + 1)
        return max(v, 1) if isinstance(v, int) else v


class Stage:

    def __init__(self, nc, mem, name):
        self.nc, self.mem, self.name, self.handles = nc, mem, name, []
        mem.callback(self.end)

    def begin(self):
        self.nc.all_engine_barrier()

    def end(self):
        self.nc.clear_and_free_semaphores(self.handles)
        self.nc.all_engine_barrier()

    def sb(self, name, shape, dt=F32):
        return self.mem.enter_context(self.nc.sbuf_tensor(f"{self.name}_{name}", shape, dt))

    def semaphore(self, name):
        sem = self.nc.alloc_semaphore(name=f"{self.name}_{name}")
        self.handles.append(sem)
        self.nc.gpsimd.sem_inc(sem, 1)
        return sem

    def counter(self, name, per=1):
        return Signal(self.semaphore(name), per)

    def dma_signal(self, name, per=1):
        return Signal(self.semaphore(name), per, 16)

    def slot_signal(self, name, per=1, slots=2):
        return SlotSignal([self.semaphore(f"{name}{u}") for u in range(slots)], per)


def bcast_rows(row, n=128):
    return row.rearrange("(a n) -> a n", a=1).to_broadcast([n, row.shape[0]])


def tiles_of(dram, i, n):
    return dram[bass.ds(i * n, n)].rearrange("t p d -> p t d")


def every_head(v):
    return bass.AP(v.tensor, v.offset, [[0, H8]] + list(v.ap))


def diagonal(v, h2):
    (row, rows), (block, blocks), _ = v.ap
    return bass.AP(v.tensor, v.offset + 8 * h2, [[row, rows], [block, blocks], [48, 2], [1, 8]])


def attention8(nc, ps, name, x_in, x_out, w, ctx=None, pre_norm=False, qkv_bias=False, rope=None,
               causal=False, mask=None, tail="ln", plan=None):
    QUADS = SLOTS // 4 if plan else TILES // 2
    SCALE = 8.0 ** -0.5
    has_ctx = ctx is not None
    with ExitStack() as mem:
        st = Stage(nc, mem, name)
        ident = st.sb("ident", [128, 128])
        WS = 2 if plan else 1
        wqkv = st.sb("wqkv", [128, WS, 386])
        wo = st.sb("wo", [128, WS, 128])
        head_mask = st.sb("head_mask", [128, 4])
        x = st.sb("x", [128, 2, 2, 128])
        xr = st.sb("xr", [128, 2, 2, 128])
        qT = st.sb("qT", [128, 2, 256])
        kT = st.sb("kT", [128, 256])
        km = st.sb("km", [128, 2, 4, 4, 64])
        vbd = st.sb("vbd", [128, 2, 4, 4, 2, 32])
        p = st.sb("p", [128, 2, 2048])
        top = st.sb("top", [128, 32])
        total = st.sb("total", [128, 32])
        rec = st.sb("rec", [128, 32])
        pT = st.sb("pT", [128, 2, 1024])
        oT = st.sb("oT", [128, 256])
        res = st.sb("res", [128, 2, 128])
        stats = st.sb("stats", [128, 2, 6])
        mv = st.sb("mv", [128, 2, 2])
        rstd = st.sb("rstd", [128, 2])
        half_neg = st.sb("half_neg", [128, 2])
        eps = st.sb("eps", [128, 2])
        seen = st.sb("seen", [128, 2])
        y = st.sb("y", [128, 2, 2, 128])
        loads = [(ident[:], w["ident"]), (head_mask[:], w["head_mask"])]
        if not plan:
            loads += [(wqkv[:, 0, 0:128], w["wq"]), (wqkv[:, 0, 128:256], w["wk"]), (wqkv[:, 0, 256:384], w["wv"]),
                      (wo[:, 0], w["wo"])]
        if has_ctx:
            c = st.sb("c", [128, 2, 2, 128])
            xT = st.sb("xT", [128, 256])
        kvT = st.sb("kvT", [128, 4, 2, 64])
        kv_once = kvT[:, :, 0, :]
        q_src = xT[:] if has_ctx else kv_once
        if pre_norm:
            xn = st.sb("xn", [128, 2, 128])
            nstats = st.sb("nstats", [128, 2, 6])
            nmv = st.sb("nmv", [128, 2, 2])
            nsq = st.sb("nsq", [128, 2])
            nrstd = st.sb("nrstd", [128, 2])
            norm_eps = st.sb("norm_eps", [128, 2])
            norm_w = st.sb("norm_w", [128, 1])
            loads.append((norm_w[:], w["norm_w"]))
        if qkv_bias:
            bv = st.sb("bv", [128, WS, 4, 128])
            rows = st.sb("rows", [128, WS, 3, 128])
            if not plan:
                loads += [(wqkv[:, 0, 384:385], w["bq"]), (wqkv[:, 0, 385:386], w["bk"]),
                          (rows[:, 0, 0], bcast_rows(w["bo"]))]
                loads += [(bv[:, 0, b, :], bcast_rows(w["bv"])) for b in range(4)]
        if rope:
            wqs = st.sb("wqs", [128, 128])
            wks = st.sb("wks", [128, 128])
            bqs = st.sb("bqs", [128, 1])
            bks = st.sb("bks", [128, 1])
            cs = st.sb("cs", [128, 2, 2, 256])
            qs = st.sb("qs", [128, 2, 256])
            qc = st.sb("qc", [128, 2, 256])
            loads += [(wqs[:], w["wqs"]), (wks[:], w["wks"]), (bqs[:], w["bqs"]), (bks[:], w["bks"])]
        if causal:
            sel_q = st.sb("sel_q", [64, 128], BF16)
            future = st.sb("future", [64, 512], BF16)
            sel_q32 = st.sb("sel_q32", [64, 128])
            future32 = st.sb("future32", [64, 512])
            loads += [(sel_q32[:], w["sel_q"]), (future32[:], w["future"])]
        if mask is not None:
            mk = st.sb("mk", [128, 2, 2, 64])
            dead = st.sb("dead", [128, 2048])
        if plan:
            batches = st.sb("batches", [1, SLOTS], I32)
            experts = st.sb("experts", [1, QUADS], I32)

        w_loaded = st.dma_signal("w_loaded", len(loads))
        table_loaded = st.dma_signal("table_loaded", 2)
        passed = st.counter("passed")
        wl_loaded = st.slot_signal("wl_loaded", 2)
        wt_loaded = st.slot_signal("wt_loaded", 2)
        x_loaded = st.slot_signal("x_loaded", 4 if plan else 1)
        c_loaded = st.slot_signal("c_loaded", 1)
        cs_loaded = st.slot_signal("cs_loaded", 2)
        mk_loaded = st.slot_signal("mk_loaded", 1)
        xr_loaded = st.slot_signal("xr_loaded", 4 if plan else 1)
        y_stored = st.slot_signal("y_stored", 1)
        consts_set = st.counter("consts_set", 1 + 2 * causal)
        half_set = st.counter("half_set", 2 + pre_norm)
        normed = st.counter("normed", 6)
        nrstd_ready = st.counter("nrstd_ready", 2)
        xT_done = st.counter("xT_done")
        xT_ready = st.counter("xT_ready", 2 if has_ctx else 1)
        qk_done = st.counter("qk_done")
        qs_done = st.counter("qs_done")
        qk_taken = st.counter("qk_taken", 2)
        qs_taken = st.counter("qs_taken", 2)
        rot_ready = st.counter("rot_ready", 2)
        km_ready = st.counter("km_ready")
        v_done = st.counter("v_done")
        v_ready = st.counter("v_ready", 2)
        s_done = st.counter("s_done")
        masked = st.counter("masked", 2)
        dead_ready = st.counter("dead_ready", 1)
        s_masked = st.counter("s_masked", 1)
        top_ready = st.counter("top_ready")
        shifted = st.counter("shifted")
        exp_done = st.counter("exp_done")
        summed = st.counter("summed")
        rec_ready = st.counter("rec_ready")
        p_ready = st.counter("p_ready")
        pT_done = st.counter("pT_done", 2)
        pT_ready = st.counter("pT_ready", 2)
        o_done = st.counter("o_done", 2)
        oT_ready = st.counter("oT_ready")
        y_done = st.counter("y_done")
        biased = st.counter("biased")
        TAIL = {"none": 0, "ln": 6, "affine": 8}[tail]
        res_taken = st.counter("res_taken")
        tailed = st.counter("tailed", max(TAIL, 1))
        rstd_ready = st.counter("rstd_ready", 2)

        S_ps = ps[:, 0:4, :]
        P_g = p[:].rearrange("p u (g t h k) -> p u g t h k", g=4, t=2, h=4)
        Y_ps = ps[:, 5, 256:512]
        lead_ps = ps[:, 4, :]

        def proj(u, z):
            return wqkv[:, u if plan else 0, 128 * z:128 * z + 128]

        def proj_bias(u, z):
            return wqkv[:, u if plan else 0, 384 + z:385 + z]

        def row_pair(u, n):
            return rows[:, u if plan else 0, n].rearrange("p (a d) -> p a d", a=1).to_broadcast([128, 2, 128])

        st.begin()
        with nc.Block() as block:

            @block.sync
            def _(sp):
                for dst, src in loads:
                    sp.dma_start(dst, src).then_inc(w_loaded.sem, 16)

                def look_up(table, n, top):
                    return sp.value_load(table[0:1, bass.ds(n, 1)], min_val=0, max_val=top)

                def fetch(i, u, dst, signal):
                    sp.sem_inc(passed.sem, 1)
                    for b in range(4):
                        n = look_up(batches, 4 * i + b, B - 1)
                        sp.dma_start(dst[64 * (b % 2):64 * (b % 2) + 64, u, b // 2],
                                     x_in[bass.ds(n, 1)].rearrange("a p d -> p (a d)")).then_inc(signal.of(u), 16)

                def lead(i, u):
                    sp.wait_ge(xT_done.sem, xT_done.at(i - 2))
                    if plan:
                        fetch(i, u, x, x_loaded)
                        sp.wait_ge(v_done.sem, v_done.at(i - 2))
                        sp.wait_ge(v_ready.sem, v_ready.at(i - 2))
                        sp.sem_inc(passed.sem, 1)
                        e = look_up(experts, i, 3)
                        sp.dma_start(wqkv[:, u], w["wqkv"][bass.ds(e, 1)].rearrange("a p n -> p (a n)")).then_inc(
                            wl_loaded.of(u), 16)
                        sp.dma_start(bv[:, u], w["bv"][bass.ds(e, 1)].rearrange("a (b n) -> a b n", b=1).to_broadcast(
                            [128, 4, 128])).then_inc(wl_loaded.of(u), 16)
                    else:
                        sp.dma_start(x[:, u], tiles_of(x_in, i, 2)).then_inc(x_loaded.of(u), 16)
                    if has_ctx:
                        sp.dma_start(c[:, u], tiles_of(ctx, i, 2)).then_inc(c_loaded.of(u), 16)
                    if rope:
                        sp.wait_ge(rot_ready.sem, rot_ready.at(i - 2))
                        for z in range(2):
                            sp.dma_start(cs[:, u, z], every_head(rope[z][:, bass.ds(256 * i, 256)])).then_inc(
                                cs_loaded.of(u), 16)
                    if mask is not None:
                        sp.wait_ge(masked.sem, masked.at(i - 2))
                        sp.dma_start(mk[:, u], mask[bass.ds(2 * i, 2)].rearrange("t p k -> p t k")).then_inc(
                            mk_loaded.of(u), 16)

                def trail(i, u):
                    if qkv_bias:
                        sp.wait_ge(biased.sem, biased.at(i - 2))
                    sp.wait_ge(res_taken.sem, res_taken.at(i - 2))
                    if plan:
                        fetch(i, u, xr, xr_loaded)
                        sp.wait_ge(tailed.sem, tailed.at(i - 2))
                        sp.sem_inc(passed.sem, 1)
                        e = look_up(experts, i, 3)
                        sp.dma_start(wo[:, u], w["wo"][bass.ds(e, 1)].rearrange("a p n -> p (a n)")).then_inc(
                            wt_loaded.of(u), 16)
                        sp.dma_start(rows[:, u].rearrange("p a d -> p (a d)"), w["rows"][bass.ds(e, 1)].to_broadcast(
                            [128, 384])).then_inc(wt_loaded.of(u), 16)
                    else:
                        sp.dma_start(xr[:, u], tiles_of(x_in, i, 2)).then_inc(xr_loaded.of(u), 16)

                def store(i, u):
                    if tail == "none":
                        sp.wait_ge(res_taken.sem, res_taken.at(i))
                    else:
                        sp.wait_ge(tailed.sem, tailed.at(i))
                    sp.dma_start(tiles_of(x_out, i, 2), y[:, u]).then_inc(y_stored.of(u), 16)

                if plan:
                    sp.dma_start(batches[:], plan["batch"]).then_inc(table_loaded.sem, 16)
                    sp.dma_start(experts[:], plan["expert"]).then_inc(table_loaded.sem, 16)
                    sp.wait_ge(table_loaded.sem, table_loaded.at(0))
                lead(0, 0)
                lead(1, 1)
                trail(0, 0)
                lead(2, 0)
                trail(1, 1)
                lead(3, 1)
                trail(2, 0)
                store(0, 0)
                with sp.Fori(1, (QUADS - 2) // 2) as r:
                    for h in range(2):
                        i, u = 2 * r + (1 + h), (1 + h) % 2
                        lead(i + 1, 1 - u)
                        trail(i, u)
                        store(i - 2, u)
                trail(QUADS - 1, 1)
                for q in (QUADS - 3, QUADS - 2, QUADS - 1):
                    store(q, q % 2)
                for u in range(2):
                    sp.wait_ge(y_stored.of(u), y_stored.at(QUADS - 2 + u, u))

            @block.tensor
            def _(pe):
                def turn(i, u):
                    pe.wait_ge(v_ready.sem, v_ready.at(i - 1))
                    if pre_norm:
                        pe.wait_ge(normed.sem, normed.at(i))
                        src = xn[:]
                    else:
                        pe.wait_ge(x_loaded.of(u), x_loaded.at(i, u))
                        src = x[:, u]
                    if has_ctx:
                        pe.wait_ge(c_loaded.of(u), c_loaded.at(i, u))
                    for t in range(2):
                        mm = nc.tensor.transpose(lead_ps[:, 128 * t:128 * t + 128], src[:, t, :], ident[:])
                    if has_ctx:
                        for t in range(2):
                            mm = nc.tensor.transpose(lead_ps[:, 256 + 128 * t:384 + 128 * t], c[:, u, t, :], ident[:])
                    mm.then_inc(xT_done.sem, 1)

                def project_qk(i, u):
                    pe.wait_ge(xT_ready.sem, xT_ready.at(i))
                    if plan:
                        pe.wait_ge(wl_loaded.of(u), wl_loaded.at(i, u))
                    nc.tensor.matmul(lead_ps[:, 0:256], proj(u, 0), q_src, start=True, stop=True)
                    nc.tensor.matmul(lead_ps[:, 256:512], proj(u, 1), kv_once, start=True, stop=True).then_inc(
                        qk_done.sem, 1)
                    if rope:
                        pe.wait_ge(qk_taken.sem, qk_taken.at(i))
                        nc.tensor.matmul(lead_ps[:, 0:256], wqs[:], q_src, start=True, stop=True)
                        nc.tensor.matmul(lead_ps[:, 256:512], wks[:], kv_once, start=True, stop=True).then_inc(
                            qs_done.sem, 1)

                def project_v(i, u):
                    if rope:
                        pe.wait_ge(qs_taken.sem, qs_taken.at(i))
                    else:
                        pe.wait_ge(qk_taken.sem, qk_taken.at(i))
                    for b in range(4):
                        mm = nc.tensor.matmul(lead_ps[:, 128 * b:128 * b + 128],
                                              kvT[:, b].rearrange("p a k -> p (a k)"), proj(u, 2), start=True, stop=True)
                    mm.then_inc(v_done.sem, 1)

                def scores(i, u):
                    if mask is not None:
                        pe.wait_ge(masked.sem, masked.at(i - 1))
                    else:
                        pe.wait_ge(shifted.sem, shifted.at(i - 1))
                    pe.wait_ge(km_ready.sem, km_ready.at(i))
                    if rope:
                        pe.wait_ge(rot_ready.sem, rot_ready.at(i))
                    else:
                        pe.wait_ge(qk_taken.sem, qk_taken.at(i))
                    if causal:
                        for g in range(4):
                            nc.tensor.matmul(S_ps[:, g, :], sel_q[:], future[:], start=True, stop=False,
                                             skip_group_check=True)
                    for b in range(4):
                        t, b2 = b // 2, b % 2
                        for g in range(4):
                            rows = slice(32 * g, 32 * g + 32)
                            mm = nc.tensor.matmul(
                                S_ps[64 * b2:64 * b2 + 64, g, 256 * t:256 * t + 256], qT[rows, u, 64 * b:64 * b + 64],
                                km[rows, u, b].rearrange("p h k -> p (h k)"), start=not causal, stop=True,
                                skip_group_check=causal)
                    mm.then_inc(s_done.sem, 1)

                def turn_p(i, u, t):
                    pe.wait_ge(p_ready.sem, p_ready.at(i))
                    pe.wait_ge(pT_ready.sem, pT_ready.at(i, t))
                    for g in range(4):
                        for jj in range(2):
                            c0 = 128 * (2 * g + jj)
                            mm = nc.tensor.transpose(
                                ps[:, 6 + c0 // 512, c0 % 512:c0 % 512 + 128],
                                P_g[:, u, g, t, 2 * jj:2 * jj + 2, :].rearrange("p h k -> p (h k)"), ident[:])
                    mm.then_inc(pT_done.sem, 1)

                def values(i, u, t):
                    pe.wait_ge(pT_ready.sem, pT_ready.at(i, t + 1))
                    pe.wait_ge(v_ready.sem, v_ready.at(i))
                    pe.wait_ge(res_taken.sem, res_taken.at(i - 1))
                    for b2 in range(2):
                        tok = 128 * t + 64 * b2
                        for g in range(4):
                            for jj in range(2):
                                c0 = 128 * (2 * g + jj) + 64 * b2
                                mm = nc.tensor.matmul(ps[32 * g:32 * g + 32, 5, tok:tok + 64],
                                                      vbd[:, u, 2 * t + b2, g, jj, :], pT[:, t, c0:c0 + 64],
                                                      start=jj == 0, stop=jj == 1)
                    mm.then_inc(o_done.sem, 1)

                def project_o(i, u):
                    pe.wait_ge(oT_ready.sem, oT_ready.at(i))
                    if plan:
                        pe.wait_ge(wt_loaded.of(u), wt_loaded.at(i, u))
                    for t in range(2):
                        mm = nc.tensor.matmul(Y_ps[:, 128 * t:128 * t + 128], oT[:, 128 * t:128 * t + 128], wo[:, u if plan else 0],
                                              start=True, stop=True)
                    mm.then_inc(y_done.sem, 1)

                def quad(i, u, lead, trail):
                    scores(i, u)
                    if trail:
                        turn_p(i - 1, 1 - u, 0)
                    if lead:
                        turn(i + 1, 1 - u)
                    if trail:
                        values(i - 1, 1 - u, 0)
                        turn_p(i - 1, 1 - u, 1)
                    if lead:
                        project_qk(i + 1, 1 - u)
                    if trail:
                        values(i - 1, 1 - u, 1)
                    if lead:
                        project_v(i + 1, 1 - u)
                    if trail:
                        project_o(i - 1, 1 - u)

                pe.wait_ge(w_loaded.sem, w_loaded.at(0))
                pe.wait_ge(consts_set.sem, consts_set.at(0))
                turn(0, 0)
                project_qk(0, 0)
                project_v(0, 0)
                quad(0, 0, True, False)
                with pe.Fori(0, (QUADS - 2) // 2) as r:
                    for h in range(2):
                        quad(2 * r + (1 + h), (1 + h) % 2, True, True)
                quad(QUADS - 1, 1, False, True)
                for t in range(2):
                    turn_p(QUADS - 1, 1, t)
                    values(QUADS - 1, 1, t)
                project_o(QUADS - 1, 1)

            @block.scalar
            def _(act):
                def take_x(i):
                    act.wait_ge(xT_done.sem, xT_done.at(i))
                    act.wait_ge(v_done.sem, v_done.at(i - 1))
                    if has_ctx:
                        nc.scalar.copy(xT[:], lead_ps[:, 0:256]).then_inc(xT_ready.sem, 1)
                    kv = lead_ps[:, 256:512] if has_ctx else lead_ps[:, 0:256]
                    nc.scalar.activation(kvT[:], kv.rearrange("p (b a k) -> p b a k", b=4, a=1).to_broadcast([128, 4, 2, 64]),
                                         ACT.Identity, scale=norm_w[:, 0:1] if pre_norm else 1.0).then_inc(xT_ready.sem, 1)

                def take_qk(i, u):
                    if rope:
                        return
                    act.wait_ge(qk_done.sem, qk_done.at(i))
                    act.wait_ge(km_ready.sem, km_ready.at(i - 1))
                    act.wait_ge(s_done.sem, s_done.at(i - 2))
                    if qkv_bias:
                        nc.scalar.activation(kT[:], lead_ps[:, 256:512], ACT.Identity, bias=proj_bias(u, 1)).then_inc(
                            qk_taken.sem, 1)
                        nc.scalar.activation(qT[:, u], lead_ps[:, 0:256], ACT.Identity, bias=proj_bias(u, 0)).then_inc(
                            qk_taken.sem, 1)
                    else:
                        nc.scalar.copy(kT[:], lead_ps[:, 256:512]).then_inc(qk_taken.sem, 1)
                        nc.scalar.copy(qT[:, u], lead_ps[:, 0:256]).then_inc(qk_taken.sem, 1)

                def exponentials(i, u):
                    act.wait_ge(shifted.sem, shifted.at(i))
                    nc.scalar.activation(p[:, u], p[:, u], ACT.Exp, scale=SCALE).then_inc(exp_done.sem, 1)

                def take_p(i, t):
                    act.wait_ge(pT_done.sem, pT_done.at(i, t + 1))
                    act.wait_ge(o_done.sem, o_done.at(i - 1))
                    nc.scalar.copy(pT[:, t], ps[:, 6:8, :].rearrange("p a n -> p (a n)")).then_inc(pT_ready.sem, 1)

                def take_o(i):
                    act.wait_ge(o_done.sem, o_done.at(i))
                    act.wait_ge(y_done.sem, y_done.at(i - 1))
                    nc.scalar.copy(oT[:], ps[:, 5, 0:256]).then_inc(oT_ready.sem, 1)

                def quad(i, u, lead, trail):
                    if trail:
                        take_p(i - 1, 0)
                    if lead:
                        take_x(i + 1)
                    if mask is None:
                        exponentials(i, u)
                    if trail:
                        take_p(i - 1, 1)
                    if lead:
                        take_qk(i + 1, 1 - u)
                    if trail:
                        take_o(i - 1)
                    if mask is not None:
                        exponentials(i, u)

                act.wait_ge(w_loaded.sem, w_loaded.at(0))
                take_x(0)
                take_qk(0, 0)
                quad(0, 0, True, False)
                with act.Fori(0, (QUADS - 2) // 2) as r:
                    for h in range(2):
                        quad(2 * r + (1 + h), (1 + h) % 2, True, True)
                quad(QUADS - 1, 1, False, True)
                take_p(QUADS - 1, 0)
                take_p(QUADS - 1, 1)
                take_o(QUADS - 1)

            @block.gpsimd
            def _(pool):
                def norm_scale(i):
                    pool.wait_ge(normed.sem, normed.at(i, 4))
                    nc.gpsimd.tensor_tensor(nrstd[:], nsq[:], norm_eps[:], ALU.add).then_inc(nrstd_ready.sem, 1)
                    pool.wait_ge(nrstd_ready.sem, nrstd_ready.at(i, 1))
                    nc.gpsimd.tensor_tensor(nrstd[:], nrstd[:], half_neg[:], ALU.pow).then_inc(nrstd_ready.sem, 1)

                def mask_heads(i, u):
                    pool.wait_ge(s_done.sem, s_done.at(i - 2))
                    if rope:
                        pool.wait_ge(rot_ready.sem, rot_ready.at(i, 1))
                    else:
                        pool.wait_ge(qk_taken.sem, qk_taken.at(i, 1))
                    nc.gpsimd.tensor_tensor(
                        km[:, u], kT[:].rearrange("p (b a k) -> p b a k", b=4, a=1).to_broadcast([128, 4, 4, 64]),
                        head_mask[:].rearrange("p (a h c) -> p a h c", a=1, c=1).to_broadcast([128, 4, 4, 64]),
                        ALU.mult).then_inc(km_ready.sem, 1)

                def normalise(i, u):
                    pool.wait_ge(rec_ready.sem, rec_ready.at(i))
                    v = p[:, u].rearrange("p (c k) -> p c k", k=64)
                    nc.gpsimd.tensor_tensor(v, v, rec[:].rearrange("p (c a) -> p c a", a=1).to_broadcast([128, 32, 64]),
                                            ALU.mult).then_inc(p_ready.sem, 1)

                def add_bias(i, u):
                    pool.wait_ge(xr_loaded.of(u), xr_loaded.at(i, u))
                    if plan:
                        pool.wait_ge(wt_loaded.of(u), wt_loaded.at(i, u))
                    nc.gpsimd.tensor_tensor(xr[:, u], xr[:, u], row_pair(u, 0), ALU.add).then_inc(biased.sem, 1)

                def tail_scale(i):
                    pool.wait_ge(tailed.sem, tailed.at(i, 4))
                    nc.gpsimd.tensor_tensor(rstd[:], mv[:, :, 1], eps[:], ALU.add).then_inc(rstd_ready.sem, 1)
                    pool.wait_ge(rstd_ready.sem, rstd_ready.at(i, 1))
                    nc.gpsimd.tensor_tensor(rstd[:], rstd[:], half_neg[:], ALU.pow).then_inc(rstd_ready.sem, 1)

                def lead_steps(i, u):
                    mask_heads(i, u)

                def quad(i, u, lead, trail, end=True, ahead=True):
                    if end and tail != "none":
                        tail_scale(i - 2)
                    if ahead and pre_norm:
                        norm_scale(i + 2)
                    if trail and qkv_bias:
                        add_bias(i - 1, 1 - u)
                    if lead:
                        lead_steps(i + 1, 1 - u)
                    normalise(i, u)

                nc.gpsimd.memset(half_neg[:], -0.5).then_inc(half_set.sem, 1)
                nc.gpsimd.memset(eps[:], LN_EPS).then_inc(half_set.sem, 1)
                if pre_norm:
                    nc.gpsimd.memset(norm_eps[:], w["norm_eps"]).then_inc(half_set.sem, 1)
                pool.wait_ge(half_set.sem, half_set.at(0))
                pool.wait_ge(w_loaded.sem, w_loaded.at(0))
                if pre_norm:
                    norm_scale(0)
                lead_steps(0, 0)
                if pre_norm:
                    norm_scale(1)
                quad(0, 0, True, False, False)
                quad(1, 1, True, True, False)
                quad(2, 0, True, True)
                with pool.Fori(1, (QUADS - 4) // 2) as r:
                    for h in range(2):
                        quad(2 * r + (1 + h), (1 + h) % 2, True, True)
                quad(QUADS - 3, 1, True, True)
                quad(QUADS - 2, 0, True, True, True, False)
                quad(QUADS - 1, 1, False, True, True, False)
                if tail != "none":
                    tail_scale(QUADS - 2)
                if qkv_bias:
                    add_bias(QUADS - 1, 1)
                if tail != "none":
                    tail_scale(QUADS - 1)

            @block.vector
            def _(dve):
                def set_constants():
                    nc.vector.memset(vbd[:], 0.0).then_inc(consts_set.sem, 1)
                    if causal:
                        dve.wait_ge(w_loaded.sem, w_loaded.at(0))
                        nc.vector.tensor_copy(sel_q[:], sel_q32[:]).then_inc(consts_set.sem, 1)
                        nc.vector.tensor_copy(future[:], future32[:]).then_inc(consts_set.sem, 1)

                def pre(i, u):
                    dve.wait_ge(x_loaded.of(u), x_loaded.at(i, u))
                    for t in range(2):
                        ins = nc.vector.bn_stats(nstats[:, t], x[:, u, t])
                    ins.then_inc(normed.sem, 1)
                    dve.wait_ge(normed.sem, normed.at(i, 1))
                    nc.vector.tensor_copy(seen[:, 1:2], nstats[:, 0, 0:1])
                    for t in range(2):
                        ins = nc.vector.bn_aggr(nmv[:, t], nstats[:, t])
                    ins.then_inc(normed.sem, 1)
                    dve.wait_ge(normed.sem, normed.at(i, 2))
                    nc.vector.tensor_tensor(nsq[:], nmv[:, :, 0], nmv[:, :, 0], ALU.mult).then_inc(normed.sem, 1)
                    dve.wait_ge(normed.sem, normed.at(i, 3))
                    nc.vector.tensor_tensor(nsq[:], nsq[:], nmv[:, :, 1], ALU.add).then_inc(normed.sem, 1)
                    dve.wait_ge(nrstd_ready.sem, nrstd_ready.at(i))
                    dve.wait_ge(xT_done.sem, xT_done.at(i - 1))
                    for t in range(2):
                        nc.vector.tensor_scalar(xn[:, t], x[:, u, t], nrstd[:, t:t + 1], None, ALU.mult).then_inc(
                            normed.sem, 1)

                def times_cos(i, u):
                    dve.wait_ge(qk_done.sem, qk_done.at(i))
                    dve.wait_ge(rot_ready.sem, rot_ready.at(i - 1))
                    dve.wait_ge(cs_loaded.of(u), cs_loaded.at(i, u))
                    for z in range(2):
                        nc.vector.scalar_tensor_tensor(qc[:, z], lead_ps[:, 256 * z:256 * z + 256], proj_bias(u, z), cs[:, u, 0],
                                                       ALU.add, ALU.mult).then_inc(qk_taken.sem, 1)

                def rotate(i, u):
                    dve.wait_ge(qs_done.sem, qs_done.at(i))
                    for z, b in enumerate((bqs, bks)):
                        nc.vector.scalar_tensor_tensor(qs[:, z], lead_ps[:, 256 * z:256 * z + 256], b[:, 0:1], cs[:, u, 1],
                                                       ALU.add, ALU.mult).then_inc(qs_taken.sem, 1)
                    dve.wait_ge(qs_taken.sem, qs_taken.at(i))
                    dve.wait_ge(km_ready.sem, km_ready.at(i - 1))
                    nc.vector.tensor_tensor(kT[:], qc[:, 1], qs[:, 1], ALU.add).then_inc(rot_ready.sem, 1)
                    dve.wait_ge(s_done.sem, s_done.at(i - 2))
                    nc.vector.tensor_tensor(qT[:, u], qc[:, 0], qs[:, 0], ALU.add).then_inc(rot_ready.sem, 1)

                def lay_values(i, u):
                    dve.wait_ge(v_done.sem, v_done.at(i))
                    dve.wait_ge(o_done.sem, o_done.at(i - 2))
                    for h2 in range(2):
                        part = slice(64 * h2, 64 * h2 + 64)
                        dst = vbd[part, u].rearrange("p b g j e -> p (b g) (j e)")
                        dst = diagonal(dst, h2)
                        src = ps[part, 4, :].rearrange("p (c j h e) -> p c j h e", j=2, h=2, e=8)[:, :, :, h2]
                        if qkv_bias:
                            bias = bv[part, u if plan else 0].rearrange("p b (g j h e) -> p (b g) j h e", j=2, h=2, e=8)[:, :, :, h2]
                            nc.vector.tensor_tensor(dst, src, bias, ALU.add).then_inc(v_ready.sem, 1)
                        else:
                            nc.vector.tensor_copy(dst, src).then_inc(v_ready.sem, 1)

                def softmax_shift(i, u):
                    dve.wait_ge(s_done.sem, s_done.at(i))
                    dve.wait_ge(pT_done.sem, pT_done.at(i - 2))
                    src = S_ps.rearrange("p g (c k) -> p (g c) k", k=64)
                    dst = p[:, u].rearrange("p (c k) -> p c k", k=64)
                    if mask is not None:
                        dve.wait_ge(mk_loaded.of(u), mk_loaded.at(i, u))
                        for t in range(2):
                            m = mk[:, u, t].rearrange("p (a c k) -> p a c k", a=1, c=1).to_broadcast([128, 4, 4, 64])
                            nc.vector.tensor_tensor(P_g[:, u, :, t], S_ps.rearrange("p g (t h k) -> p g t h k", t=2, h=4)[
                                :, :, t], m, ALU.mult).then_inc(masked.sem, 1)
                        dve.wait_ge(masked.sem, masked.at(i))
                        nc.vector.tensor_scalar(dead[:], p[:, u], 0.0, -1e9 / SCALE, ALU.is_equal, ALU.mult).then_inc(
                            dead_ready.sem, 1)
                        dve.wait_ge(dead_ready.sem, dead_ready.at(i))
                        nc.vector.tensor_tensor(p[:, u], p[:, u], dead[:], ALU.add).then_inc(s_masked.sem, 1)
                        dve.wait_ge(s_masked.sem, s_masked.at(i))
                        src = dst
                    nc.vector.reduce_max(top[:], src, AX.X).then_inc(top_ready.sem, 1)
                    dve.wait_ge(top_ready.sem, top_ready.at(i))
                    nc.vector.tensor_tensor(dst, src, top[:].rearrange("p (c a) -> p c a", a=1).to_broadcast([128, 32, 64]),
                                            ALU.subtract).then_inc(shifted.sem, 1)

                def sums(i, u):
                    dve.wait_ge(exp_done.sem, exp_done.at(i))
                    nc.vector.reduce_sum(total[:], p[:, u].rearrange("p (c k) -> p c k", k=64), AX.X).then_inc(
                        summed.sem, 1)
                    dve.wait_ge(p_ready.sem, p_ready.at(i - 1))
                    dve.wait_ge(summed.sem, summed.at(i))
                    nc.vector.reciprocal(rec[:], total[:]).then_inc(rec_ready.sem, 1)

                def finish(i, u):
                    dve.wait_ge(y_done.sem, y_done.at(i))
                    if qkv_bias:
                        dve.wait_ge(biased.sem, biased.at(i))
                    else:
                        dve.wait_ge(xr_loaded.of(u), xr_loaded.at(i, u))
                    if tail != "none":
                        dve.wait_ge(tailed.sem, tailed.at(i - 1))
                    proj = Y_ps.rearrange("p (t d) -> p t d", t=2)
                    if tail == "none":
                        dve.wait_ge(y_stored.of(u), y_stored.at(i - 2, u))
                        nc.vector.tensor_tensor(y[:, u], proj, xr[:, u], ALU.add).then_inc(res_taken.sem, 1)
                        return
                    nc.vector.tensor_tensor(res[:], proj, xr[:, u], ALU.add).then_inc(res_taken.sem, 1)
                    dve.wait_ge(res_taken.sem, res_taken.at(i))
                    for t in range(2):
                        nc.vector.bn_stats(stats[:, t], res[:, t]).then_inc(tailed.sem, 1)
                    dve.wait_ge(tailed.sem, tailed.at(i, 2))
                    nc.vector.tensor_copy(seen[:, 0:1], stats[:, 0, 0:1])
                    for t in range(2):
                        nc.vector.bn_aggr(mv[:, t], stats[:, t]).then_inc(tailed.sem, 1)

                def scale(i, u):
                    dve.wait_ge(rstd_ready.sem, rstd_ready.at(i))
                    dve.wait_ge(y_stored.of(u), y_stored.at(i - 2, u))
                    for t in range(2):
                        nc.vector.tensor_scalar(y[:, u, t], res[:, t], mv[:, t, 0:1], rstd[:, t:t + 1],
                                                ALU.subtract, ALU.mult).then_inc(tailed.sem, 1)
                    if tail == "affine":
                        dve.wait_ge(tailed.sem, tailed.at(i, 6))
                        nc.vector.tensor_tensor(y[:, u], y[:, u], row_pair(u, 1), ALU.mult).then_inc(tailed.sem, 1)
                        dve.wait_ge(tailed.sem, tailed.at(i, 7))
                        nc.vector.tensor_tensor(y[:, u], y[:, u], row_pair(u, 2), ALU.add).then_inc(tailed.sem, 1)

                def quad(i, u, lead, end=True, ahead=True):
                    if end:
                        finish(i - 2, u)
                    softmax_shift(i, u)
                    if ahead and pre_norm:
                        pre(i + 2, u)
                    if end and tail != "none":
                        scale(i - 2, u)
                    if lead and rope:
                        times_cos(i + 1, 1 - u)
                    sums(i, u)
                    if lead and rope:
                        rotate(i + 1, 1 - u)
                    if lead:
                        lay_values(i + 1, 1 - u)

                set_constants()
                if pre_norm:
                    pre(0, 0)
                dve.wait_ge(w_loaded.sem, w_loaded.at(0))
                dve.wait_ge(consts_set.sem, consts_set.at(0))
                if rope:
                    times_cos(0, 0)
                    rotate(0, 0)
                lay_values(0, 0)
                if pre_norm:
                    pre(1, 1)
                quad(0, 0, True, False)
                quad(1, 1, True, False)
                quad(2, 0, True)
                with dve.Fori(1, (QUADS - 4) // 2) as r:
                    for h in range(2):
                        quad(2 * r + (1 + h), (1 + h) % 2, True)
                quad(QUADS - 3, 1, True)
                quad(QUADS - 2, 0, True, True, False)
                quad(QUADS - 1, 1, False, True, False)
                for h in range(2):
                    finish(QUADS - 2 + h, h)
                    if tail != "none":
                        scale(QUADS - 2 + h, h)


def mamba(nc, ps, dram, x_in, x_out):
    CHUNKS, N, G = TILES // 4, 64, 2
    GROUPS = N // G
    SLOTS, AHEAD = 8, 2
    LOG1P = [1.0, -1 / 2, 1 / 3, -1 / 4, 1 / 5, -1 / 6, 1 / 7]
    NORM_EPS = 1e-5
    with ExitStack() as mem:
        st = Stage(nc, mem, "mb")
        ident = st.sb("ident", [128, 128])
        sel = st.sb("sel", [128, N], BF16)
        sel_f = st.sb("sel_f", [128, N])
        norm_w = st.sb("norm_w", [128, 1])
        w_in = st.sb("w_in", [128, 4, 128])
        conv_w = st.sb("conv_w", [128, 2, 4])
        conv_b = st.sb("conv_b", [128, 2])
        w_dt = st.sb("w_dt", [128, 2, 2, 128])
        dt_b = st.sb("dt_b", [128, 2])
        w_bc = st.sb("w_bc", [128, 2, 2, 128])
        a_neg = st.sb("a_neg", [128, N])
        w_out = st.sb("w_out", [128, 2, 128])
        x = st.sb("x", [128, 2, 4, 128])
        xn = st.sb("xn", [128, 4, 128])
        xT = st.sb("xT", [128, 512])
        xpad = st.sb("xpad", [128, 2, 8, 67])
        cv = st.sb("cv", [128, 2, 8, 64])
        xc = st.sb("xc", [128, 2, 512])
        zs = st.sb("zs", [128, 2, 2, 512])
        ex = st.sb("ex", [128, 2, 512])
        lp = st.sb("lp", [128, 2, 512])
        dt = st.sb("dt", [128, 2, 2, 8, 64])
        w = st.sb("w", [128, 2, 2, 512])
        bc = st.sb("bc", [128, 2, 512])
        rest = st.sb("rest", [64, 2, 512])
        mid = st.sb("mid", [64, 2, 512], BF16)
        bc_hi = st.sb("bc_hi", [128, 2, 2, 512], BF16)
        bc_lo = st.sb("bc_lo", [128, 2, 2, 512], BF16)
        Bb = st.sb("Bb", [128, 2, G, 512])
        dA = st.sb("dA", [128, SLOTS, G, 8, 64])
        h = st.sb("h", [128, SLOTS, G, 512])
        yz = st.sb("yz", [128, 2, 512])
        y = st.sb("y", [128, 2, 4, 128])
        stats = st.sb("stats", [128, 4, 6])
        mv = st.sb("mv", [128, 4, 2])
        msq = st.sb("msq", [128, 4])
        nrstd = st.sb("nrstd", [128, 4])
        half_neg = st.sb("half_neg", [128, 4])
        eps = st.sb("eps", [128, 4])
        seen = st.sb("seen", [128, 1])

        loads = [(ident[:], dram["ident"]), (sel_f[:], dram["mb_sel"]), (norm_w[:], dram["mb_norm_w"]),
                 (w_in[:], dram["mb_in"]), (conv_w[:], dram["mb_conv_w"]), (conv_b[:], dram["mb_conv_b"]),
                 (w_dt[:], dram["mb_dt"]), (dt_b[:], dram["mb_dt_b"]), (w_bc[:], dram["mb_bc"]),
                 (a_neg[:], bcast_rows(dram["mb_a_log"])), (w_out[:], dram["mb_out"])]
        K = 2 * GROUPS
        w_loaded = st.dma_signal("w_loaded", len(loads))
        x_loaded = st.slot_signal("x_loaded")
        y_stored = st.slot_signal("y_stored")
        set_pool = st.counter("set_pool", 4 + SLOTS)
        set_act = st.counter("set_act", 2)
        set_dve = st.counter("set_dve", 1)
        normed = st.counter("normed", 5)
        nrstd_ready = st.counter("nrstd_ready", 2)
        xT_done = st.counter("xT_done")
        xT_ready = st.counter("xT_ready")
        in_done = st.counter("in_done", 4)
        in_taken = st.counter("in_taken", 4)
        conv_step = st.counter("conv_step", 8)
        xc_ready = st.counter("xc_ready", 2)
        bc_done = st.counter("bc_done", 2)
        bc_taken = st.counter("bc_taken", 2)
        hi_ready = st.counter("hi_ready", 2)
        rest_ready = st.counter("rest_ready", 2)
        mid_ready = st.counter("mid_ready", 1)
        lo_ready = st.counter("lo_ready", 1)
        dt_done = st.counter("dt_done", 2)
        ex_ready = st.counter("ex_ready", 2)
        dt_step = st.counter("dt_step", 20)
        b_done = st.counter("b_done", N)
        b_taken = st.counter("b_taken", N)
        c_done = st.counter("c_done", GROUPS)
        dA_ready = st.counter("dA_ready", K)
        u_ready = st.counter("u_ready", K)
        scanned = st.counter("scanned", K)
        weighed = st.counter("weighed", K)
        product = st.counter("product", GROUPS // 2)
        summed = st.counter("summed", K)
        gated = st.counter("gated", 2)
        out_done = st.counter("out_done")
        y_ready = st.counter("y_ready")

        def paired(q, f):
            return f == 1 and q % 2 == 1

        def bcast_sel(n):
            return sel[:, n:n + 1].to_broadcast([128, 128])

        def loop(eng, chunk, first, last):
            first()
            chunk(0, 0, True, False)
            with eng.Fori(0, (CHUNKS - 2) // 2) as r:
                for v in range(2):
                    chunk(2 * r + (1 + v), (1 + v) % 2, True, True)
            chunk(CHUNKS - 1, (CHUNKS - 1) % 2, False, True)
            last(CHUNKS - 1, (CHUNKS - 1) % 2)

        st.begin()
        with nc.Block() as block:

            @block.sync
            def _(sp):
                for dst, src in loads:
                    sp.dma_start(dst, src).then_inc(w_loaded.sem, 16)

                def load(i, u):
                    sp.wait_ge(y_ready.sem, y_ready.at(i - 2))
                    sp.dma_start(x[:, u], tiles_of(x_in, i, 4)).then_inc(x_loaded.of(u), 16)

                def store(i, u):
                    sp.wait_ge(y_ready.sem, y_ready.at(i))
                    sp.dma_start(tiles_of(x_out, i, 4), y[:, u]).then_inc(y_stored.of(u), 16)

                load(0, 0)
                load(1, 1)
                with sp.Fori(0, CHUNKS // 2 - 1) as r:
                    for u in range(2):
                        store(2 * r + u, u)
                        load(2 * r + (u + 2), u)
                for u in range(2):
                    store(CHUNKS - 2 + u, u)
                for u in range(2):
                    sp.wait_ge(y_stored.of(u), y_stored.at(CHUNKS - 2 + u, u))

            @block.tensor
            def _(pe):
                def turn(i):
                    pe.wait_ge(normed.sem, normed.at(i))
                    pe.wait_ge(y_ready.sem, y_ready.at(i - 2))
                    for t in range(4):
                        mm = nc.tensor.transpose(ps[:, 1, 128 * t:128 * t + 128], xn[:, t], ident[:])
                    mm.then_inc(xT_done.sem, 1)

                def project_in(i, m):
                    if m == 0:
                        pe.wait_ge(xT_ready.sem, xT_ready.at(i))
                    else:
                        pe.wait_ge(in_taken.sem, in_taken.at(i, m))
                    nc.tensor.matmul(ps[:, 1, :], w_in[:, m], xT[:], start=True, stop=True).then_inc(in_done.sem, 1)

                def project_bc(i, z):
                    if z == 0:
                        pe.wait_ge(in_taken.sem, in_taken.at(i))
                        pe.wait_ge(xc_ready.sem, xc_ready.at(i))
                    else:
                        pe.wait_ge(bc_taken.sem, bc_taken.at(i, 1))
                    nc.tensor.matmul(ps[:, 1, :], w_bc[:, 0, z], xc[:, 0], start=True, stop=False)
                    nc.tensor.matmul(ps[:, 1, :], w_bc[:, 1, z], xc[:, 1], start=False, stop=True).then_inc(bc_done.sem, 1)

                def project_dt(i, f):
                    if f == 0:
                        pe.wait_ge(bc_taken.sem, bc_taken.at(i))
                    else:
                        pe.wait_ge(ex_ready.sem, ex_ready.at(i, 1))
                    nc.tensor.matmul(ps[:, 1, :], w_dt[:, 0, f], xc[:, 0], start=True, stop=False)
                    nc.tensor.matmul(ps[:, 1, :], w_dt[:, 1, f], xc[:, 1], start=False, stop=True).then_inc(dt_done.sem, 1)

                pieces = {6: turn} | {8 + 2 * m: lambda i, m=m: project_in(i, m) for m in range(4)} | {
                    16: lambda i: project_bc(i, 0), 18: lambda i: project_bc(i, 1),
                    20: lambda i: project_dt(i, 0), 22: lambda i: project_dt(i, 1)}

                def spread_b(i, u, q, j):
                    n = G * q + j
                    pe.wait_ge(b_taken.sem, b_taken.at(i, n))
                    if n == 0:
                        pe.wait_ge(lo_ready.sem, lo_ready.at(i))
                    nc.tensor.matmul(ps[:, 0, :], bcast_sel(n), bc_hi[:, u, 0], start=True, stop=False)
                    nc.tensor.matmul(ps[:, 0, :], bcast_sel(n), bc_lo[:, u, 0], start=False, stop=True).then_inc(
                        b_done.sem, 1)

                def spread_c(i, u, q):
                    pe.wait_ge(weighed.sem, weighed.at(i, 2 * (q - 1)))
                    if q == 0:
                        pe.wait_ge(lo_ready.sem, lo_ready.at(i))
                    for j in range(G):
                        n, bank = G * q + j, 2 + 2 * (q % 2) + j
                        nc.tensor.matmul(ps[:, bank, :], bcast_sel(n), bc_hi[:, u, 1], start=True, stop=False)
                        mm = nc.tensor.matmul(ps[:, bank, :], bcast_sel(n), bc_lo[:, u, 1], start=False, stop=True)
                    mm.then_inc(c_done.sem, 1)

                def sum_state(i, q, f, j):
                    if j == 0:
                        pe.wait_ge(weighed.sem, weighed.at(i, 2 * q + f + 1))
                        if q == 0:
                            pe.wait_ge(gated.sem, gated.at(i - 1))
                    last = 0 if paired(q, f) else G - 1
                    if j > last:
                        return
                    mm = nc.tensor.matmul(ps[:, 6 + f, :], ident[:], h[:, (2 * q + f) % SLOTS, j], start=q == 0 and j == 0,
                                          stop=q == GROUPS - 1 and j == last)
                    if j == last:
                        mm.then_inc(summed.sem, 1)

                def project_out(i):
                    pe.wait_ge(gated.sem, gated.at(i))
                    if isinstance(i, int) and i == CHUNKS - 1:
                        pe.wait_ge(ex_ready.sem, ex_ready.at(i))
                    else:
                        pe.wait_ge(ex_ready.sem, ex_ready.at(i + 1))
                    for t in range(4):
                        for f in range(2):
                            mm = nc.tensor.matmul(ps[:, 1, 128 * t:128 * t + 128], yz[:, f, 128 * t:128 * t + 128],
                                                  w_out[:, f], start=f == 0, stop=f == 1)
                    mm.then_inc(out_done.sem, 1)

                def first():
                    pe.wait_ge(w_loaded.sem, w_loaded.at(0))
                    pe.wait_ge(set_act.sem, set_act.at(0))
                    for q in sorted(pieces):
                        pieces[q](0)
                    for q in range(AHEAD):
                        for j in range(G):
                            spread_b(0, 0, q, j)
                    spread_c(0, 0, 0)

                def chunk(i, u, lead, trail):
                    for q in range(GROUPS):
                        for j in range(G):
                            if q < GROUPS - AHEAD:
                                spread_b(i, u, q + AHEAD, j)
                            elif lead:
                                spread_b(i + 1, 1 - u, q + AHEAD - GROUPS, j)
                            if j == 0:
                                if q < GROUPS - 1:
                                    spread_c(i, u, q + 1)
                                elif lead:
                                    spread_c(i + 1, 1 - u, 0)
                            for g in range(G):
                                if q >= 1:
                                    sum_state(i, q - 1, j, g)
                                elif trail:
                                    sum_state(i - 1, GROUPS - 1, j, g)
                        if q == 1 and trail:
                            project_out(i - 1)
                        if lead and q in pieces:
                            pieces[q](i + 1)

                def last(i, u):
                    for f in range(2):
                        for j in range(G):
                            sum_state(i, GROUPS - 1, f, j)
                    project_out(i)

                loop(pe, chunk, first, last)

            @block.scalar
            def _(act):
                def take_turn(i):
                    act.wait_ge(xT_done.sem, xT_done.at(i))
                    act.wait_ge(in_done.sem, in_done.at(i - 1))
                    nc.scalar.activation(xT[:], ps[:, 1, :], ACT.Identity, scale=norm_w[:, 0:1]).then_inc(xT_ready.sem, 1)

                def take_x(i, f):
                    act.wait_ge(in_done.sem, in_done.at(i, f + 1))
                    act.wait_ge(conv_step.sem, conv_step.at(i - 1))
                    nc.scalar.copy(xpad[:, f, :, 1:65], ps[:, 1, :].rearrange("p (b t) -> p b t", b=8)).then_inc(
                        in_taken.sem, 1)

                def take_z(i, u, f):
                    act.wait_ge(in_done.sem, in_done.at(i, f + 3))
                    act.wait_ge(gated.sem, gated.at(i - 2))
                    nc.scalar.activation(zs[:, u, f], ps[:, 1, :], ACT.Silu).then_inc(in_taken.sem, 1)

                def silu_x(i, f):
                    act.wait_ge(conv_step.sem, conv_step.at(i, 4 * f + 4))
                    act.wait_ge(dt_step.sem, dt_step.at(i - 1))
                    nc.scalar.activation(xc[:, f], cv[:, f].rearrange("p b t -> p (b t)"), ACT.Silu).then_inc(
                        xc_ready.sem, 1)

                def take_bc(i, u, z):
                    act.wait_ge(bc_done.sem, bc_done.at(i, z + 1))
                    act.wait_ge(rest_ready.sem, rest_ready.at(i - 1))
                    act.wait_ge(c_done.sem, c_done.at(i - 2))
                    nc.scalar.copy(bc[:, z], ps[:, 1, :]).then_inc(bc_taken.sem, 1)
                    act.wait_ge(bc_taken.sem, bc_taken.at(i, z + 1))
                    nc.scalar.copy(bc_hi[:, u, z], bc[:, z]).then_inc(hi_ready.sem, 1)

                def round_mid(i):
                    act.wait_ge(rest_ready.sem, rest_ready.at(i, 1))
                    act.wait_ge(lo_ready.sem, lo_ready.at(i - 1))
                    nc.scalar.copy(mid[:], rest[:]).then_inc(mid_ready.sem, 1)

                def exp_dt(i, f):
                    act.wait_ge(dt_done.sem, dt_done.at(i, f + 1))
                    act.wait_ge(dt_step.sem, dt_step.at(i - 1))
                    nc.scalar.activation(ex[:, f], ps[:, 1, :], ACT.Exp, bias=dt_b[:, f:f + 1]).then_inc(ex_ready.sem, 1)

                pieces = {6: [lambda i, u: take_turn(i)], 8: [lambda i, u: take_x(i, 0)],
                          10: [lambda i, u: take_x(i, 1)], 12: [lambda i, u: take_z(i, u, 0), lambda i, u: silu_x(i, 0)],
                          14: [lambda i, u: take_z(i, u, 1), lambda i, u: silu_x(i, 1)],
                          16: [lambda i, u: take_bc(i, u, 0)], 18: [lambda i, u: take_bc(i, u, 1)],
                          20: [lambda i, u: exp_dt(i, 0)], 22: [lambda i, u: exp_dt(i, 1)],
                          24: [lambda i, u: round_mid(i)]}

                def take_b(i, q, j):
                    act.wait_ge(b_done.sem, b_done.at(i, G * q + j + 1))
                    if j == 0:
                        act.wait_ge(u_ready.sem, u_ready.at(i, 2 * (q - 1)))
                    nc.scalar.copy(Bb[:, q % 2, j], ps[:, 0, :]).then_inc(b_taken.sem, 1)

                def decay(i, u, q, f):
                    k = 2 * q + f
                    act.wait_ge(scanned.sem, scanned.at(i, k + 1 - SLOTS))
                    if q == 0:
                        act.wait_ge(dt_step.sem, dt_step.at(i))
                    for j in range(G):
                        n = G * q + j
                        ins = nc.scalar.activation(dA[:, k % SLOTS, j, :, 1:64], dt[:, u, f, :, 1:64], ACT.Exp,
                                                   scale=a_neg[:, n:n + 1])
                    ins.then_inc(dA_ready.sem, 1)

                def first():
                    act.wait_ge(w_loaded.sem, w_loaded.at(0))
                    nc.scalar.copy(sel[:], sel_f[:]).then_inc(set_act.sem, 1)
                    nc.scalar.activation(a_neg[:], a_neg[:], ACT.Exp).then_inc(set_act.sem, 1)
                    act.wait_ge(set_pool.sem, set_pool.at(0))
                    act.wait_ge(set_dve.sem, set_dve.at(0))
                    for q in sorted(pieces):
                        for piece in pieces[q]:
                            piece(0, 0)
                    for q in range(AHEAD):
                        for j in range(G):
                            take_b(0, q, j)
                    for f in range(2):
                        decay(0, 0, 0, f)

                def chunk(i, u, lead, trail):
                    for q in range(GROUPS):
                        end = q == GROUPS - 1
                        if not end:
                            decay(i, u, q + 1, 0)
                        elif lead:
                            decay(i + 1, 1 - u, 0, 0)
                        for j in range(G):
                            if q < GROUPS - AHEAD:
                                take_b(i, q + AHEAD, j)
                            elif lead:
                                take_b(i + 1, q + AHEAD - GROUPS, j)
                        if lead and q in pieces:
                            for piece in pieces[q]:
                                piece(i + 1, 1 - u)
                        if not end:
                            decay(i, u, q + 1, 1)
                        elif lead:
                            decay(i + 1, 1 - u, 0, 1)

                loop(act, chunk, first, lambda i, u: None)

            @block.gpsimd
            def _(pool):
                def norm_scale(i):
                    pool.wait_ge(normed.sem, normed.at(i, 4))
                    nc.gpsimd.tensor_tensor(nrstd[:], msq[:], eps[:], ALU.add).then_inc(nrstd_ready.sem, 1)
                    pool.wait_ge(nrstd_ready.sem, nrstd_ready.at(i, 1))
                    nc.gpsimd.tensor_tensor(nrstd[:], nrstd[:], half_neg[:], ALU.pow).then_inc(nrstd_ready.sem, 1)


                def take_rest(i, u):
                    pool.wait_ge(nrstd_ready.sem, nrstd_ready.at(i))
                    pool.wait_ge(u_ready.sem, u_ready.at(i - 1, 2 * 21 + 1))
                    pool.wait_ge(hi_ready.sem, hi_ready.at(i))
                    pool.wait_ge(lo_ready.sem, lo_ready.at(i - 1))
                    nc.gpsimd.tensor_tensor(rest[:], bc[0:64], bc_hi[0:64, u], ALU.subtract).then_inc(rest_ready.sem, 1)
                    pool.wait_ge(rest_ready.sem, rest_ready.at(i, 1))

                def take_mid(i, u):
                    pool.wait_ge(u_ready.sem, u_ready.at(i - 1, 2 * 23 + 1))
                    nc.gpsimd.tensor_tensor(bc_hi[64:128, u], bc[64:128], bc_hi[64:128, u], ALU.subtract).then_inc(
                        rest_ready.sem, 1)
                    pool.wait_ge(rest_ready.sem, rest_ready.at(i, 2))

                def take_lo(i, u):
                    pool.wait_ge(u_ready.sem, u_ready.at(i - 1, 2 * 27 + 1))
                    pool.wait_ge(mid_ready.sem, mid_ready.at(i))
                    nc.gpsimd.tensor_tensor(bc_lo[0:64, u], rest[:], mid[:], ALU.subtract).then_inc(lo_ready.sem, 1)
                    pool.wait_ge(lo_ready.sem, lo_ready.at(i))

                pieces = {4: lambda i, u: norm_scale(i), 20: take_rest, 22: take_mid, 26: take_lo}

                def inputs(i, u, q, f):
                    k = 2 * q + f
                    pool.wait_ge(summed.sem, summed.at(i, k + 1 - SLOTS))
                    if f == 0:
                        pool.wait_ge(b_taken.sem, b_taken.at(i, G * (q + 1)))
                    if q == 0:
                        pool.wait_ge(dt_step.sem, dt_step.at(i))
                    nc.gpsimd.tensor_tensor(h[:, k % SLOTS], Bb[:, q % 2],
                                            w[:, u, f].rearrange("p (a t) -> p a t", a=1).to_broadcast([128, G, 512]),
                                            ALU.mult).then_inc(u_ready.sem, 1)

                def first():
                    nc.gpsimd.memset(half_neg[:], -0.5).then_inc(set_pool.sem, 1)
                    nc.gpsimd.memset(eps[:], NORM_EPS).then_inc(set_pool.sem, 1)
                    nc.gpsimd.memset(xpad[:], 0.0).then_inc(set_pool.sem, 1)
                    nc.gpsimd.memset(bc_lo[:], 0.0).then_inc(set_pool.sem, 1)
                    for s in range(SLOTS):
                        nc.gpsimd.memset(dA[:, s, :, :, 0:1], 0.0).then_inc(set_pool.sem, 1)
                    pool.wait_ge(set_pool.sem, set_pool.at(0))
                    for q in sorted(pieces):
                        pieces[q](0, 0)
                    for f in range(2):
                        inputs(0, 0, 0, f)

                def chunk(i, u, lead, trail):
                    for q in range(GROUPS):
                        for f in range(2):
                            if q < GROUPS - 1:
                                inputs(i, u, q + 1, f)
                            elif lead:
                                inputs(i + 1, 1 - u, 0, f)
                            if f == 0 and lead and q in pieces:
                                pieces[q](i + 1, 1 - u)

                loop(pool, chunk, first, lambda i, u: None)

            @block.vector
            def _(dve):
                def norm(i, u):
                    dve.wait_ge(x_loaded.of(u), x_loaded.at(i, u))
                    for t in range(4):
                        ins = nc.vector.bn_stats(stats[:, t], x[:, u, t])
                    ins.then_inc(normed.sem, 1)
                    dve.wait_ge(normed.sem, normed.at(i, 1))
                    nc.vector.tensor_copy(seen[:], stats[:, 0, 0:1])
                    for t in range(4):
                        ins = nc.vector.bn_aggr(mv[:, t], stats[:, t])
                    ins.then_inc(normed.sem, 1)
                    dve.wait_ge(normed.sem, normed.at(i, 2))
                    nc.vector.tensor_tensor(msq[:], mv[:, :, 0], mv[:, :, 0], ALU.mult).then_inc(normed.sem, 1)
                    dve.wait_ge(normed.sem, normed.at(i, 3))
                    nc.vector.tensor_tensor(msq[:], msq[:], mv[:, :, 1], ALU.add).then_inc(normed.sem, 1)

                def scale(i, u):
                    dve.wait_ge(nrstd_ready.sem, nrstd_ready.at(i))
                    dve.wait_ge(xT_done.sem, xT_done.at(i - 1))
                    for t in range(4):
                        ins = nc.vector.tensor_scalar(xn[:, t], x[:, u, t], nrstd[:, t:t + 1], None, ALU.mult)
                    ins.then_inc(normed.sem, 1)

                def conv(i, f, k):
                    if k == 0:
                        dve.wait_ge(in_taken.sem, in_taken.at(i, f + 1))
                        dve.wait_ge(xc_ready.sem, xc_ready.at(i - 1))
                        nc.vector.tensor_scalar(cv[:, f], xpad[:, f, :, 0:64], conv_w[:, f, 0:1], conv_b[:, f:f + 1],
                                                ALU.mult, ALU.add).then_inc(conv_step.sem, 1)
                        return
                    dve.wait_ge(conv_step.sem, conv_step.at(i, 4 * f + k))
                    nc.vector.scalar_tensor_tensor(cv[:, f], xpad[:, f, :, k:k + 64], conv_w[:, f, k:k + 1], cv[:, f],
                                                   ALU.mult, ALU.add).then_inc(conv_step.sem, 1)

                def make_dt(i, u, f, k):
                    e, p, d = ex[:, f], lp[:, f], dt[:, u, f].rearrange("p b t -> p (b t)")
                    if k == 1:
                        dve.wait_ge(ex_ready.sem, ex_ready.at(i, f + 1))
                        dve.wait_ge(dA_ready.sem, dA_ready.at(i - 2))
                        dve.wait_ge(u_ready.sem, u_ready.at(i - 2))
                        ins = nc.vector.tensor_scalar(e, e, 0.11, None, ALU.min)
                    else:
                        dve.wait_ge(dt_step.sem, dt_step.at(i, 10 * f + k - 1))
                        if k == 2:
                            ins = nc.vector.tensor_scalar(p, e, LOG1P[6], LOG1P[5], ALU.mult, ALU.add)
                        elif k == 3:
                            ins = nc.vector.tensor_tensor(p, p, e, ALU.mult)
                        elif k <= 8:
                            ins = nc.vector.scalar_tensor_tensor(p, p, LOG1P[8 - k], e, ALU.add, ALU.mult)
                        elif k == 9:
                            ins = nc.vector.tensor_scalar(d, p, 1e-3, 0.1, ALU.max, ALU.min)
                        else:
                            ins = nc.vector.tensor_tensor(w[:, u, f], d, xc[:, f], ALU.mult)
                    ins.then_inc(dt_step.sem, 1)

                pieces = {4: [norm], 6: [scale]}
                for n in range(8):
                    pieces.setdefault(10 + n // 2, []).append(lambda i, u, n=n: conv(i, n // 4, n % 4))
                for n in range(20):
                    pieces.setdefault(22 + (2 * n) // 5, []).append(lambda i, u, n=n: make_dt(i, u, n // 10, n % 10 + 1))

                def scan(i, q, f):
                    k = 2 * q + f
                    dve.wait_ge(dA_ready.sem, dA_ready.at(i, k + 1))
                    dve.wait_ge(u_ready.sem, u_ready.at(i, k + 1))
                    s = k % SLOTS
                    nc.vector.tensor_tensor_scan(h[:, s].rearrange("p n t -> p (n t)"),
                                                 dA[:, s].rearrange("p n b t -> p (n b t)"),
                                                 h[:, s].rearrange("p n t -> p (n t)"), 0.0, ALU.mult, ALU.add).then_inc(
                                                     scanned.sem, 1)

                def weigh(i, q, f):
                    k = 2 * q + f
                    dve.wait_ge(scanned.sem, scanned.at(i, k + 1))
                    dve.wait_ge(c_done.sem, c_done.at(i, q + 1))
                    c = 2 + 2 * (q % 2)
                    s = k % SLOTS
                    ins = nc.vector.tensor_tensor(h[:, s], h[:, s], ps[:, c:c + 2, :], ALU.mult)
                    if paired(q, f):
                        ins.then_inc(product.sem, 1)
                        dve.wait_ge(product.sem, product.at(i, q // 2 + 1))
                        ins = nc.vector.tensor_tensor(h[:, s, 0], h[:, s, 0], h[:, s, 1], ALU.add)
                    ins.then_inc(weighed.sem, 1)

                def gating(i, u):
                    dve.wait_ge(summed.sem, summed.at(i))
                    dve.wait_ge(out_done.sem, out_done.at(i - 1))
                    for f in range(2):
                        nc.vector.tensor_tensor(yz[:, f], ps[:, 6 + f, :], zs[:, u, f], ALU.mult).then_inc(gated.sem, 1)

                def output(i, u):
                    dve.wait_ge(out_done.sem, out_done.at(i))
                    dve.wait_ge(y_stored.of(u), y_stored.at(i - 2, u))
                    nc.vector.tensor_tensor(y[:, u], ps[:, 1, :].rearrange("p (t d) -> p t d", t=4), x[:, u],
                                            ALU.add).then_inc(y_ready.sem, 1)

                def first():
                    dve.wait_ge(w_loaded.sem, w_loaded.at(0))
                    dve.wait_ge(set_act.sem, set_act.at(0))
                    nc.vector.tensor_scalar(a_neg[:], a_neg[:], -1.0, None, ALU.mult).then_inc(set_dve.sem, 1)
                    dve.wait_ge(set_pool.sem, set_pool.at(0))
                    for q in sorted(pieces):
                        for piece in pieces[q]:
                            piece(0, 0)

                def chunk(i, u, lead, trail):
                    for q in range(GROUPS):
                        scan(i, q, 0)
                        if q == 1 and trail:
                            gating(i - 1, 1 - u)
                        scan(i, q, 1)
                        weigh(i, q, 0)
                        if q == 2 and trail:
                            output(i - 1, 1 - u)
                        if lead:
                            for piece in pieces.get(q, []):
                                piece(i + 1, 1 - u)
                        weigh(i, q, 1)

                def last(i, u):
                    gating(i, u)
                    output(i, u)

                loop(dve, chunk, first, last)


def rope_tables(nc, dram, tables):
    PARTS = 128 // 8
    N = B * S // PARTS
    TWO_PI = 2 * np.pi
    C1 = 6.28125
    C2 = float(np.float32(np.floor((TWO_PI - C1) * 2.0 ** 21) / 2.0 ** 21))
    C3 = float(TWO_PI - C1 - C2)
    ROUND = 1.5 * 2.0 ** 23
    PI_IN = 3.1415925
    with ExitStack() as mem:
        st = Stage(nc, mem, "rope")
        freq = st.sb("freq", [128, 1])
        sign = st.sb("sign", [128, 1])
        pos_i = st.sb("pos_i", [128, N], I32)
        angle = st.sb("angle", [128, N])
        count = st.sb("count", [128, 2, N])
        turned = st.sb("turned", [128, 2, N])
        loaded = st.dma_signal("loaded", 2 + PARTS)
        cast = st.counter("cast", 2)
        reduced = st.counter("reduced", 14)
        sine = st.counter("sine", 2)
        signed = st.counter("signed")
        stored = st.dma_signal("stored", 2 * PARTS)
        st.begin()
        with nc.Block() as block:

            @block.sync
            def _(sp):
                sp.dma_start(freq[:], dram["rope_freq"]).then_inc(loaded.sem, 16)
                sp.dma_start(sign[:], dram["rope_sign"]).then_inc(loaded.sem, 16)
                for c in range(PARTS):
                    sp.dma_start(pos_i[8 * c:8 * c + 8, :], bcast_rows(dram["pos"][N * c:N * c + N], 8)).then_inc(
                        loaded.sem, 16)
                for z, ready in enumerate((sine, signed)):
                    sp.wait_ge(ready.sem, ready.at(0, 1))
                    for c in range(PARTS):
                        sp.dma_start(tables[z][:, N * c:N * c + N], turned[8 * c:8 * c + 8, z]).then_inc(stored.sem, 16)
                sp.wait_ge(stored.sem, stored.at(0))

            @block.vector
            def _(dve):
                dve.wait_ge(loaded.sem, loaded.at(0))
                nc.vector.tensor_copy(angle[:], pos_i[:]).then_inc(cast.sem, 1)
                dve.wait_ge(cast.sem, cast.at(0, 1))
                nc.vector.tensor_scalar(angle[:], angle[:], freq[:, 0:1], None, ALU.mult).then_inc(cast.sem, 1)
                dve.wait_ge(cast.sem, cast.at(0, 2))
                for z, shift in enumerate((0.25, 0.0)):
                    k, n, v = 7 * z, count[:, z], turned[:, z]
                    steps = [lambda: nc.vector.tensor_scalar(n, angle[:], 1.0 / TWO_PI, shift, ALU.mult, ALU.add),
                             lambda: nc.vector.tensor_scalar(n, n, ROUND, None, ALU.add),
                             lambda: nc.vector.tensor_scalar(n, n, ROUND, None, ALU.subtract),
                             lambda: nc.vector.scalar_tensor_tensor(v, n, -C1, angle[:], ALU.mult, ALU.add),
                             lambda: nc.vector.scalar_tensor_tensor(v, n, -C2, v, ALU.mult, ALU.add),
                             lambda: nc.vector.scalar_tensor_tensor(v, n, -C3, v, ALU.mult, ALU.add)]
                    if z == 0:
                        steps.append(lambda: nc.vector.tensor_scalar(v, v, np.pi / 2, PI_IN, ALU.add, ALU.min))
                    else:
                        steps.append(lambda: nc.vector.tensor_scalar(v, v, PI_IN, -PI_IN, ALU.min, ALU.max))
                    for m, step in enumerate(steps):
                        step().then_inc(reduced.sem, 1)
                        dve.wait_ge(reduced.sem, reduced.at(0, k + m + 1))
                dve.wait_ge(sine.sem, sine.at(0))
                nc.vector.tensor_scalar(turned[:, 1], turned[:, 1], sign[:, 0:1], None, ALU.mult).then_inc(signed.sem, 1)

            @block.scalar
            def _(act):
                for z in range(2):
                    act.wait_ge(reduced.sem, reduced.at(0, 7 * z + 7))
                    nc.scalar.activation(turned[:, z], turned[:, z], ACT.Sin).then_inc(sine.sem, 1)


def swiglu(nc, ps, name, dram, x_skip, x_in, x_out):
    moe = name == "mo"
    E = 9 if moe else 1
    CHUNKS = TILES // 4
    norm_eps = 1e-6 if moe else 1e-5
    with ExitStack() as mem:
        st = Stage(nc, mem, name)
        ident = st.sb("ident", [128, 128])
        norm_w = st.sb("norm_w", [128, 1])
        wg = st.sb("wg", [128, E, 256])
        wu = st.sb("wu", [128, E, 256])
        wd = st.sb("wd", [128, E, 2, 128])
        x = st.sb("x", [128, 2, 4, 128])
        skip = st.sb("skip", [128, 2, 4, 128])
        xn = st.sb("xn", [128, 4, 128])
        hT = st.sb("hT", [128, 2, 512])
        gate = st.sb("gate", [128, 2, 512])
        gu = st.sb("gu", [128, 4, 512])
        acc = st.sb("acc", [128, 4, 128])
        y = st.sb("y", [128, 2, 4, 128])
        stats = st.sb("stats", [128, 4, 6])
        mv = st.sb("mv", [128, 4, 2])
        msq = st.sb("msq", [128, 4])
        nrstd = st.sb("nrstd", [128, 4])
        ystats = st.sb("ystats", [128, 4, 6])
        ymv = st.sb("ymv", [128, 4, 2])
        rstd = st.sb("rstd", [128, 4])
        half_neg = st.sb("half_neg", [128, 4])
        eps = st.sb("eps", [128, 4])
        eps_n = st.sb("eps_n", [128, 4])
        seen = st.sb("seen", [128, 2])
        loads = [(ident[:], dram["ident"]), (norm_w[:], dram[name + "norm_w"])]
        loads += [(wg[:], dram[name + "wg"]), (wu[:], dram[name + "wu"]), (wd[:], dram[name + "wd"])]
        if moe:
            wr = st.sb("wr", [128, 8])
            order = st.sb("order", [128, 8])
            loads += [(wr[:], dram["router"]), (order[:], bcast_rows(dram["order"]))]
            lg = st.sb("lg", [128, 4, 8])
            pr = st.sb("pr", [128, 4, 8])
            cand = st.sb("cand", [128, 4, 8])
            one1 = st.sb("one1", [128, 4, 8])
            one2 = st.sb("one2", [128, 4, 8])
            r1 = st.sb("r1", [128, 4])
            m1 = st.sb("m1", [128, 4])
            m2 = st.sb("m2", [128, 4])
            comb = st.sb("comb", [128, 4, 8])
        w_loaded = st.dma_signal("w_loaded", len(loads))
        x_loaded = st.slot_signal("x_loaded", 2)
        y_stored = st.slot_signal("y_stored", 1)
        half_set = st.counter("half_set", 3)
        normed = st.counter("normed", 5)
        nrstd_ready = st.counter("nrstd_ready", 2)
        xT_done = st.counter("xT_done")
        hT_ready = st.counter("hT_ready")
        gu_done = st.counter("gu_done", 2 * E)
        gate_ready = st.counter("gate_ready", 2 * E)
        gu_ready = st.counter("gu_ready", 2 * E)
        down_done = st.counter("down_done", E)
        acc_set = st.counter("acc_set")
        added = st.counter("added", E)
        r_done = st.counter("r_done")
        r_step = st.counter("r_step", 24)
        r_exp = st.counter("r_exp", 2)
        tailed = st.counter("tailed", 2)
        y_ready = st.counter("y_ready")
        rstd_ready = st.counter("rstd_ready", 2)

        st.begin()
        with nc.Block() as block:

            @block.sync
            def _(sp):
                for dst, src in loads:
                    sp.dma_start(dst, src).then_inc(w_loaded.sem, 16)

                def load(i, u):
                    sp.wait_ge(y_ready.sem, y_ready.at(i - 2))
                    sp.dma_start(x[:, u], tiles_of(x_in, i, 4)).then_inc(x_loaded.of(u), 16)
                    sp.dma_start(skip[:, u], tiles_of(x_skip, i, 4)).then_inc(x_loaded.of(u), 16)

                def store(i, u):
                    sp.wait_ge(y_ready.sem, y_ready.at(i))
                    sp.dma_start(tiles_of(x_out, i, 4), y[:, u]).then_inc(y_stored.of(u), 16)

                load(0, 0)
                load(1, 1)
                with sp.Fori(0, CHUNKS // 2 - 1) as r:
                    for u in range(2):
                        store(2 * r + u, u)
                        load(2 * r + (u + 2), u)
                for u in range(2):
                    store(CHUNKS - 2 + u, u)
                for u in range(2):
                    sp.wait_ge(y_stored.of(u), y_stored.at(CHUNKS - 2 + u, u))

            @block.tensor
            def _(pe):
                def turn(i):
                    pe.wait_ge(normed.sem, normed.at(i))
                    pe.wait_ge(hT_ready.sem, hT_ready.at(i - 1))
                    for t in range(4):
                        mm = nc.tensor.transpose(ps[:, 6, 128 * t:128 * t + 128], xn[:, t], ident[:])
                    mm.then_inc(xT_done.sem, 1)

                def route(i, u):
                    pe.wait_ge(hT_ready.sem, hT_ready.at(i))
                    pe.wait_ge(r_step.sem, r_step.at(i - 1))
                    for t in range(4):
                        mm = nc.tensor.matmul(ps[:, 7, 8 * t:8 * t + 8], hT[:, u, 128 * t:128 * t + 128], wr[:],
                                              start=True, stop=True)
                    mm.then_inc(r_done.sem, 1)

                def gate_up(i, u, n):
                    e, f, b = n // 2, n % 2, 2 * (n % 2)
                    if n >= 2:
                        pe.wait_ge(gu_ready.sem, gu_ready.at(i, n - 1))
                    else:
                        pe.wait_ge(gu_ready.sem, gu_ready.at(i - 1))
                        pe.wait_ge(hT_ready.sem, hT_ready.at(i))
                    nc.tensor.matmul(ps[:, b, :], wg[:, e, 128 * f:128 * f + 128], hT[:, u], start=True, stop=True)
                    nc.tensor.matmul(ps[:, b + 1, :], wu[:, e, 128 * f:128 * f + 128], hT[:, u], start=True,
                                     stop=True).then_inc(gu_done.sem, 1)

                def down(i, e):
                    pe.wait_ge(gu_ready.sem, gu_ready.at(i, 2 * e + 2))
                    if e >= 2:
                        pe.wait_ge(added.sem, added.at(i, e - 1))
                    else:
                        pe.wait_ge(added.sem, added.at(i - 1))
                    s = 2 * (e % 2)
                    for t in range(4):
                        for f in range(2):
                            mm = nc.tensor.matmul(ps[:, 4 + e % 2, 128 * t:128 * t + 128],
                                                  gu[:, s + f, 128 * t:128 * t + 128], wd[:, e, f], start=f == 0,
                                                  stop=f == 1)
                    mm.then_inc(down_done.sem, 1)

                def chunk(i, u, lead):
                    if moe:
                        route(i, u)
                    for n in range(2 * E):
                        gate_up(i, u, n)
                        if n >= 3 and n % 2:
                            down(i, (n - 3) // 2)
                        if n == min(3, 2 * E - 1) and lead:
                            turn(i + 1)
                    down(i, E - 1)

                pe.wait_ge(w_loaded.sem, w_loaded.at(0))
                turn(0)
                with pe.Fori(0, CHUNKS // 2 - 1) as r:
                    for u in range(2):
                        chunk(2 * r + u, u, True)
                chunk(CHUNKS - 2, 0, True)
                chunk(CHUNKS - 1, 1, False)

            @block.scalar
            def _(act):
                def take(i, u):
                    act.wait_ge(xT_done.sem, xT_done.at(i))
                    act.wait_ge(gu_done.sem, gu_done.at(i - 2))
                    nc.scalar.activation(hT[:, u], ps[:, 6, :], ACT.Identity, scale=norm_w[:, 0:1]).then_inc(
                        hT_ready.sem, 1)

                def router_exp(i):
                    act.wait_ge(r_step.sem, r_step.at(i, 2))
                    nc.scalar.activation(pr[:], lg[:], ACT.Exp).then_inc(r_exp.sem, 1)
                    act.wait_ge(r_step.sem, r_step.at(i, 17))
                    nc.scalar.activation(m2[:], m2[:], ACT.Exp).then_inc(r_exp.sem, 1)

                def gates(i, n):
                    act.wait_ge(gu_done.sem, gu_done.at(i, n + 1))
                    if n >= 2:
                        act.wait_ge(gu_ready.sem, gu_ready.at(i, n - 1))
                    else:
                        act.wait_ge(gu_ready.sem, gu_ready.at(i - 1))
                    nc.scalar.activation(gate[:, n % 2], ps[:, 2 * (n % 2), :], ACT.Silu).then_inc(gate_ready.sem, 1)

                def chunk(i, u, lead):
                    if moe:
                        router_exp(i)
                    for n in range(2 * E):
                        gates(i, n)
                        if n == min(5, 2 * E - 1) and lead:
                            take(i + 1, 1 - u)

                act.wait_ge(w_loaded.sem, w_loaded.at(0))
                take(0, 0)
                with act.Fori(0, CHUNKS // 2 - 1) as r:
                    for u in range(2):
                        chunk(2 * r + u, u, True)
                chunk(CHUNKS - 2, 0, True)
                chunk(CHUNKS - 1, 1, False)

            @block.gpsimd
            def _(pool):
                def norm_scale(i):
                    pool.wait_ge(normed.sem, normed.at(i, 4))
                    nc.gpsimd.tensor_tensor(nrstd[:], msq[:], eps_n[:], ALU.add).then_inc(nrstd_ready.sem, 1)
                    pool.wait_ge(nrstd_ready.sem, nrstd_ready.at(i, 1))
                    nc.gpsimd.tensor_tensor(nrstd[:], nrstd[:], half_neg[:], ALU.pow).then_inc(nrstd_ready.sem, 1)

                def tail_scale(i):
                    pool.wait_ge(tailed.sem, tailed.at(i))
                    nc.gpsimd.tensor_tensor(rstd[:], ymv[:, :, 1], eps[:], ALU.add).then_inc(rstd_ready.sem, 1)
                    pool.wait_ge(rstd_ready.sem, rstd_ready.at(i, 1))
                    nc.gpsimd.tensor_tensor(rstd[:], rstd[:], half_neg[:], ALU.pow).then_inc(rstd_ready.sem, 1)

                nc.gpsimd.memset(half_neg[:], -0.5).then_inc(half_set.sem, 1)
                nc.gpsimd.memset(eps[:], LN_EPS).then_inc(half_set.sem, 1)
                nc.gpsimd.memset(eps_n[:], norm_eps).then_inc(half_set.sem, 1)
                pool.wait_ge(half_set.sem, half_set.at(0))
                norm_scale(0)
                with pool.Fori(0, CHUNKS - 1) as i:
                    norm_scale(i + 1)
                    tail_scale(i)
                tail_scale(CHUNKS - 1)

            @block.vector
            def _(dve):
                def pre(i, u):
                    dve.wait_ge(x_loaded.of(u), x_loaded.at(i, u))
                    for t in range(4):
                        ins = nc.vector.bn_stats(stats[:, t], x[:, u, t])
                    ins.then_inc(normed.sem, 1)
                    dve.wait_ge(normed.sem, normed.at(i, 1))
                    nc.vector.tensor_copy(seen[:, 0:1], stats[:, 0, 0:1])
                    for t in range(4):
                        ins = nc.vector.bn_aggr(mv[:, t], stats[:, t])
                    ins.then_inc(normed.sem, 1)
                    dve.wait_ge(normed.sem, normed.at(i, 2))
                    nc.vector.tensor_tensor(msq[:], mv[:, :, 0], mv[:, :, 0], ALU.mult).then_inc(normed.sem, 1)
                    dve.wait_ge(normed.sem, normed.at(i, 3))
                    nc.vector.tensor_tensor(msq[:], msq[:], mv[:, :, 1], ALU.add).then_inc(normed.sem, 1)
                    dve.wait_ge(nrstd_ready.sem, nrstd_ready.at(i))
                    dve.wait_ge(xT_done.sem, xT_done.at(i - 1))
                    for t in range(4):
                        ins = nc.vector.tensor_scalar(xn[:, t], x[:, u, t], nrstd[:, t:t + 1], None, ALU.mult)
                    ins.then_inc(normed.sem, 1)

                def start_acc(i, u):
                    dve.wait_ge(x_loaded.of(u), x_loaded.at(i, u))
                    dve.wait_ge(y_ready.sem, y_ready.at(i - 1))
                    nc.vector.tensor_tensor(acc[:], x[:, u], skip[:, u], ALU.add).then_inc(acc_set.sem, 1)

                def multiply(i, n):
                    e = n // 2
                    dve.wait_ge(gate_ready.sem, gate_ready.at(i, n + 1))
                    if e >= 2:
                        dve.wait_ge(down_done.sem, down_done.at(i, e - 1))
                    else:
                        dve.wait_ge(down_done.sem, down_done.at(i - 1))
                    nc.vector.tensor_tensor(gu[:, n % 4], gate[:, n % 2], ps[:, 2 * (n % 2) + 1, :], ALU.mult).then_inc(
                        gu_ready.sem, 1)

                def add(i, e):
                    dve.wait_ge(down_done.sem, down_done.at(i, e + 1))
                    out = ps[:, 4 + e % 2, :].rearrange("p (t d) -> p t d", t=4)
                    if e == 0:
                        dve.wait_ge(acc_set.sem, acc_set.at(i))
                        nc.vector.tensor_tensor(acc[:], acc[:], out, ALU.add).then_inc(added.sem, 1)
                        return
                    dve.wait_ge(added.sem, added.at(i, e))
                    if e == 1:
                        dve.wait_ge(r_step.sem, r_step.at(i))
                    for t in range(4):
                        ins = nc.vector.scalar_tensor_tensor(acc[:, t], out[:, t], comb[:, t, e - 1:e], acc[:, t],
                                                             ALU.mult, ALU.add)
                    ins.then_inc(added.sem, 1)

                def finish(i, u):
                    dve.wait_ge(added.sem, added.at(i))
                    for t in range(4):
                        ins = nc.vector.bn_stats(ystats[:, t], acc[:, t])
                    ins.then_inc(tailed.sem, 1)
                    dve.wait_ge(tailed.sem, tailed.at(i, 1))
                    nc.vector.tensor_copy(seen[:, 1:2], ystats[:, 0, 0:1])
                    for t in range(4):
                        ins = nc.vector.bn_aggr(ymv[:, t], ystats[:, t])
                    ins.then_inc(tailed.sem, 1)
                    dve.wait_ge(rstd_ready.sem, rstd_ready.at(i))
                    dve.wait_ge(y_stored.of(u), y_stored.at(i - 2, u))
                    for t in range(4):
                        ins = nc.vector.tensor_scalar(y[:, u, t], acc[:, t], ymv[:, t, 0:1], rstd[:, t:t + 1],
                                                      ALU.subtract, ALU.mult)
                    ins.then_inc(y_ready.sem, 1)

                def wide(v):
                    return v.rearrange("p (t a) -> p t a", a=1).to_broadcast([128, 4, 8])

                def step(i, k, ins):
                    ins.then_inc(r_step.sem, 1)
                    dve.wait_ge(r_step.sem, r_step.at(i, k))

                def pick(i, k, src, top, onehot):
                    step(i, k + 1, nc.vector.reduce_max(top[:], src[:], AX.X))
                    step(i, k + 2, nc.vector.tensor_tensor(cand[:], src[:], wide(top[:]), ALU.is_equal))
                    step(i, k + 3, nc.vector.tensor_tensor(
                        cand[:], cand[:], order[:].rearrange("p (a e) -> p a e", a=1).to_broadcast([128, 4, 8]), ALU.mult))
                    step(i, k + 4, nc.vector.reduce_max(r1[:], cand[:], AX.X))
                    step(i, k + 5, nc.vector.tensor_tensor(onehot[:], cand[:], wide(r1[:]), ALU.is_equal))

                def router(i):
                    dve.wait_ge(r_done.sem, r_done.at(i))
                    logits = ps[:, 7, 0:32].rearrange("p (t e) -> p t e", t=4)
                    step(i, 1, nc.vector.reduce_max(r1[:], logits, AX.X))
                    step(i, 2, nc.vector.tensor_tensor(lg[:], logits, wide(r1[:]), ALU.subtract))
                    dve.wait_ge(r_exp.sem, r_exp.at(i, 1))
                    step(i, 3, nc.vector.reduce_sum(r1[:], pr[:], AX.X))
                    step(i, 4, nc.vector.reciprocal(r1[:], r1[:]))
                    step(i, 5, nc.vector.tensor_tensor(pr[:], pr[:], wide(r1[:]), ALU.mult))
                    pick(i, 5, pr, m1, one1)
                    step(i, 11, nc.vector.scalar_tensor_tensor(pr[:], one1[:], -4.0, pr[:], ALU.mult, ALU.add))
                    pick(i, 11, pr, m2, one2)
                    step(i, 17, nc.vector.tensor_tensor(m2[:], m2[:], m1[:], ALU.subtract))
                    dve.wait_ge(r_exp.sem, r_exp.at(i, 2))
                    step(i, 18, nc.vector.tensor_scalar(m1[:], m2[:], 1.0, None, ALU.add))
                    step(i, 19, nc.vector.reciprocal(m1[:], m1[:]))
                    step(i, 20, nc.vector.tensor_tensor(m2[:], m2[:], m1[:], ALU.mult))
                    step(i, 21, nc.vector.tensor_tensor(one1[:], one1[:], wide(m1[:]), ALU.mult))
                    step(i, 22, nc.vector.tensor_tensor(one2[:], one2[:], wide(m2[:]), ALU.mult))
                    step(i, 23, nc.vector.tensor_tensor(comb[:], one1[:], one2[:], ALU.add))
                    step(i, 24, nc.vector.tensor_copy(cand[:, 0, 0:1], comb[:, 0, 0:1]))

                def chunk(i, u, lead):
                    start_acc(i, u)
                    if moe:
                        router(i)
                    for n in range(2 * E):
                        multiply(i, n)
                        if n >= 4 and n % 2 == 0:
                            add(i, (n - 4) // 2)
                        if n == 1 and lead:
                            pre(i + 1, 1 - u)
                    for e in range(max(E - 2, 0), E):
                        add(i, e)
                    finish(i, u)

                dve.wait_ge(w_loaded.sem, w_loaded.at(0))
                pre(0, 0)
                with dve.Fori(0, CHUNKS // 2 - 1) as r:
                    for u in range(2):
                        chunk(2 * r + u, u, True)
                chunk(CHUNKS - 2, 0, True)
                chunk(CHUNKS - 1, 1, False)


def gqa(nc, ps, dram, x_in, x_out):
    QUADS = TILES // 2
    SCALE = 64.0 ** -0.5
    TURN_X, Q0, Q1, K, V, QT0, QT1, KT = range(8)
    P0, O0, OT0, P1, O1, OT1, WO, BACK = range(8)
    with ExitStack() as mem:
        st = Stage(nc, mem, "gq")
        ident = st.sb("ident", [128, 128])
        wq = st.sb("wq", [128, 1024])
        wk = st.sb("wk", [128, 256])
        wv = st.sb("wv", [128, 256])
        wo = st.sb("wo", [128, 8, 128])
        cos = st.sb("cos", [128, 64])
        sin = st.sb("sin", [128, 64])
        alibi = st.sb("alibi", [128, 1024])
        x = st.sb("x", [128, 2, 2, 128])
        xr = st.sb("xr", [128, 2, 2, 128])
        xT = st.sb("xT", [128, 4, 2, 64])
        xT1 = st.sb("xT1", [128, 256])
        qc = st.sb("qc", [128, 1024])
        qs = st.sb("qs", [128, 1024])
        qr = st.sb("qr", [128, 2, 1024])
        kc = st.sb("kc", [128, 512])
        ks = st.sb("ks", [128, 512])
        kr = st.sb("kr", [128, 8, 2, 64])
        qT = st.sb("qT", [128, 2, 2, 1024])
        kbd = st.sb("kbd", [128, 2, 4, 4, 128])
        vbd = st.sb("vbd", [128, 2, 4, 4, 128])
        p = st.sb("p", [128, 2, 2048])
        top = st.sb("top", [128, 32])
        total = st.sb("total", [128, 32])
        rec = st.sb("rec", [128, 32])
        pT = st.sb("pT", [128, 1024])
        o = st.sb("o", [128, 1024])
        oT = st.sb("oT", [128, 8, 256])
        yT = st.sb("yT", [128, 256])
        res = st.sb("res", [128, 2, 128])
        stats = st.sb("stats", [128, 2, 6])
        mv = st.sb("mv", [128, 2, 2])
        rstd = st.sb("rstd", [128, 2])
        half_neg = st.sb("half_neg", [128, 2])
        eps = st.sb("eps", [128, 2])
        seen = st.sb("seen", [128, 1])
        y = st.sb("y", [128, 2, 2, 128])
        loads = [(ident[:], dram["ident"]), (wq[:], dram["g_wq"]), (wk[:], dram["g_wk"]), (wv[:], dram["g_wv"]),
                 (wo[:], dram["g_wo"]), (cos[:], dram["g_cos"]), (sin[:], dram["g_sin"]), (alibi[:], dram["g_alibi"])]
        w_loaded = st.dma_signal("w_loaded", len(loads))
        x_loaded = st.slot_signal("x_loaded")
        xr_loaded = st.slot_signal("xr_loaded")
        y_stored = st.slot_signal("y_stored")
        blank = st.counter("blank", 2)
        half_set = st.counter("half_set", 2)
        lead_done = st.counter("lead_done", 8)
        lead_taken = st.counter("lead_taken", 8)
        trail_done = st.counter("trail_done", 8)
        trail_taken = st.counter("trail_taken", 8)
        q_turned = st.counter("q_turned", 2)
        k_turned = st.counter("k_turned")
        s_done = st.counter("s_done")
        biased = st.counter("biased")
        top_ready = st.counter("top_ready")
        shifted = st.counter("shifted")
        exp_done = st.counter("exp_done")
        summed = st.counter("summed")
        rec_ready = st.counter("rec_ready")
        p_ready = st.counter("p_ready")
        tailed = st.counter("tailed", 6)
        rstd_ready = st.counter("rstd_ready", 2)

        ORDER = [("lead", TURN_X), ("trail", P0), ("lead", Q0), ("scores", 0), ("trail", O0), ("lead", Q1), ("scores", 1),
                 ("trail", OT0), ("trail", P1), ("lead", K), ("trail", O1), ("lead", V), ("trail", OT1), ("lead", QT0),
                 ("trail", WO), ("lead", QT1), ("trail", BACK), ("lead", KT)]
        lead_ps = ps[:, 4:6, :].rearrange("p a n -> p (a n)")
        trail_ps = ps[:, 6:8, :].rearrange("p a n -> p (a n)")
        S_ps = ps[:, 0:4, :].rearrange("p a n -> p (a n)")

        def cols(bank0, c, n):
            return slice(None), bank0 + c // 512, slice(c % 512, c % 512 + n)

        st.begin()
        with nc.Block() as block:

            @block.sync
            def _(sp):
                for dst, src in loads:
                    sp.dma_start(dst, src).then_inc(w_loaded.sem, 16)

                def lead(i, u):
                    sp.wait_ge(lead_done.sem, lead_done.at(i - 2))
                    sp.dma_start(x[:, u], tiles_of(x_in, i, 2)).then_inc(x_loaded.of(u), 16)

                def trail(i, u):
                    sp.wait_ge(trail_taken.sem, trail_taken.at(i - 2))
                    sp.dma_start(xr[:, u], tiles_of(x_in, i, 2)).then_inc(xr_loaded.of(u), 16)

                def store(i, u):
                    sp.wait_ge(tailed.sem, tailed.at(i))
                    sp.dma_start(tiles_of(x_out, i, 2), y[:, u]).then_inc(y_stored.of(u), 16)

                lead(0, 0)
                lead(1, 1)
                trail(0, 0)
                lead(2, 0)
                trail(1, 1)
                lead(3, 1)
                trail(2, 0)
                store(0, 0)
                with sp.Fori(1, (QUADS - 2) // 2) as r:
                    for h in range(2):
                        i, u = 2 * r + (1 + h), (1 + h) % 2
                        lead(i + 1, 1 - u)
                        trail(i, u)
                        store(i - 2, u)
                trail(QUADS - 1, 1)
                for q in (QUADS - 3, QUADS - 2, QUADS - 1):
                    store(q, q % 2)
                for u in range(2):
                    sp.wait_ge(y_stored.of(u), y_stored.at(QUADS - 2 + u, u))

            @block.tensor
            def _(pe):
                def lead(i, u, step):
                    pe.wait_ge(lead_taken.sem, lead_taken.at(i, step))
                    if step == TURN_X:
                        pe.wait_ge(x_loaded.of(u), x_loaded.at(i, u))
                        for t in range(2):
                            mm = nc.tensor.transpose(ps[:, 4, 128 * t:128 * t + 128], x[:, u, t], ident[:])
                    elif step in (Q0, Q1):
                        t = step - Q0
                        for n in range(2):
                            mm = nc.tensor.matmul(ps[:, 4 + n, :], xT1[:, 128 * t:128 * t + 128],
                                                  wq[:, 512 * n:512 * n + 512], start=True, stop=True)
                    elif step == K:
                        for t in range(2):
                            mm = nc.tensor.matmul(ps[:, 4, 256 * t:256 * t + 256], xT1[:, 128 * t:128 * t + 128], wk[:],
                                                  start=True, stop=True)
                    elif step == V:
                        for b in range(4):
                            mm = nc.tensor.matmul(ps[cols(4, 256 * b, 256)], xT[:, b].rearrange("p a k -> p (a k)"), wv[:],
                                                  start=True, stop=True)
                    elif step in (QT0, QT1):
                        t = step - QT0
                        pe.wait_ge(q_turned.sem, q_turned.at(i, t + 1))
                        for j in range(8):
                            mm = nc.tensor.transpose(ps[cols(4, 128 * j, 128)], qr[:, t, 128 * j:128 * j + 128], ident[:])
                    else:
                        pe.wait_ge(k_turned.sem, k_turned.at(i))
                        for c in range(8):
                            mm = nc.tensor.transpose(ps[cols(4, 128 * c, 128)], kr[:, c].rearrange("p a d -> p (a d)"),
                                                     ident[:])
                    mm.then_inc(lead_done.sem, 1)

                def scores(i, u, t):
                    if t == 0:
                        pe.wait_ge(biased.sem, biased.at(i - 1))
                        pe.wait_ge(lead_taken.sem, lead_taken.at(i))
                        nc.tensor.transpose(ps[:, 0, 0:128], ident[:], ident[:])
                    for b2 in range(2):
                        for j in range(8):
                            c = 1024 * t + 128 * j
                            mm = nc.tensor.matmul(
                                ps[64 * b2:64 * b2 + 64, c // 512, c % 512:c % 512 + 128],
                                qT[:, u, t, 128 * j + 64 * b2:128 * j + 64 * b2 + 64],
                                kbd[:, u, 2 * t + b2, j // 2], start=True, stop=True)
                    if t == 1:
                        mm.then_inc(s_done.sem, 1)

                def trail(i, u, step):
                    pe.wait_ge(trail_taken.sem, trail_taken.at(i, step))
                    if step in (P0, P1):
                        t = int(step == P1)
                        pe.wait_ge(p_ready.sem, p_ready.at(i))
                        for j in range(8):
                            c = 1024 * t + 128 * j
                            mm = nc.tensor.transpose(ps[cols(6, 128 * j, 128)], p[:, u, c:c + 128], ident[:])
                    elif step in (O0, O1):
                        t = int(step == O1)
                        nc.tensor.transpose(ps[:, 6, 0:128], ident[:], ident[:])
                        for b2 in range(2):
                            for j in range(8):
                                mm = nc.tensor.matmul(
                                    ps[64 * b2:64 * b2 + 64, 6 + j // 4, 128 * (j % 4):128 * (j % 4) + 128],
                                    pT[:, 128 * j + 64 * b2:128 * j + 64 * b2 + 64], vbd[:, u, 2 * t + b2, j // 2],
                                    start=True, stop=True)
                    elif step in (OT0, OT1):
                        for j in range(8):
                            mm = nc.tensor.transpose(ps[cols(6, 128 * j, 128)], o[:, 128 * j:128 * j + 128], ident[:])
                    elif step == WO:
                        for j in range(8):
                            mm = nc.tensor.matmul(ps[:, 6, 0:256], wo[:, j], oT[:, j], start=j == 0, stop=j == 7)
                    else:
                        for t in range(2):
                            mm = nc.tensor.transpose(ps[:, 7, 128 * t:128 * t + 128], yT[:, 128 * t:128 * t + 128], ident[:])
                    mm.then_inc(trail_done.sem, 1)

                def quad(i, u, with_lead, with_trail):
                    for kind, step in ORDER:
                        if kind == "scores":
                            scores(i, u, step)
                        elif kind == "trail" and with_trail:
                            trail(i - 1, 1 - u, step)
                        elif kind == "lead" and with_lead:
                            lead(i + 1, 1 - u, step)

                pe.wait_ge(w_loaded.sem, w_loaded.at(0))
                for step in range(8):
                    lead(0, 0, step)
                quad(0, 0, True, False)
                with pe.Fori(0, (QUADS - 2) // 2) as r:
                    for h in range(2):
                        quad(2 * r + (1 + h), (1 + h) % 2, True, True)
                quad(QUADS - 1, 1, False, True)
                for step in range(8):
                    trail(QUADS - 1, 1, step)

            @block.scalar
            def _(act):
                def lead(i, u, step):
                    act.wait_ge(lead_done.sem, lead_done.at(i, step + 1))
                    if step == TURN_X:
                        nc.scalar.copy(xT1[:], ps[:, 4, 0:256])
                        ins = nc.scalar.activation(xT[:], ps[:, 4, 0:256].rearrange(
                            "p (b a k) -> p b a k", b=4, a=1).to_broadcast([128, 4, 2, 64]), ACT.Identity)
                    elif step in (QT0, QT1):
                        act.wait_ge(s_done.sem, s_done.at(i - 2))
                        ins = nc.scalar.copy(qT[:, u, step - QT0], lead_ps)
                    elif step == V:
                        act.wait_ge(trail_done.sem, trail_done.at(i - 2, O1 + 1))
                        for h2 in range(2):
                            rows = slice(64 * h2, 64 * h2 + 64)
                            ins = nc.scalar.copy(
                                vbd[rows, u].rearrange("p b v d -> p (b v) d")[:, :, 64 * h2:64 * h2 + 64],
                                lead_ps[rows].rearrange("p (c d) -> p c d", d=64))
                    else:
                        src = lead_ps.rearrange("p (t v b k) -> p t v b k", t=2, v=4, b=2)
                        for t in range(2):
                            for h2 in range(2):
                                rows = slice(64 * h2, 64 * h2 + 64)
                                ins = nc.scalar.copy(
                                    kbd[rows, u, 2 * t:2 * t + 2, :, 64 * h2:64 * h2 + 64].rearrange("p b v k -> p v b k"),
                                    src[rows, t])
                    ins.then_inc(lead_taken.sem, 1)

                def trail(i, step):
                    act.wait_ge(trail_done.sem, trail_done.at(i, step + 1))
                    if step in (P0, P1):
                        ins = nc.scalar.copy(pT[:], trail_ps)
                    elif step in (O0, O1):
                        ins = nc.scalar.copy(o[:], trail_ps)
                    elif step in (OT0, OT1):
                        t = int(step == OT1)
                        ins = nc.scalar.copy(oT[:, :, 128 * t:128 * t + 128],
                                             trail_ps.rearrange("p (j q) -> p j q", j=8))
                    else:
                        ins = nc.scalar.copy(yT[:], ps[:, 6, 0:256])
                    ins.then_inc(trail_taken.sem, 1)

                def exponentials(i, u):
                    act.wait_ge(shifted.sem, shifted.at(i))
                    nc.scalar.activation(p[:, u], p[:, u], ACT.Exp, scale=SCALE).then_inc(exp_done.sem, 1)

                def quad(i, u, with_lead, with_trail):
                    for kind, step in ORDER:
                        if kind == "trail" and with_trail and step != BACK:
                            trail(i - 1, step)
                        elif kind == "lead" and with_lead and step not in (Q0, Q1, K):
                            lead(i + 1, 1 - u, step)
                        if (kind, step) == ("lead", QT0):
                            exponentials(i, u)

                act.wait_ge(blank.sem, blank.at(0))
                for step in (TURN_X, V, QT0, QT1, KT):
                    lead(0, 0, step)
                quad(0, 0, True, False)
                with act.Fori(0, (QUADS - 2) // 2) as r:
                    for h in range(2):
                        quad(2 * r + (1 + h), (1 + h) % 2, True, True)
                quad(QUADS - 1, 1, False, True)
                for step in (P0, O0, OT0, P1, O1, OT1, WO):
                    trail(QUADS - 1, step)

            @block.gpsimd
            def _(pool):
                def turn_q(i, t):
                    pool.wait_ge(lead_taken.sem, lead_taken.at(i, Q0 + t + 1))
                    nc.gpsimd.tensor_tensor(qr[:, t], qc[:], qs[:], ALU.add).then_inc(q_turned.sem, 1)

                def turn_k(i):
                    pool.wait_ge(lead_taken.sem, lead_taken.at(i, K + 1))
                    nc.gpsimd.tensor_tensor(
                        kr[:], kc[:].rearrange("p (c a d) -> p c a d", c=8, a=1).to_broadcast([128, 8, 2, 64]),
                        ks[:].rearrange("p (c a d) -> p c a d", c=8, a=1).to_broadcast([128, 8, 2, 64]),
                        ALU.add).then_inc(k_turned.sem, 1)

                def normalise(i, u):
                    pool.wait_ge(rec_ready.sem, rec_ready.at(i))
                    v = p[:, u].rearrange("p (c k) -> p c k", k=64)
                    nc.gpsimd.tensor_tensor(v, v, rec[:].rearrange("p (c a) -> p c a", a=1).to_broadcast([128, 32, 64]),
                                            ALU.mult).then_inc(p_ready.sem, 1)

                def tail_scale(i):
                    pool.wait_ge(tailed.sem, tailed.at(i, 4))
                    nc.gpsimd.tensor_tensor(rstd[:], mv[:, :, 1], eps[:], ALU.add).then_inc(rstd_ready.sem, 1)
                    pool.wait_ge(rstd_ready.sem, rstd_ready.at(i, 1))
                    nc.gpsimd.tensor_tensor(rstd[:], rstd[:], half_neg[:], ALU.pow).then_inc(rstd_ready.sem, 1)

                def lead_steps(i):
                    turn_q(i, 0)
                    turn_q(i, 1)
                    turn_k(i)

                def quad(i, u, with_lead, end=True):
                    if end:
                        tail_scale(i - 2)
                    if with_lead:
                        lead_steps(i + 1)
                    normalise(i, u)

                nc.gpsimd.memset(half_neg[:], -0.5).then_inc(half_set.sem, 1)
                nc.gpsimd.memset(eps[:], LN_EPS).then_inc(half_set.sem, 1)
                pool.wait_ge(half_set.sem, half_set.at(0))
                lead_steps(0)
                quad(0, 0, True, False)
                quad(1, 1, True, False)
                quad(2, 0, True)
                with pool.Fori(1, (QUADS - 2) // 2) as r:
                    for h in range(2):
                        quad(2 * r + (1 + h), (1 + h) % 2, True)
                quad(QUADS - 1, 1, False)
                tail_scale(QUADS - 2)
                tail_scale(QUADS - 1)

            @block.vector
            def _(dve):
                def rotate(src, c, s, heads):
                    src = src.rearrange("p (h d) -> p h d", d=64)
                    cv, sv = c.rearrange("p (h d) -> p h d", d=64), s.rearrange("p (h d) -> p h d", d=64)
                    one = lambda a, n: a.rearrange("p (h d) -> p h d", h=1).to_broadcast([128, heads, n])
                    nc.vector.tensor_tensor(cv, src, one(cos[:], 64), ALU.mult)
                    nc.vector.tensor_tensor(sv[:, :, 0:32], src[:, :, 32:64], one(sin[:, 0:32], 32), ALU.mult)
                    return nc.vector.tensor_tensor(sv[:, :, 32:64], src[:, :, 0:32], one(sin[:, 32:64], 32), ALU.mult)

                def lead(i, u, step):
                    dve.wait_ge(lead_done.sem, lead_done.at(i, step + 1))
                    if step in (Q0, Q1):
                        if step == Q0:
                            dve.wait_ge(q_turned.sem, q_turned.at(i - 1))
                        else:
                            dve.wait_ge(q_turned.sem, q_turned.at(i, 1))
                        ins = rotate(lead_ps, qc[:], qs[:], 16)
                    else:
                        dve.wait_ge(k_turned.sem, k_turned.at(i - 1))
                        ins = rotate(ps[:, 4, :], kc[:], ks[:], 8)
                    ins.then_inc(lead_taken.sem, 1)

                def add_alibi(i, u):
                    dve.wait_ge(s_done.sem, s_done.at(i))
                    dve.wait_ge(trail_done.sem, trail_done.at(i - 2))
                    nc.vector.tensor_tensor(p[:, u].rearrange("p (t n) -> p t n", t=2), S_ps.rearrange(
                        "p (t n) -> p t n", t=2), alibi[:].rearrange("p (a n) -> p a n", a=1).to_broadcast(
                            [128, 2, 1024]), ALU.add).then_inc(biased.sem, 1)

                def softmax_shift(i, u):
                    v = p[:, u].rearrange("p (c k) -> p c k", k=64)
                    dve.wait_ge(biased.sem, biased.at(i))
                    nc.vector.reduce_max(top[:], v, AX.X).then_inc(top_ready.sem, 1)
                    dve.wait_ge(top_ready.sem, top_ready.at(i))
                    nc.vector.tensor_tensor(v, v, top[:].rearrange("p (c a) -> p c a", a=1).to_broadcast([128, 32, 64]),
                                            ALU.subtract).then_inc(shifted.sem, 1)

                def sums(i, u):
                    dve.wait_ge(exp_done.sem, exp_done.at(i))
                    nc.vector.reduce_sum(total[:], p[:, u].rearrange("p (c k) -> p c k", k=64), AX.X).then_inc(
                        summed.sem, 1)
                    dve.wait_ge(p_ready.sem, p_ready.at(i - 1))
                    dve.wait_ge(summed.sem, summed.at(i))
                    nc.vector.reciprocal(rec[:], total[:]).then_inc(rec_ready.sem, 1)

                def finish(i, u):
                    dve.wait_ge(trail_done.sem, trail_done.at(i))
                    dve.wait_ge(xr_loaded.of(u), xr_loaded.at(i, u))
                    dve.wait_ge(tailed.sem, tailed.at(i - 1))
                    nc.vector.tensor_tensor(res[:], ps[:, 7, 0:256].rearrange("p (t d) -> p t d", t=2), xr[:, u],
                                            ALU.add).then_inc(trail_taken.sem, 1)
                    dve.wait_ge(trail_taken.sem, trail_taken.at(i))
                    for t in range(2):
                        nc.vector.bn_stats(stats[:, t], res[:, t]).then_inc(tailed.sem, 1)
                    dve.wait_ge(tailed.sem, tailed.at(i, 2))
                    nc.vector.tensor_copy(seen[:], stats[:, 0, 0:1])
                    for t in range(2):
                        nc.vector.bn_aggr(mv[:, t], stats[:, t]).then_inc(tailed.sem, 1)

                def scale(i, u):
                    dve.wait_ge(rstd_ready.sem, rstd_ready.at(i))
                    dve.wait_ge(y_stored.of(u), y_stored.at(i - 2, u))
                    for t in range(2):
                        nc.vector.tensor_scalar(y[:, u, t], res[:, t], mv[:, t, 0:1], rstd[:, t:t + 1],
                                                ALU.subtract, ALU.mult).then_inc(tailed.sem, 1)

                def quad(i, u, with_lead, end=True):
                    if end:
                        finish(i - 2, u)
                    if with_lead:
                        lead(i + 1, 1 - u, Q0)
                    if end:
                        scale(i - 2, u)
                    if with_lead:
                        lead(i + 1, 1 - u, Q1)
                    add_alibi(i, u)
                    if with_lead:
                        lead(i + 1, 1 - u, K)
                    softmax_shift(i, u)
                    sums(i, u)

                nc.vector.memset(kbd[:], 0.0).then_inc(blank.sem, 1)
                nc.vector.memset(vbd[:], 0.0).then_inc(blank.sem, 1)
                dve.wait_ge(blank.sem, blank.at(0))
                dve.wait_ge(w_loaded.sem, w_loaded.at(0))
                for step in (Q0, Q1, K):
                    lead(0, 0, step)
                quad(0, 0, True, False)
                quad(1, 1, True, False)
                quad(2, 0, True)
                with dve.Fori(1, (QUADS - 2) // 2) as r:
                    for h in range(2):
                        quad(2 * r + (1 + h), (1 + h) % 2, True)
                quad(QUADS - 1, 1, False)
                for h in range(2):
                    finish(QUADS - 2 + h, h)
                    scale(QUADS - 2 + h, h)


def route(nc, ps, dram, x_in, plan):
    E = 4
    QUADS = SLOTS // 4
    ROUND = 1.5 * 2.0 ** 23
    with ExitStack() as mem:
        st = Stage(nc, mem, "rt")
        x = st.sb("x", [128, TILES, 128])
        average = st.sb("average", [128, 2])
        before = st.sb("before", [128, 128])
        number = st.sb("number", [128, 128])
        ones = st.sb("ones", [128, 128])
        iota = st.sb("iota", [128, SLOTS])
        chunk_of = st.sb("chunk_of", [128, QUADS])
        wg = st.sb("wg", [128, E])
        bg = st.sb("bg", [128, E])
        order = st.sb("order", [128, E])
        mean = st.sb("mean", [128, 128])
        lg = st.sb("lg", [128, E])
        rest = st.sb("rest", [128, E])
        pr = st.sb("pr", [128, E])
        cand = st.sb("cand", [128, E])
        one = [st.sb(f"one{r}", [128, E]) for r in range(2)]
        both = st.sb("both", [128, E])
        m1 = st.sb("m1", [128, 1])
        r1 = st.sb("r1", [128, 1])
        share = st.sb("share", [128, E])
        base = st.sb("base", [128, E])
        slot = st.sb("slot", [128, 2])
        gate = st.sb("gate", [128, 2])
        holds = st.sb("holds", [128, SLOTS])
        expert = st.sb("expert", [128, QUADS])
        batch_i = st.sb("batch_i", [128, SLOTS], I32)
        expert_i = st.sb("expert_i", [128, QUADS], I32)
        slot_i = st.sb("slot_i", [128, 2], I32)
        loads = [(average[:], dram["rt_average"]), (before[:], dram["rt_before"]), (number[:], dram["rt_number"]),
                 (iota[:], bcast_rows(dram["rt_iota"])), (chunk_of[:], bcast_rows(dram["rt_chunk"])),
                 (wg[:], dram["ex_wg"]), (bg[:], bcast_rows(dram["ex_bg"])), (order[:], bcast_rows(dram["ex_order"]))]
        PARTS = 4
        w_loaded = st.dma_signal("w_loaded", len(loads))
        x_loaded = [st.dma_signal(f"x_loaded{n}") for n in range(PARTS)]
        ones_set = st.counter("ones_set")
        mean_done = st.counter("mean_done")
        mean_taken = st.counter("mean_taken")
        logits_done = st.counter("logits_done")
        exp_done = st.counter("exp_done")
        ranked = st.counter("ranked")
        placed = st.counter("placed")
        step_done = st.counter("step_done", 64)
        planned = st.counter("planned")
        stored = st.dma_signal("stored", 4)
        BOTH, HOLDS = 15, 36
        st.begin()
        with nc.Block() as block:

            @block.sync
            def _(sp):
                n = TILES // PARTS
                for k in range(PARTS):
                    sp.dma_start(x[:, n * k:n * k + n], x_in[n * k:n * k + n].rearrange("t p d -> p t d")).then_inc(
                        x_loaded[k].sem, 16)
                for dst, src in loads:
                    sp.dma_start(dst, src).then_inc(w_loaded.sem, 16)
                sp.wait_ge(planned.sem, planned.at(0))
                sp.dma_start(plan["batch"], batch_i[0:1, :]).then_inc(stored.sem, 16)
                sp.dma_start(plan["expert"], expert_i[0:1, :]).then_inc(stored.sem, 16)
                sp.dma_start(plan["slot"], slot_i[:]).then_inc(stored.sem, 16)
                sp.dma_start(plan["gate"], gate[:]).then_inc(stored.sem, 16)
                sp.wait_ge(stored.sem, stored.at(0))

            @block.tensor
            def _(pe):
                pe.wait_ge(w_loaded.sem, w_loaded.at(0))
                for t in range(TILES):
                    if t % (TILES // PARTS) == 0:
                        k = t // (TILES // PARTS)
                        pe.wait_ge(x_loaded[k].sem, x_loaded[k].at(0))
                    mm = nc.tensor.matmul(ps[:, 0, 2 * t:2 * t + 2], x[:, t], average[:], start=True, stop=True)
                mm.then_inc(mean_done.sem, 1)
                pe.wait_ge(mean_taken.sem, mean_taken.at(0))
                nc.tensor.matmul(ps[:, 1, 0:E], mean[:], wg[:], start=True, stop=True).then_inc(logits_done.sem, 1)
                pe.wait_ge(step_done.sem, step_done.at(0, BOTH))
                pe.wait_ge(ones_set.sem, ones_set.at(0))
                nc.tensor.matmul(ps[:, 2, 0:E], before[:], both[:], start=True, stop=True)
                nc.tensor.matmul(ps[:, 2, E:2 * E], ones[:], both[:], start=True, stop=True).then_inc(ranked.sem, 1)
                pe.wait_ge(step_done.sem, step_done.at(0, HOLDS))
                nc.tensor.matmul(ps[:, 3, 0:SLOTS], number[:], holds[:], start=True, stop=True).then_inc(placed.sem, 1)

            @block.scalar
            def _(act):
                act.wait_ge(mean_done.sem, mean_done.at(0))
                nc.scalar.copy(mean[:], ps[:, 0, 0:128]).then_inc(mean_taken.sem, 1)
                act.wait_ge(step_done.sem, step_done.at(0, 3))
                nc.scalar.activation(pr[:], lg[:], ACT.Exp).then_inc(exp_done.sem, 1)

            @block.gpsimd
            def _(pool):
                nc.gpsimd.memset(ones[:], 1.0).then_inc(ones_set.sem, 1)

            @block.vector
            def _(dve):
                count = [0]

                def step(ins):
                    count[0] += 1
                    ins.then_inc(step_done.sem, 1)
                    dve.wait_ge(step_done.sem, step_done.at(0, count[0]))

                def pick(src, onehot):
                    step(nc.vector.reduce_max(m1[:], src[:], AX.X))
                    step(nc.vector.tensor_scalar(cand[:], src[:], m1[:, 0:1], None, ALU.is_equal))
                    step(nc.vector.tensor_tensor(cand[:], cand[:], order[:], ALU.mult))
                    step(nc.vector.reduce_max(r1[:], cand[:], AX.X))
                    step(nc.vector.tensor_scalar(onehot[:], cand[:], r1[:, 0:1], None, ALU.is_equal))

                dve.wait_ge(w_loaded.sem, w_loaded.at(0))
                dve.wait_ge(logits_done.sem, logits_done.at(0))
                step(nc.vector.tensor_tensor(rest[:], ps[:, 1, 0:E], bg[:], ALU.add))
                step(nc.vector.reduce_max(r1[:], rest[:], AX.X))
                step(nc.vector.tensor_scalar(lg[:], rest[:], r1[:, 0:1], None, ALU.subtract))
                pick(lg, one[0])
                step(nc.vector.scalar_tensor_tensor(rest[:], one[0][:], -3e38, lg[:], ALU.mult, ALU.add))
                pick(rest, one[1])
                step(nc.vector.tensor_tensor(both[:], one[0][:], one[1][:], ALU.add))
                dve.wait_ge(exp_done.sem, exp_done.at(0))
                step(nc.vector.reduce_sum(r1[:], pr[:], AX.X))
                step(nc.vector.reciprocal(r1[:], r1[:]))
                step(nc.vector.tensor_scalar(pr[:], pr[:], r1[:, 0:1], None, ALU.mult))
                for r in range(2):
                    step(nc.vector.tensor_tensor(cand[:], pr[:], one[r][:], ALU.mult))
                    step(nc.vector.reduce_sum(gate[:, r:r + 1], cand[:], AX.X))
                dve.wait_ge(ranked.sem, ranked.at(0))
                step(nc.vector.tensor_scalar(share[:], ps[:, 2, E:2 * E], 3.5, 0.125, ALU.add, ALU.mult))
                step(nc.vector.tensor_scalar(share[:], share[:], ROUND, None, ALU.add))
                step(nc.vector.tensor_scalar(share[:], share[:], ROUND, None, ALU.subtract))
                step(nc.vector.memset(base[:, 0:1], 0.0))
                for e in range(1, E):
                    step(nc.vector.tensor_tensor(base[:, e:e + 1], base[:, e - 1:e], share[:, e - 1:e], ALU.add))
                step(nc.vector.scalar_tensor_tensor(share[:], base[:], 8.0, ps[:, 2, 0:E], ALU.mult, ALU.add))
                for r in range(2):
                    step(nc.vector.tensor_tensor(cand[:], share[:], one[r][:], ALU.mult))
                    step(nc.vector.reduce_sum(slot[:, r:r + 1], cand[:], AX.X))
                step(nc.vector.tensor_scalar(holds[:], iota[:], slot[:, 0:1], None, ALU.is_equal))
                assert count[0] == HOLDS - 1, count[0]
                step(nc.vector.scalar_tensor_tensor(holds[:], iota[:], slot[:, 1:2], holds[:], ALU.is_equal, ALU.add))
                step(nc.vector.tensor_scalar(expert[:], chunk_of[:], base[:, 1:2], None, ALU.is_ge))
                for e in (2, 3):
                    step(nc.vector.scalar_tensor_tensor(expert[:], chunk_of[:], base[:, e:e + 1], expert[:], ALU.is_ge,
                                                        ALU.add))
                step(nc.vector.tensor_copy(expert_i[:], expert[:]))
                step(nc.vector.tensor_copy(slot_i[:], slot[:]))
                dve.wait_ge(placed.sem, placed.at(0))
                nc.vector.tensor_copy(batch_i[:], ps[:, 3, 0:SLOTS]).then_inc(planned.sem, 1)


def expert_ffn(nc, ps, dram, t_in, t_out, plan):
    F = 4
    CHUNKS = SLOTS // 8
    DEEP = 4
    with ExitStack() as mem:
        st = Stage(nc, mem, "ef")
        ident = st.sb("ident", [128, 128])
        table = st.sb("table", [1, SLOTS // 4], I32)
        w = st.sb("w", [128, DEEP, 1029])
        ln = st.sb("ln", [128, DEEP, 2, 128])
        tk = st.sb("tk", [128, DEEP, 4, 128])
        tT = st.sb("tT", [128, 2, 512])
        hid = st.sb("hid", [128, 2, F, 512])
        fT = st.sb("fT", [128, 512])
        z = st.sb("z", [128, 2, 4, 128])
        stats = st.sb("stats", [128, 4, 6])
        mv = st.sb("mv", [128, 4, 2])
        rstd = st.sb("rstd", [128, 4])
        half_neg = st.sb("half_neg", [128, 4])
        eps = st.sb("eps", [128, 4])
        seen = st.sb("seen", [128, 1])
        w_loaded = st.dma_signal("w_loaded")
        t_loaded = st.dma_signal("t_loaded")
        passed = st.counter("passed")
        loaded = st.slot_signal("loaded", 3, DEEP)
        z_stored = st.slot_signal("z_stored")
        half_set = st.counter("half_set", 2)
        turn_done = st.counter("turn_done")
        turn_taken = st.counter("turn_taken")
        up_done = st.counter("up_done", F)
        up_taken = st.counter("up_taken", F)
        down_done = st.counter("down_done")
        down_taken = st.counter("down_taken")
        back_done = st.counter("back_done")
        res_taken = st.counter("res_taken")
        st_done = st.counter("st_done")
        mv_ready = st.counter("mv_ready")
        rstd_ready = st.counter("rstd_ready", 2)
        scaled = st.counter("scaled")
        weighted = st.counter("weighted")
        shifted = st.counter("shifted")

        def w1(u, f):
            return w[:, u, 128 * f:128 * f + 128]

        def w2(u, f):
            return w[:, u, 512 + 128 * f:640 + 128 * f]

        def loop(eng, chunk):
            for i in range(DEEP):
                chunk(i, i)
            with eng.Fori(1, (CHUNKS - 3) // DEEP) as r:
                for u in range(DEEP):
                    chunk(DEEP * r + u, u)
            for i in range(CHUNKS - 3, CHUNKS):
                chunk(i, i % DEEP)

        def is_last(i):
            return isinstance(i, int) and i == CHUNKS - 1

        st.begin()
        with nc.Block() as block:

            @block.sync
            def _(sp):
                sp.dma_start(ident[:], dram["ident"]).then_inc(w_loaded.sem, 16)
                sp.dma_start(table[:], plan["expert"]).then_inc(t_loaded.sem, 16)

                def load(i, u):
                    sp.wait_ge(down_taken.sem, down_taken.at(i - DEEP))
                    sp.wait_ge(res_taken.sem, res_taken.at(i - DEEP))
                    sp.wait_ge(shifted.sem, shifted.at(i - DEEP))
                    sp.sem_inc(passed.sem, 1)
                    e = sp.value_load(table[0:1, bass.ds(2 * i, 1)], min_val=0, max_val=3)
                    sp.dma_start(tk[:, u], tiles_of(t_in, i, 4)).then_inc(loaded.of(u), 16)
                    sp.dma_start(w[:, u], dram["ef_w"][bass.ds(e, 1)].rearrange("a p n -> p (a n)")).then_inc(
                        loaded.of(u), 16)
                    sp.dma_start(ln[:, u].rearrange("p a d -> p (a d)"), dram["ef_ln"][bass.ds(e, 1)].to_broadcast(
                        [128, 256])).then_inc(loaded.of(u), 16)

                def store(i, u):
                    sp.wait_ge(shifted.sem, shifted.at(i))
                    sp.dma_start(tiles_of(t_out, i, 4), z[:, u % 2]).then_inc(z_stored.of(u % 2), 16)

                def chunk(i, u):
                    if not isinstance(i, int) or i < CHUNKS - 3:
                        load(i + 3, (u + 3) % DEEP)
                    store(i, u)

                sp.wait_ge(t_loaded.sem, t_loaded.at(0))
                for i in range(3):
                    load(i, i)
                loop(sp, chunk)
                sp.wait_ge(z_stored.of(1), z_stored.at(CHUNKS - 2, 1))
                sp.wait_ge(z_stored.of(0), z_stored.at(CHUNKS - 1, 0))

            @block.tensor
            def _(pe):
                def turn(i, u):
                    pe.wait_ge(loaded.of(u), loaded.at(i, u))
                    pe.wait_ge(turn_taken.sem, turn_taken.at(i - 1))
                    for t in range(4):
                        mm = nc.tensor.transpose(ps[:, 6, 128 * t:128 * t + 128], tk[:, u, t], ident[:])
                    mm.then_inc(turn_done.sem, 1)

                def up(i, u):
                    pe.wait_ge(turn_taken.sem, turn_taken.at(i))
                    for f in range(F):
                        pe.wait_ge(up_taken.sem, up_taken.at(i - 1, f + 1))
                        nc.tensor.matmul(ps[:, f, :], w1(u, f), tT[:, u % 2], start=True, stop=True).then_inc(up_done.sem, 1)

                def down(i, u):
                    pe.wait_ge(down_taken.sem, down_taken.at(i - 1))
                    for f in range(F):
                        pe.wait_ge(up_taken.sem, up_taken.at(i, f + 1))
                        mm = nc.tensor.matmul(ps[:, 4, :], w2(u, f), hid[:, u % 2, f], start=f == 0, stop=f == F - 1)
                    mm.then_inc(down_done.sem, 1)

                def back(i):
                    pe.wait_ge(down_taken.sem, down_taken.at(i))
                    pe.wait_ge(res_taken.sem, res_taken.at(i - 1))
                    for t in range(4):
                        mm = nc.tensor.transpose(ps[:, 5, 128 * t:128 * t + 128], fT[:, 128 * t:128 * t + 128], ident[:])
                    mm.then_inc(back_done.sem, 1)

                def chunk(i, u):
                    if not is_last(i):
                        turn(i + 1, (u + 1) % DEEP)
                    down(i, u)
                    if not is_last(i):
                        up(i + 1, (u + 1) % DEEP)
                    back(i)

                pe.wait_ge(w_loaded.sem, w_loaded.at(0))
                turn(0, 0)
                up(0, 0)
                loop(pe, chunk)

            @block.scalar
            def _(act):
                def take_turn(i, u):
                    act.wait_ge(turn_done.sem, turn_done.at(i))
                    act.wait_ge(up_done.sem, up_done.at(i - 2))
                    nc.scalar.copy(tT[:, u % 2], ps[:, 6, :]).then_inc(turn_taken.sem, 1)

                def relus(i, u):
                    act.wait_ge(down_done.sem, down_done.at(i - 2))
                    for f in range(F):
                        act.wait_ge(up_done.sem, up_done.at(i, f + 1))
                        nc.scalar.activation(hid[:, u % 2, f], ps[:, f, :], ACT.Relu, bias=w[:, u, 1024 + f:1025 + f]).then_inc(
                            up_taken.sem, 1)

                def take_down(i, u):
                    act.wait_ge(down_done.sem, down_done.at(i))
                    act.wait_ge(back_done.sem, back_done.at(i - 1))
                    nc.scalar.activation(fT[:], ps[:, 4, :], ACT.Identity, bias=w[:, u, 1028:1029]).then_inc(
                        down_taken.sem, 1)

                def chunk(i, u):
                    if not is_last(i):
                        take_turn(i + 1, (u + 1) % DEEP)
                    take_down(i, u)
                    if not is_last(i):
                        relus(i + 1, (u + 1) % DEEP)

                take_turn(0, 0)
                relus(0, 0)
                loop(act, chunk)

            @block.gpsimd
            def _(pool):
                def chunk(i, u):
                    pool.wait_ge(mv_ready.sem, mv_ready.at(i))
                    nc.gpsimd.tensor_tensor(rstd[:], mv[:, :, 1], eps[:], ALU.add).then_inc(rstd_ready.sem, 1)
                    pool.wait_ge(rstd_ready.sem, rstd_ready.at(i, 1))
                    nc.gpsimd.tensor_tensor(rstd[:], rstd[:], half_neg[:], ALU.pow).then_inc(rstd_ready.sem, 1)
                    pool.wait_ge(scaled.sem, scaled.at(i))
                    row = lambda n: ln[:, u, n].rearrange("p (a d) -> p a d", a=1).to_broadcast([128, 4, 128])
                    nc.gpsimd.tensor_tensor(z[:, u % 2], z[:, u % 2], row(0), ALU.mult).then_inc(weighted.sem, 1)
                    pool.wait_ge(weighted.sem, weighted.at(i))
                    nc.gpsimd.tensor_tensor(z[:, u % 2], z[:, u % 2], row(1), ALU.add).then_inc(shifted.sem, 1)

                nc.gpsimd.memset(half_neg[:], -0.5).then_inc(half_set.sem, 1)
                nc.gpsimd.memset(eps[:], LN_EPS).then_inc(half_set.sem, 1)
                pool.wait_ge(half_set.sem, half_set.at(0))
                loop(pool, chunk)

            @block.vector
            def _(dve):
                def chunk(i, u):
                    dve.wait_ge(back_done.sem, back_done.at(i))
                    dve.wait_ge(z_stored.of(u % 2), z_stored.at(i - 2, u % 2))
                    nc.vector.tensor_tensor(z[:, u % 2], ps[:, 5, :].rearrange("p (t d) -> p t d", t=4), tk[:, u],
                                            ALU.add).then_inc(res_taken.sem, 1)
                    dve.wait_ge(res_taken.sem, res_taken.at(i))
                    for t in range(4):
                        ins = nc.vector.bn_stats(stats[:, t], z[:, u % 2, t])
                    ins.then_inc(st_done.sem, 1)
                    dve.wait_ge(st_done.sem, st_done.at(i))
                    nc.vector.tensor_copy(seen[:], stats[:, 0, 0:1])
                    for t in range(4):
                        ins = nc.vector.bn_aggr(mv[:, t], stats[:, t])
                    ins.then_inc(mv_ready.sem, 1)
                    dve.wait_ge(rstd_ready.sem, rstd_ready.at(i))
                    for t in range(4):
                        ins = nc.vector.tensor_scalar(z[:, u % 2, t], z[:, u % 2, t], mv[:, t, 0:1], rstd[:, t:t + 1],
                                                      ALU.subtract, ALU.mult)
                    ins.then_inc(scaled.sem, 1)

                loop(dve, chunk)


def combine(nc, ps, x_in, t_in, x_out, plan):
    CHUNKS = TILES // 4
    with ExitStack() as mem:
        st = Stage(nc, mem, "cb")
        slots = st.sb("slots", [1, 2 * B], I32)
        gate = st.sb("gate", [128, TILES, 2])
        x = st.sb("x", [128, 2, 4, 128])
        part = [st.sb(f"part{r}", [128, 2, 4, 128]) for r in range(2)]
        acc = st.sb("acc", [128, 4, 128])
        y = st.sb("y", [128, 2, 4, 128])
        stats = st.sb("stats", [128, 4, 6])
        mv = st.sb("mv", [128, 4, 2])
        rstd = st.sb("rstd", [128, 4])
        half_neg = st.sb("half_neg", [128, 4])
        eps = st.sb("eps", [128, 4])
        seen = st.sb("seen", [128, 1])
        t_loaded = st.dma_signal("t_loaded")
        passed = [st.counter(f"passed{r}") for r in range(2)]
        g_loaded = st.dma_signal("g_loaded", 2)
        loaded = [st.slot_signal("loaded0_", 9), st.slot_signal("loaded1_", 8)]
        y_stored = st.slot_signal("y_stored")
        half_set = st.counter("half_set", 2)
        added = st.counter("added", 2)
        st_done = st.counter("st_done")
        mv_ready = st.counter("mv_ready")
        rstd_ready = st.counter("rstd_ready", 2)
        y_ready = st.counter("y_ready")
        st.begin()

        def gather(eng, i, u, r):
            eng.wait_ge(added.sem, added.at(i - 2))
            eng.sem_inc(passed[r].sem, 1)
            for b in range(8):
                s = eng.value_load(slots[0:1, bass.ds(16 * i + (2 * b + r), 1)], min_val=0, max_val=SLOTS - 1)
                eng.dma_start(part[r][64 * (b % 2):64 * (b % 2) + 64, u, b // 2],
                              t_in[bass.ds(s, 1)].rearrange("a p d -> p (a d)")).then_inc(loaded[r].of(u), 16)

        with nc.Block() as block:

            @block.sync
            def _(sp):
                sp.dma_start(slots[:], plan["slot"].rearrange("(a b) r -> a (b r)", a=1)).then_inc(t_loaded.sem, 16)
                for b2 in range(2):
                    src = plan["gate"].rearrange("(t b) r -> b t r", b=2)[b2:b2 + 1]
                    sp.dma_start(gate[64 * b2:64 * b2 + 64], src.to_broadcast([64, TILES, 2])).then_inc(g_loaded.sem, 16)

                def load(i, u):
                    gather(sp, i, u, 0)
                    sp.dma_start(x[:, u], tiles_of(x_in, i, 4)).then_inc(loaded[0].of(u), 16)

                def store(i, u):
                    sp.wait_ge(y_ready.sem, y_ready.at(i))
                    sp.dma_start(tiles_of(x_out, i, 4), y[:, u]).then_inc(y_stored.of(u), 16)

                sp.wait_ge(t_loaded.sem, t_loaded.at(0))
                load(0, 0)
                load(1, 1)
                with sp.Fori(0, CHUNKS // 2 - 1) as r:
                    for u in range(2):
                        load(2 * r + (u + 2), u)
                        store(2 * r + u, u)
                for u in range(2):
                    store(CHUNKS - 2 + u, u)
                for u in range(2):
                    sp.wait_ge(y_stored.of(u), y_stored.at(CHUNKS - 2 + u, u))

            @block.scalar
            def _(act):
                act.wait_ge(t_loaded.sem, t_loaded.at(0))
                for u in range(2):
                    gather(act, u, u, 1)
                with act.Fori(1, CHUNKS // 2) as r:
                    for u in range(2):
                        gather(act, 2 * r + u, u, 1)

            @block.gpsimd
            def _(pool):
                nc.gpsimd.memset(half_neg[:], -0.5).then_inc(half_set.sem, 1)
                nc.gpsimd.memset(eps[:], LN_EPS).then_inc(half_set.sem, 1)
                pool.wait_ge(half_set.sem, half_set.at(0))
                with pool.Fori(0, CHUNKS) as i:
                    pool.wait_ge(mv_ready.sem, mv_ready.at(i))
                    nc.gpsimd.tensor_tensor(rstd[:], mv[:, :, 1], eps[:], ALU.add).then_inc(rstd_ready.sem, 1)
                    pool.wait_ge(rstd_ready.sem, rstd_ready.at(i, 1))
                    nc.gpsimd.tensor_tensor(rstd[:], rstd[:], half_neg[:], ALU.pow).then_inc(rstd_ready.sem, 1)

            @block.vector
            def _(dve):
                dve.wait_ge(g_loaded.sem, g_loaded.at(0))

                def chunk(i, u, g):
                    for r in range(2):
                        dve.wait_ge(loaded[r].of(u), loaded[r].at(i, u))
                    dve.wait_ge(y_ready.sem, y_ready.at(i - 1))
                    for t in range(4):
                        ins = nc.vector.scalar_tensor_tensor(acc[:, t], part[0][:, u, t], g(t, 0), x[:, u, t], ALU.mult,
                                                             ALU.add)
                    ins.then_inc(added.sem, 1)
                    dve.wait_ge(added.sem, added.at(i, 1))
                    for t in range(4):
                        ins = nc.vector.scalar_tensor_tensor(acc[:, t], part[1][:, u, t], g(t, 1), acc[:, t], ALU.mult,
                                                             ALU.add)
                    ins.then_inc(added.sem, 1)
                    dve.wait_ge(added.sem, added.at(i))
                    for t in range(4):
                        ins = nc.vector.bn_stats(stats[:, t], acc[:, t])
                    ins.then_inc(st_done.sem, 1)
                    dve.wait_ge(st_done.sem, st_done.at(i))
                    nc.vector.tensor_copy(seen[:], stats[:, 0, 0:1])
                    for t in range(4):
                        ins = nc.vector.bn_aggr(mv[:, t], stats[:, t])
                    ins.then_inc(mv_ready.sem, 1)
                    dve.wait_ge(rstd_ready.sem, rstd_ready.at(i))
                    dve.wait_ge(y_stored.of(u), y_stored.at(i - 2, u))
                    for t in range(4):
                        ins = nc.vector.tensor_scalar(y[:, u, t], acc[:, t], mv[:, t, 0:1], rstd[:, t:t + 1],
                                                      ALU.subtract, ALU.mult)
                    ins.then_inc(y_ready.sem, 1)

                for i in range(CHUNKS):
                    chunk(i, i % 2, lambda t, r, i=i: gate[:, 4 * i + t, r:r + 1])


def feed_forward_layout(a, inp):
    f = np.float32
    part = np.arange(128)
    freq = (f(10000.0) ** (-(np.arange(4, dtype=f) * f(2.0)) / f(8))).astype(f)
    a["rope_freq"] = freq[(part % 8) // 2].reshape(128, 1)
    a["rope_sign"] = np.where(part % 2 == 0, f(-1), f(1)).reshape(128, 1)
    up = lambda w: w.transpose(1, 0, 2)
    down = lambda w: w.reshape(-1, 2, 128, D).transpose(2, 0, 1, 3)
    t = "L0_attn_"
    a["mb_sel"] = (part[:, None] % 64 == np.arange(64)[None, :]).astype(f)
    a["mb_norm_w"] = inp[t + "input_norm_w"].reshape(D, 1)
    a["mb_in"] = inp[t + "in_proj_W"].reshape(D, 4, 128)
    a["mb_conv_w"] = inp[t + "conv_W"].reshape(4, 2, 128).transpose(2, 1, 0)
    a["mb_conv_b"], a["mb_dt_b"] = inp[t + "conv_b"].reshape(2, 128).T, inp[t + "dt_b"].reshape(2, 128).T
    a["mb_dt"] = inp[t + "dt_W"].reshape(2, 128, 2, 128).transpose(1, 0, 2, 3)
    twice = [np.tile(inp[t + z].reshape(2, 128, 64), (1, 1, 2)) for z in ("B_W", "C_W")]
    a["mb_bc"] = np.stack(twice, 2).transpose(1, 0, 2, 3)
    a["mb_a_log"] = inp[t + "A_log"]
    a["mb_out"] = inp[t + "out_proj_W"].reshape(2, 128, D).transpose(1, 0, 2)
    a["s0norm_w"] = inp[t + "ffn_norm_w"].reshape(D, 1)
    a["s0wg"], a["s0wu"], a["s0wd"] = up(inp[t + "gate_W"][None]), up(inp[t + "up_W"][None]), down(inp[t + "down_W"][None])
    t = "L0_ffn_"
    a["monorm_w"] = inp[t + "norm2_w"].reshape(D, 1)
    a["mowg"] = up(np.concatenate([inp[t + "sh_gate"][None], inp[t + "e_gate"]]))
    a["mowu"] = up(np.concatenate([inp[t + "sh_up"][None], inp[t + "e_up"]]))
    a["mowd"] = down(np.concatenate([inp[t + "sh_down"][None], inp[t + "e_down"]]))
    a["router"] = inp[t + "router_w"]
    a["order"] = np.arange(8, 0, -1).astype(f)
    t = "L1_attn_"
    a["g_wq"], a["g_wk"], a["g_wv"] = inp[t + "Wq"], inp[t + "Wk"], inp[t + "Wv"]
    a["g_wo"] = inp[t + "Wo"].reshape(8, 128, D).transpose(1, 0, 2)
    inv = f(1) / f(10000.0) ** (np.arange(0, 64, 2, dtype=f) / f(64))
    ang = (part % 64).astype(f)[:, None] * np.concatenate([inv, inv])[None, :]
    a["g_cos"] = np.cos(ang)
    a["g_sin"] = np.sin(ang) * np.where(np.arange(64) < 32, f(-1), f(1))
    t = "L1_ffn_"
    wide = lambda w: w.reshape(4, D, -1)
    w, b = inp[t + "in_proj_w"].reshape(4, 3, D, D), inp[t + "in_proj_b"].reshape(4, 3, D)
    a["ea_wqkv"] = np.concatenate([w[:, 0].transpose(0, 2, 1), w[:, 1].transpose(0, 2, 1), w[:, 2].transpose(0, 2, 1),
                                   b[:, 0, :, None], b[:, 1, :, None]], 2)
    a["ea_bv"] = b[:, 2]
    a["ea_wo"] = inp[t + "out_proj_w"].transpose(0, 2, 1)
    a["ea_rows"] = np.concatenate([inp[t + "out_proj_b"], inp[t + "ln1_w"], inp[t + "ln1_b"]], 1)
    a["ef_w"] = np.concatenate([inp[t + "lin1_w"].transpose(0, 2, 1),
                                wide(inp[t + "lin2_w"].reshape(4, D, 4, 128).transpose(0, 3, 2, 1)),
                                inp[t + "lin1_b"].reshape(4, 4, 128).transpose(0, 2, 1), inp[t + "lin2_b"][:, :, None]], 2)
    a["ef_ln"] = np.concatenate([inp[t + "ln2_w"], inp[t + "ln2_b"]], 1)
    a["rt_average"] = np.where(part[:, None] // 64 == np.arange(2)[None, :], f(1 / 64), f(0))
    a["rt_before"] = (part[:, None] < part[None, :]).astype(f)
    a["rt_number"] = np.repeat(part[:, None], 128, 1).astype(f)
    a["rt_iota"] = np.arange(SLOTS).astype(f)
    a["rt_chunk"] = (np.arange(SLOTS // 4) // 2).astype(f)
    a["ex_wg"], a["ex_bg"] = inp[t + "gate_w"].T, inp[t + "gate_b"]
    a["ex_order"] = np.arange(4, 0, -1).astype(f)
    slopes = ((2.0 ** -0.5) ** (1 + np.arange(16))).astype(f)
    rel = (np.arange(64)[None, :] - (part % 64)[:, None]).astype(f)
    a["g_alibi"] = (f(8) * (slopes[None, :, None] * rel[:, None, :])).reshape(128, 1024)


def host_layout(inp):
    f = np.float32
    a = {}
    a["x"] = inp["x"].reshape(TILES, 128, D)
    a["ctx"] = inp["ctx_1024"].reshape(TILES, 128, D)
    a["pos"] = inp["pos_BxS2"].reshape(B * S)
    a["mask"] = inp["mask_Bx1xSxS2_ff1"].reshape(TILES, 128, S)
    part = np.arange(128)
    a["ident"] = np.eye(128, dtype=f)
    a["head_mask"] = ((part[:, None] // 8) % 4 == np.arange(4)[None, :]).astype(f)
    a["sel_q"] = (part[None, :] % 64 == np.arange(64)[:, None]).astype(f)
    a["future"] = np.where(np.arange(512)[None, :] % 64 > np.arange(64)[:, None], f(-1e30), f(0))

    def pair_swap(v):
        return v.reshape(v.shape[:-1] + (-1, 2))[..., ::-1].reshape(v.shape)

    col = lambda v: v.reshape(-1, 1)
    for pre, q, k, v, o, t in (("x0", "w_q", "w_k", "w_v", "w_o", "L0_xattn_"), ("f0", "wq", "wk", "wv", "wo", "L0_ffn_"),
                               ("x1", "wq_w", "wk_w", "wv_w", "wo_w", "L1_xattn_")):
        a[pre + "wq"], a[pre + "wk"], a[pre + "wv"] = inp[t + q], inp[t + k], inp[t + v]
        a[pre + "wo"] = inp[t + o]
    for pre, b in (("x0", "L0_xattn_b_%s"), ("x1", "L1_xattn_w%s_b")):
        for z in "qkvo":
            v = inp[b % z]
            a[pre + "b" + z] = col(v) if z in "qk" else v
    a["x0wqs"], a["x0wks"] = pair_swap(inp["L0_xattn_w_q"]), pair_swap(inp["L0_xattn_w_k"])
    a["x0bqs"], a["x0bks"] = col(pair_swap(inp["L0_xattn_b_q"])), col(pair_swap(inp["L0_xattn_b_k"]))
    a["f0norm_w"] = col(inp["L0_ffn_norm1_w"])
    feed_forward_layout(a, inp)
    return {k: np.ascontiguousarray(v) for k, v in a.items()}


def stage_weights(dram, prefix, names):
    return {n: dram[prefix + n] for n in names} | {"ident": dram["ident"], "head_mask": dram["head_mask"]}


def build(nc, dram, out):
    with ExitStack() as mem:
        ps = mem.enter_context(nc.psum_tensor("ps", [128, 8, 512], F32))
        h = [nc.dram_tensor(f"hidden{n}", (TILES, 128, D), F32, kind="Internal").ap() for n in range(7)]
        wn = ["wq", "wk", "wv", "wo"]
        bn = ["bq", "bk", "bv", "bo"]
        x = dram["x"]

        def xattn0(src, dst):
            tables = [nc.dram_tensor(f"rope{z}", (8, B * S), F32, kind="Internal").ap() for z in range(2)]
            rope_tables(nc, dram, tables)
            w = stage_weights(dram, "x0", wn + bn + ["wqs", "wks", "bqs", "bks"])
            w |= {"sel_q": dram["sel_q"], "future": dram["future"]}
            attention8(nc, ps, "x0", src, dst, w, ctx=dram["ctx"], qkv_bias=True,
                       rope=tables, causal=True)

        def attn_moe(src, dst):
            w = stage_weights(dram, "f0", wn + ["norm_w"]) | {"norm_eps": 1e-6}
            attention8(nc, ps, "f0", src, dst, w, pre_norm=True, tail="none")

        def xattn1(src, dst):
            attention8(nc, ps, "x1", src, dst, stage_weights(dram, "x1", wn + bn), ctx=dram["ctx"],
                       qkv_bias=True, mask=dram["mask"])

        def mixture(src, dst):
            plan = {"batch": nc.dram_tensor("plan_batch", (1, SLOTS), I32, kind="Internal").ap(),
                    "expert": nc.dram_tensor("plan_expert", (1, SLOTS // 4), I32, kind="Internal").ap(),
                    "slot": nc.dram_tensor("plan_slot", (B, 2), I32, kind="Internal").ap(),
                    "gate": nc.dram_tensor("plan_gate", (B, 2), F32, kind="Internal").ap()}
            pairs = [nc.dram_tensor(f"pairs{n}", (SLOTS, S, D), F32, kind="Internal").ap() for n in range(2)]
            tiles = [t.rearrange("(t a) s d -> t (a s) d", a=2) for t in pairs]
            route(nc, ps, dram, src, plan)
            w = {"wqkv": dram["ea_wqkv"], "bv": dram["ea_bv"], "wo": dram["ea_wo"], "rows": dram["ea_rows"],
                 "ident": dram["ident"], "head_mask": dram["head_mask"]}
            attention8(nc, ps, "ea", src.rearrange("t (a s) d -> (t a) s d", a=2), tiles[0], w, qkv_bias=True,
                       tail="affine", plan=plan)
            expert_ffn(nc, ps, dram, tiles[0], tiles[1], plan)
            combine(nc, ps, src, pairs[1], dst, plan)

        mamba(nc, ps, dram, x, h[0])
        swiglu(nc, ps, "s0", dram, x, h[0], h[1])
        xattn0(h[1], h[2])
        attn_moe(h[2], h[3])
        swiglu(nc, ps, "mo", dram, h[2], h[3], h[4])
        gqa(nc, ps, dram, h[4], h[5])
        xattn1(h[5], h[6])
        mixture(h[6], out)


def kernel(**inputs):
    import concourse.bacc as bacc
    from concourse.bass_utils import run_bass_kernel_spmd

    arrays = host_layout({k: np.asarray(v) for k, v in inputs.items()})
    nc = bacc.Bacc("TRN2", target_bir_lowering=False, num_devices=1)
    dram = {k: nc.dram_tensor("in_" + k, v.shape, mybir.dt.from_np(v.dtype), kind="ExternalInput").ap()
            for k, v in arrays.items()}
    out = nc.dram_tensor("out", (TILES, 128, D), F32, kind="ExternalOutput").ap()
    build(nc, dram, out)
    got = run_bass_kernel_spmd(nc, [{"in_" + k: v for k, v in arrays.items()}], core_ids=[0])
    return got.results[0]["out"].reshape(B, S, D)
```
